# Optimizing a Trainium2 kernel written in Bass

```python
import numpy as np
import jax
import jax.numpy as jnp

def _softmax(x, axis=-1):
    return jax.nn.softmax(x, axis=axis)

def _gelu(x):
    return jax.nn.gelu(x, approximate=True)

def _silu(x):
    return jax.nn.silu(x)

def _sigmoid(x):
    return jax.nn.sigmoid(x)

def _layernorm(x, axis=-1, eps=1e-05):
    m = jnp.mean(x, axis=axis, keepdims=True)
    v = jnp.var(x, axis=axis, keepdims=True)
    return (x - m) / jnp.sqrt(v + eps)

def _scatter_add(tgt, idx, src, axis=0):
    return tgt.at[idx].add(src)

def _segment_sum(src, seg, n):
    return jax.ops.segment_sum(src, seg, n)
kernel_name = 'mk_vit_tower_d2_tok_img768_r4_d871fe'

def setup_inputs(seed: int=0):
    np.random.seed(seed)
    _w = jnp.asarray

    def _rec_inputs():
        import jax
        import jax.numpy as jnp
        _rk = jax.random.key(seed)
        x = -0.000137204 + 0.999937 * jax.random.normal(jax.random.fold_in(_rk, 1), (16, 3, 84, 84), jnp.float32)
        return x
    x = _rec_inputs()

    def _L0_tok_setup():
        import jax, jax.numpy as jnp
        import numpy as np
        B, C, H, W_IMG = (128, 3, 224, 224)
        N_PATCH, EMBED = (256, 192)
        GRID = 32
        key = jax.random.key(seed)
        k1, k2, k3, k4 = jax.random.split(key, 4)
        x = jax.random.normal(k1, (B, C, H, W_IMG), dtype=jnp.float32)
        curve = jax.random.randint(k2, (N_PATCH, 2), 0, GRID, dtype=jnp.int32)
        proj_w = jax.random.normal(k3, (EMBED, C), dtype=jnp.float32) * 0.02
        proj_b = jax.random.normal(k4, (EMBED,), dtype=jnp.float32) * 0.02
        return {'x': x, 'curve': curve, 'proj_w': proj_w, 'proj_b': proj_b}
    _L0_tok_all = _L0_tok_setup()
    _L0_tok_in = {k: v for k, v in _L0_tok_all.items() if k in ('curve', 'proj_w', 'proj_b')}
    del _L0_tok_all

    def _L0_attn_setup():
        import jax, jax.numpy as jnp
        import numpy as np

        def depthwise_conv1d(x, w, pad):
            return jax.lax.conv_general_dilated(x, w, window_strides=(1,), padding=[(pad, pad)], dimension_numbers=('NCH', 'OIH', 'NCH'), feature_group_count=x.shape[1])
        key = jax.random.key(seed)
        ks = jax.random.split(key, 6)
        B, L, D, F = (2, 512, 192, 64)
        return {'x': jax.random.normal(ks[0], (B, L, D), jnp.float32), 'w_in': jax.random.normal(ks[1], (D, 4 * D), jnp.float32) * D ** (-0.5), 'b_in': jnp.zeros((4 * D,), jnp.float32), 'w_filt': jax.random.normal(ks[2], (F, D), jnp.float32) * F ** (-0.5), 'b_filt': jnp.zeros((D,), jnp.float32), 'w_short': jax.random.normal(ks[3], (D, 1, 3), jnp.float32) * 0.5, 'b_short': jnp.zeros((D,), jnp.float32), 'w_out': jax.random.normal(ks[4], (D, D), jnp.float32) * D ** (-0.5), 'b_out': jnp.zeros((D,), jnp.float32)}
    _L0_attn_all = _L0_attn_setup()
    _L0_attn_in = {k: v for k, v in _L0_attn_all.items() if k in ('w_in', 'b_in', 'w_filt', 'b_filt', 'w_short', 'b_short', 'w_out', 'b_out')}
    del _L0_attn_all

    def _L0_ffn_setup():
        import jax, jax.numpy as jnp
        import numpy as np
        B, T, C = (4, 512, 192)
        E, K = (8, 2)

        def _mlp(x, wfc, wproj):
            h = jnp.square(jax.nn.relu(x @ wfc))
            return h @ wproj
        key = jax.random.key(seed)
        ks = jax.random.split(key, 6)
        s = 0.02
        return {'x': jax.random.normal(ks[0], (B, T, C), jnp.float32), 'w_fc_sh': jax.random.normal(ks[1], (C, C), jnp.float32) * s, 'w_proj_sh': jax.random.normal(ks[2], (C, C), jnp.float32) * s, 'w1': jax.random.normal(ks[3], (E, C, C), jnp.float32) * s, 'w2': jax.random.normal(ks[4], (E, C, C), jnp.float32) * s, 'router_w': jax.random.normal(ks[5], (E, C), jnp.float32) * s, 'balance_bias': jnp.zeros((E,), jnp.float32)}
    _L0_ffn_all = _L0_ffn_setup()
    _L0_ffn_in = {k: v for k, v in _L0_ffn_all.items() if k in ('w_fc_sh', 'w_proj_sh', 'w1', 'w2', 'router_w', 'balance_bias')}
    del _L0_ffn_all

    def _L1_attn_setup():
        import jax, jax.numpy as jnp
        import numpy as np
        import math
        HIDDEN = 192
        HEADS = 12
        HEAD_DIM = HIDDEN // HEADS
        BLOCK = 64
        TOPK = 3
        BATCH = 2
        SEQ = 512

        def _rope(x, sin, cos):
            d2 = x.shape[-1] // 2
            x1, x2 = (x[..., :d2], x[..., d2:])
            return x * cos + jnp.concatenate([-x2, x1], axis=-1) * sin
        key = jax.random.key(seed)
        ks = jax.random.split(key, 5)
        s = 1.0 / math.sqrt(HIDDEN)
        return {'hidden_states': jax.random.normal(ks[0], (BATCH, SEQ, HIDDEN), jnp.float32), 'Wq': jax.random.normal(ks[1], (HIDDEN, HIDDEN), jnp.float32) * s, 'Wk': jax.random.normal(ks[2], (HIDDEN, HIDDEN), jnp.float32) * s, 'Wv': jax.random.normal(ks[3], (HIDDEN, HIDDEN), jnp.float32) * s, 'Wo': jax.random.normal(ks[4], (HIDDEN, HIDDEN), jnp.float32) * s}
    _L1_attn_all = _L1_attn_setup()
    _L1_attn_in = {k: v for k, v in _L1_attn_all.items() if k in ('Wq', 'Wk', 'Wv', 'Wo')}
    del _L1_attn_all

    def _L1_ffn_setup():
        import jax, jax.numpy as jnp
        import numpy as np
        N_EXPERTS = 8
        TOPK = 2
        B, S, H, F = (8, 512, 192, 768)
        key = jax.random.key(seed)
        ks = jax.random.split(key, 4)
        return {'hidden_states': jax.random.normal(ks[0], (B, S, H), dtype=jnp.float32), 'Wr': jax.random.normal(ks[1], (H, N_EXPERTS), dtype=jnp.float32) * 0.02, 'br': jnp.zeros((N_EXPERTS,), dtype=jnp.float32), 'Wfc': jax.random.normal(ks[2], (N_EXPERTS, H, F), dtype=jnp.float32) * 0.02, 'bfc': jnp.zeros((N_EXPERTS, F), dtype=jnp.float32), 'Wproj': jax.random.normal(ks[3], (N_EXPERTS, F, H), dtype=jnp.float32) * 0.02, 'bproj': jnp.zeros((N_EXPERTS, H), dtype=jnp.float32)}
    _L1_ffn_all = _L1_ffn_setup()
    _L1_ffn_in = {k: v for k, v in _L1_ffn_all.items() if k in ('Wr', 'br', 'Wfc', 'bfc', 'Wproj', 'bproj')}
    del _L1_ffn_all
    return {'x': x, 'L0_tok_curve': _L0_tok_in['curve'], 'L0_tok_proj_w': _L0_tok_in['proj_w'], 'L0_tok_proj_b': _L0_tok_in['proj_b'], 'L0_attn_w_in': _L0_attn_in['w_in'], 'L0_attn_b_in': _L0_attn_in['b_in'], 'L0_attn_w_filt': _L0_attn_in['w_filt'], 'L0_attn_b_filt': _L0_attn_in['b_filt'], 'L0_attn_w_short': _L0_attn_in['w_short'], 'L0_attn_b_short': _L0_attn_in['b_short'], 'L0_attn_w_out': _L0_attn_in['w_out'], 'L0_attn_b_out': _L0_attn_in['b_out'], 'L0_ffn_w_fc_sh': _L0_ffn_in['w_fc_sh'], 'L0_ffn_w_proj_sh': _L0_ffn_in['w_proj_sh'], 'L0_ffn_w1': _L0_ffn_in['w1'], 'L0_ffn_w2': _L0_ffn_in['w2'], 'L0_ffn_router_w': _L0_ffn_in['router_w'], 'L0_ffn_balance_bias': _L0_ffn_in['balance_bias'], 'L1_attn_Wq': _L1_attn_in['Wq'], 'L1_attn_Wk': _L1_attn_in['Wk'], 'L1_attn_Wv': _L1_attn_in['Wv'], 'L1_attn_Wo': _L1_attn_in['Wo'], 'L1_ffn_Wr': _L1_ffn_in['Wr'], 'L1_ffn_br': _L1_ffn_in['br'], 'L1_ffn_Wfc': _L1_ffn_in['Wfc'], 'L1_ffn_bfc': _L1_ffn_in['bfc'], 'L1_ffn_Wproj': _L1_ffn_in['Wproj'], 'L1_ffn_bproj': _L1_ffn_in['bproj']}

def reference(x, L0_tok_curve, L0_tok_proj_w, L0_tok_proj_b, L0_attn_w_in, L0_attn_b_in, L0_attn_w_filt, L0_attn_b_filt, L0_attn_w_short, L0_attn_b_short, L0_attn_w_out, L0_attn_b_out, L0_ffn_w_fc_sh, L0_ffn_w_proj_sh, L0_ffn_w1, L0_ffn_w2, L0_ffn_router_w, L0_ffn_balance_bias, L1_attn_Wq, L1_attn_Wk, L1_attn_Wv, L1_attn_Wo, L1_ffn_Wr, L1_ffn_br, L1_ffn_Wfc, L1_ffn_bfc, L1_ffn_Wproj, L1_ffn_bproj):
    import jax
    import jax.numpy as jnp

    def _L0_tok_ref(x, curve, proj_w, proj_b):
        import jax, jax.numpy as jnp
        import numpy as np
        B, C, H, W_IMG = (128, 3, 224, 224)
        N_PATCH, EMBED = (256, 192)
        GRID = 32
        gathered = x[:, :, curve[:, 1], curve[:, 0]]
        return jnp.einsum('bcn,ec->bne', gathered, proj_w) + proj_b

    def _L0_attn_ref(x, w_in, b_in, w_filt, b_filt, w_short, b_short, w_out, b_out):
        import jax, jax.numpy as jnp
        import numpy as np

        def depthwise_conv1d(x, w, pad):
            return jax.lax.conv_general_dilated(x, w, window_strides=(1,), padding=[(pad, pad)], dimension_numbers=('NCH', 'OIH', 'NCH'), feature_group_count=x.shape[1])
        B, L, D = x.shape
        F = w_filt.shape[0]
        x_short = depthwise_conv1d(x.transpose(0, 2, 1), w_short, 1).transpose(0, 2, 1) + b_short
        proj = x @ w_in + b_in
        x_proj, z_proj, v1, v2 = jnp.split(proj, 4, axis=-1)
        z = jax.nn.silu(z_proj)
        t = jnp.arange(L, dtype=jnp.float32)[:, None]
        f = jnp.arange(F, dtype=jnp.float32)[None, :]
        pos_basis = jnp.sin(t * f / F)
        filt = (pos_basis @ w_filt + b_filt).T
        conv = depthwise_conv1d(x_proj.transpose(0, 2, 1), filt[:, None, :], L // 2)[:, :, :L]
        y = conv.transpose(0, 2, 1) * v1 * v2 * z
        return (y + x_short) @ w_out + b_out

    def _L0_ffn_ref(x, w_fc_sh, w_proj_sh, w1, w2, router_w, balance_bias):
        import jax, jax.numpy as jnp
        import numpy as np
        B, T, C = (4, 512, 192)
        E, K = (8, 2)

        def _mlp(x, wfc, wproj):
            h = jnp.square(jax.nn.relu(x @ wfc))
            return h @ wproj
        Bx, Tx, Cx = x.shape
        shared = _mlp(x, w_fc_sh, w_proj_sh)
        xf = x.reshape(-1, Cx)
        logits = xf.astype(jnp.float32) @ router_w.T
        scores = jax.nn.sigmoid(logits)
        _, idx = jax.lax.top_k(scores + balance_bias, K)
        tw = jnp.take_along_axis(scores, idx, axis=-1)
        tw = tw / (tw.sum(-1, keepdims=True) + 1e-20)
        combine = (jax.nn.one_hot(idx, E, dtype=tw.dtype) * tw[..., None]).sum(1)
        h = jnp.square(jax.nn.relu(jnp.einsum('nc,ech->neh', xf, w1)))
        y = jnp.einsum('neh,ehc->nec', h, w2)
        routed = jnp.einsum('nec,ne->nc', y, combine)
        return shared + routed.reshape(Bx, Tx, Cx)

    def _L1_attn_ref(hidden_states, Wq, Wk, Wv, Wo):
        import jax, jax.numpy as jnp
        import numpy as np
        import math
        HIDDEN = 192
        HEADS = 12
        HEAD_DIM = HIDDEN // HEADS
        BLOCK = 64
        TOPK = 3
        BATCH = 2
        SEQ = 512

        def _rope(x, sin, cos):
            d2 = x.shape[-1] // 2
            x1, x2 = (x[..., :d2], x[..., d2:])
            return x * cos + jnp.concatenate([-x2, x1], axis=-1) * sin
        B, S, Hd = hidden_states.shape
        H, D, bs, K = (HEADS, HEAD_DIM, BLOCK, TOPK)
        nb = S // bs
        scale = 1.0 / math.sqrt(D)

        def split_heads(x):
            return x.reshape(B, S, H, D).transpose(0, 2, 1, 3)
        q = split_heads(hidden_states @ Wq.T)
        k = split_heads(hidden_states @ Wk.T)
        v = split_heads(hidden_states @ Wv.T)
        inv_freq = 1.0 / 10000.0 ** (jnp.arange(0, D, 2, dtype=jnp.float32) / D)
        ang = jnp.arange(S, dtype=jnp.float32)[:, None] * inv_freq[None, :]
        emb = jnp.concatenate([ang, ang], axis=-1)
        sin, cos = (jnp.sin(emb), jnp.cos(emb))
        q = _rope(q, sin, cos)
        k = _rope(k, sin, cos)
        block_reps = k.reshape(B, H, nb, bs, D).mean(axis=3)
        bscores = jnp.einsum('bhsd,bhnd->bhsn', q, block_reps) * scale
        pos = jnp.arange(S)
        cur = pos // bs
        blk = jnp.arange(nb)
        future = blk[None, None, None, :] > cur[None, None, :, None]
        bscores = jnp.where(future, -jnp.inf, bscores)
        is_cur = blk[None, None, None, :] == cur[None, None, :, None]
        bscores = jnp.where(is_cur, jnp.finfo(bscores.dtype).max, bscores)
        _, topk_idx = jax.lax.top_k(bscores, min(K, nb))
        selected = jnp.sum(jax.nn.one_hot(topk_idx, nb, dtype=jnp.float32), axis=-2) > 0
        sel_t = selected[:, :, :, cur]
        intra_ok = (cur[None, :] != cur[:, None]) | (pos[None, :] <= pos[:, None])
        mask = sel_t & intra_ok[None, None]
        scores = jnp.einsum('bhqd,bhkd->bhqk', q, k) * scale
        scores = jnp.where(mask, scores, -jnp.inf)
        probs = jax.nn.softmax(scores, axis=-1)
        out = jnp.einsum('bhqk,bhkd->bhqd', probs, v)
        out = out.transpose(0, 2, 1, 3).reshape(B, S, Hd)
        return out @ Wo.T

    def _L1_ffn_ref(hidden_states, Wr, br, Wfc, bfc, Wproj, bproj):
        import jax, jax.numpy as jnp
        import numpy as np
        N_EXPERTS = 8
        TOPK = 2
        B, S, H, F = (8, 512, 192, 768)
        b, s, h = hidden_states.shape
        x = hidden_states.reshape(-1, h)
        logits = x @ Wr + br
        probs = jax.nn.softmax(logits, axis=-1)
        topk_w, topk_i = jax.lax.top_k(probs, TOPK)
        topk_w = topk_w / jnp.sum(topk_w, axis=-1, keepdims=True)
        out = jnp.zeros_like(x)
        for e in range(N_EXPERTS):
            w = jnp.sum(jnp.where(topk_i == e, topk_w, 0.0), axis=-1)
            he = jax.nn.gelu(x @ Wfc[e] + bfc[e], approximate=True) @ Wproj[e] + bproj[e]
            out = out + w[:, None] * he
        return out.reshape(b, s, h)
    h = _L0_tok_ref(x, L0_tok_curve, L0_tok_proj_w, L0_tok_proj_b)
    h = h + _L0_attn_ref(_layernorm(h, axis=-1), L0_attn_w_in, L0_attn_b_in, L0_attn_w_filt, L0_attn_b_filt, L0_attn_w_short, L0_attn_b_short, L0_attn_w_out, L0_attn_b_out)
    h = h + _L0_ffn_ref(_layernorm(h, axis=-1), L0_ffn_w_fc_sh, L0_ffn_w_proj_sh, L0_ffn_w1, L0_ffn_w2, L0_ffn_router_w, L0_ffn_balance_bias)
    h = h + _L1_attn_ref(_layernorm(h, axis=-1), L1_attn_Wq, L1_attn_Wk, L1_attn_Wv, L1_attn_Wo)
    h = h + _L1_ffn_ref(_layernorm(h, axis=-1), L1_ffn_Wr, L1_ffn_br, L1_ffn_Wfc, L1_ffn_bfc, L1_ffn_Wproj, L1_ffn_bproj)
    return h

_drawn_inputs = setup_inputs


def setup_inputs(seed=0):
    import zlib

    import numpy as np

    out = dict(_drawn_inputs(seed))
    spreads = {'L0_attn_b_in': (0.0, 0.1),
     'L0_attn_b_filt': (0.0, 0.1),
     'L0_attn_b_short': (0.0, 0.701),
     'L0_attn_b_out': (0.0, 0.674),
     'L0_ffn_balance_bias': (0.0, 0.8),
     'L1_ffn_br': (0.0, 0.8),
     'L1_ffn_bfc': (0.0, 0.8),
     'L1_ffn_bproj': (0.0, 0.8)}
    factors = {'L0_ffn_w_fc_sh': 8.0,
     'L0_ffn_w_proj_sh': 8.0,
     'L0_ffn_w1': 8.0,
     'L0_ffn_w2': 8.0,
     'L0_ffn_router_w': 8.0,
     'L1_ffn_Wr': 5.783,
     'L1_ffn_Wfc': 8.0,
     'L1_ffn_Wproj': 7.505,
     'L1_attn_Wq': 3.694,
     'L1_attn_Wk': 3.864}
    for name, (base, spread) in spreads.items():
        noise = np.random.default_rng([zlib.crc32(name.encode()), seed]).standard_normal(out[name].shape)
        drawn = base * np.exp(spread * noise) if base else spread * noise
        out[name] = jnp.asarray(drawn.astype(out[name].dtype))
    for name, factor in factors.items():
        out[name] = (out[name] * factor).astype(out[name].dtype)
    return out
```

```python
from contextlib import ExitStack

import concourse.bass as bass
from concourse import mybir

F32 = mybir.dt.float32
BF16 = mybir.dt.bfloat16
I32 = mybir.dt.int32
U32 = mybir.dt.uint32
ALU = mybir.AluOpType
ACT = mybir.ActivationFunctionType
AX = mybir.AxisListType

P = 128
B, S, D = 16, 256, 192
G = S // P
T = B * G
C = 2
K = D // C
E = 8
XT = -(-2 * B * S // P) + E
HID = 768
HT = HID // P
HEADS, HD = 12, 16
HG = HEADS // 4
BLK = 64
NBLK = S // BLK
NEG = -1.0e30
EPS = 1e-5
IMG = 84


class Own:

    def __init__(self, eng, sem):
        self.eng, self.sem, self.base, self.k = eng, sem, 0, 0

    def step(self, ins):
        ins.then_inc(self.sem, 1)
        self.k += 1
        return ins

    def wait(self):
        self.eng.wait_ge(self.sem, self.base + self.k)

    def chain(self, ins):
        self.step(ins)
        self.wait()

    def enter(self, i, per):
        self.start = self.base + self.k
        self.per, self.k = per, 0
        self.base = self.start + i * per

    def leave(self, trips):
        assert self.k == self.per, (self.k, self.per)
        self.base, self.k = self.start + trips * self.per, 0


def build(nc, a, out):
    top = ExitStack()
    with top:
        def sb_in(ctx, name, shape, dt=F32):
            return ctx.enter_context(nc.sbuf_tensor(name, shape, dt))

        stage_sems = []

        def sem_in(ctx, *names):
            made = [nc.alloc_semaphore(n) for n in names]
            if ctx is not top:
                stage_sems.extend(made)
            return made if len(made) > 1 else made[0]

        bank = [top.enter_context(nc.psum_tensor(f"bank{n}", [P, 2, 512], F32)) for n in range(4)]

        def ps(n):
            return bank[n // 2][:, n % 2, :]

        h = sb_in(top, "h", [P, T, D])
        stats = sb_in(top, "stats", [P, T, 6])
        mean = sb_in(top, "mean", [P, T])
        rstd = sb_in(top, "rstd", [P, T])
        ident = sb_in(top, "ident", [P, P])
        zeros = sb_in(top, "zeros", [P, D])
        wload, setup_load = sem_in(top, "weights_loaded", "constants_loaded")
        stored = sem_in(top, "outputs_stored")
        zero_filled = sem_in(top, "slots_zeroed")

        slots_x = nc.dram_tensor("slots_x", (XT * P, D), F32, kind="Internal").ap()
        slots_y = nc.dram_tensor("slots_y", (XT * P, D), F32, kind="Internal").ap()

        def row_stats(eng, tile):
            return eng.bn_stats(stats[:, tile, :], h[:, tile, :])

        def tokens():
            with ExitStack() as ctx:
                sb = lambda *x: sb_in(ctx, *x)
                curve = sb("curve", [P, G, 2], I32)
                cf = sb("cf", [P, G, 2])
                neg = sb("neg", [P, G, 2])
                at = sb("at", [P, G], I32)
                atf = sb("atf", [P, G])
                pix = sb("pix", [P, G, 3 * B])
                pixT = sb("pixT", [3 * B + 1, G, P])
                wtok = sb("wtok", [3 * B + 1, B, D])
                load, ready = sem_in(ctx, "tok_load", "tok_index")
                gathered = sem_in(top, "tok_gathered")
                tr, trc, mm, hd, own, zz, ones = sem_in(
                    ctx, "tok_pixT_in_psum", "tok_pixT", "tok_matmul", "tok_h", "tok_dve", "tok_zeros", "tok_ones")
                steps = [(g, b) for b in range(0, B, 2) for g in range(G)]
                with nc.Block() as block:
                    @block.sync
                    def _(e):
                        e.dma_start(curve[:, :, :], a["curve"].rearrange("(g p) c -> p g c", p=P)).then_inc(load, 16)
                        e.dma_start(ident[:, :], a["c_ident"]).then_inc(load, 16)
                        e.dma_start(wtok[:, :, :], a["tok_w"]).then_inc(load, 16)
                        e.wait_ge(zz, 1)
                        e.dma_start(slots_x.rearrange("(s p) d -> p s d", p=P),
                                    zeros[:, :].unsqueeze(1).to_broadcast([P, XT, D])).then_inc(zero_filled, 16)

                    @block.gpsimd
                    def _(e):
                        e.memset(zeros[:, :], 0.0).then_inc(zz, 1)
                        e.memset(pixT[:, :, :], 1.0).then_inc(ones, 1)
                        e.wait_ge(ready, 1)
                        for g in range(G):
                            e.indirect_dma_start(pix[:, g, :], None, a["x"], bass.IndirectOffsetOnAxis(
                                at[:, g:g + 1].bitcast(U32), 0)).then_inc(gathered, 16)

                    @block.vector
                    def _(e):
                        own_ = Own(e, own)
                        e.wait_ge(load, 48)
                        own_.chain(e.tensor_copy(cf[:, :, :], curve[:, :, :]))
                        own_.chain(e.tensor_scalar(neg[:, :, :], cf[:, :, :], 0.0, float(IMG), ALU.is_lt, ALU.mult))
                        own_.chain(e.tensor_tensor(cf[:, :, :], cf[:, :, :], neg[:, :, :], ALU.add))
                        own_.chain(e.tensor_scalar(cf[:, :, :], cf[:, :, :], 0.0, float(IMG - 1), ALU.max, ALU.min))
                        own_.chain(e.scalar_tensor_tensor(atf[:, :], cf[:, :, 1], float(IMG), cf[:, :, 0],
                                                          ALU.mult, ALU.add))
                        e.tensor_copy(at[:, :], atf[:, :]).then_inc(ready, 1)
                        e.wait_ge(ones, 1)
                        e.wait_ge(tr, 1)
                        e.tensor_copy(pixT[0:3 * B, :, :], ps(0)[0:3 * B, 0:G * P].rearrange("p (g t) -> p g t", g=G)
                                      ).then_inc(trc, 1)
                        for n, (g, b) in enumerate(steps):
                            e.wait_ge(mm, n + 1)
                            e.tensor_copy(h[:, b * G + g:(b + 1) * G + g + 1:G, :],
                                          ps(1 + n % 4)[:, 0:2 * D].rearrange("p (b d) -> p b d", b=2)
                                          ).then_inc(hd, 1)
                        e.wait_ge(hd, len(steps))
                        for t in range(T):
                            row_stats(e, t)

                    @block.tensor
                    def _(e):
                        e.wait_ge(load, 48)
                        e.wait_ge(gathered, 16 * G)
                        for g in range(G):
                            m = e.transpose(ps(0)[0:3 * B, g * P:(g + 1) * P], pix[:, g, :], ident[:, :])
                        m.then_inc(tr, 1)
                        e.wait_ge(trc, 1)
                        for n, (g, b) in enumerate(steps):
                            if n >= 4:
                                e.wait_ge(hd, n - 3)
                            e.matmul(ps(1 + n % 4)[:, 0:2 * D], pixT[:, g, :], wtok[:, b:b + 2, :].rearrange(
                                "p b d -> p (b d)"), start=True, stop=True).then_inc(mm, 1)

        def ln_tensors(ctx, name):
            return dict(own=sem_in(ctx, name + "_ln_step"), var=sem_in(ctx, name + "_ln_var"),
                        root=sem_in(ctx, name + "_ln_root"), tmp=sb_in(ctx, name + "_ln_tmp", [P, 4, T]))

        def statistics(e, ln):
            s = Own(e, ln["own"])
            t = ln["tmp"]
            m0, q0, m1, q1 = (stats[:, :, n] for n in (1, 2, 4, 5))
            s.step(e.tensor_tensor(t[:, 0, :], m0, m1, ALU.add))
            s.step(e.tensor_tensor(t[:, 1, :], m0, m1, ALU.subtract))
            s.step(e.tensor_tensor(t[:, 2, :], q0, q1, ALU.add))
            s.wait()
            s.step(e.tensor_scalar(mean[:, :], t[:, 0, :], 0.5, None, ALU.mult))
            s.chain(e.tensor_tensor(t[:, 3, :], t[:, 1, :], t[:, 1, :], ALU.mult))
            s.chain(e.scalar_tensor_tensor(t[:, 0, :], t[:, 3, :], D / 4.0, t[:, 2, :], ALU.mult, ALU.add))
            e.tensor_scalar(t[:, 1, :], t[:, 0, :], 1.0 / D, EPS, ALU.mult, ALU.add).then_inc(ln["var"], 1)
            e.wait_ge(ln["root"], 1)
            s.chain(e.reciprocal(rstd[:, :], t[:, 2, :]))

        def root(e, ln):
            e.wait_ge(ln["var"], 1)
            e.activation(ln["tmp"][:, 2, :], ln["tmp"][:, 1, :], ACT.Sqrt).then_inc(ln["root"], 1)

        def normalise(e, xn, i, g):
            t = i * G + g
            return e.tensor_scalar(xn[:, g, :], h[:, t, :], mean[:, t:t + 1] if isinstance(t, int) else mean[:, bass.ds(t, 1)],
                                   rstd[:, t:t + 1] if isinstance(t, int) else rstd[:, bass.ds(t, 1)],
                                   ALU.subtract, ALU.mult)

        def turn(e, psum, src):
            for c in range(C):
                for g in range(G):
                    m = e.transpose(psum[0:K, c * S + g * P:c * S + (g + 1) * P], src[:, g, c * K:(c + 1) * K],
                                    ident[:, :])
            return m

        def hyena():
            NF = 4
            with ExitStack() as ctx:
                sb = lambda *x: sb_in(ctx, *x)
                w_in = sb("w_in", [K + 1, C, 4 * D])
                w_out = sb("w_out", [K + 1, C, D])
                fwd = sb("fwd", [P, G, NF * K])
                inv = sb("inv", [K, NF, S])
                short = sb("short", [K, C, 4])
                specA = sb("specA", [K, 2, C * D])
                specB = sb("specB", [K, 2, C * D])
                ln = ln_tensors(ctx, "hy")
                load = sem_in(ctx, "hy_load")

                with ExitStack() as c2:
                    basis = sb_in(c2, "basis", [65, S])
                    wf = sb_in(c2, "wf", [65, D])
                    filt = sb_in(c2, "filt", [P, G, D])
                    to_spec = sb_in(c2, "to_spec", [P, G, 6 * K])
                    fl, fp, ff, sp, sc = sem_in(c2, "filter_load", "filter_in_psum", "filter", "spectrum_in_psum",
                                                "spectrum")
                    with nc.Block() as block:
                        @block.sync
                        def _(e):
                            e.dma_start(basis[:, :], a["c_basis"]).then_inc(fl, 16)
                            e.dma_start(wf[0:64, :], a["w_filt"]).then_inc(fl, 16)
                            e.dma_start(wf[64:65, :], a["b_filt"]).then_inc(fl, 16)
                            e.dma_start(to_spec[:, :, :], a["c_to_spec"]).then_inc(fl, 16)
                            e.dma_start(w_in[0:K, :, :], a["w_in"]).then_inc(load, 16)
                            e.dma_start(w_in[K:K + 1, 1, :], a["b_in"]).then_inc(load, 16)
                            e.dma_start(fwd[:, :, :], a["c_fwd"]).then_inc(load, 16)
                            e.dma_start(inv[:, :, :], a["c_inv"]).then_inc(load, 16)
                            e.dma_start(short[:, :, :], a["short"]).then_inc(load, 16)
                            e.dma_start(w_out[0:K, :, :], a["w_out"]).then_inc(load, 16)
                            e.dma_start(w_out[K:K + 1, 1, :], a["b_out"]).then_inc(load, 16)

                        @block.tensor
                        def _(e):
                            e.wait_ge(fl, 64)
                            for g in range(G):
                                m = e.matmul(ps(0)[:, g * D:(g + 1) * D], basis[:, g * P:(g + 1) * P], wf[:, :],
                                             start=True, stop=True)
                            m.then_inc(fp, 1)
                            e.wait_ge(ff, 1)
                            for n in range(6):
                                for g in range(G):
                                    m = e.matmul(ps(1 + n // 2)[0:K, (n % 2) * D:(n % 2 + 1) * D],
                                                 to_spec[:, g, n * K:(n + 1) * K], filt[:, g, :],
                                                 start=(g == 0), stop=(g == G - 1))
                            m.then_inc(sp, 1)

                        @block.vector
                        def _(e):
                            e.wait_ge(fp, 1)
                            e.tensor_copy(filt[:, :, :], ps(0)[:, 0:G * D].rearrange("p (g d) -> p g d", g=G)
                                          ).then_inc(ff, 1)
                            statistics(e, ln)
                            e.wait_ge(sp, 1)
                            for n, (spec, half) in enumerate(((specA, 0), (specA, 1), (specB, 1))):
                                e.tensor_copy(spec[:, half, :], ps(1 + n)[0:K, 0:C * D])
                            e.tensor_copy(specB[:, 0, :], ps(2)[0:K, 0:C * D])

                        @block.scalar
                        def _(e):
                            root(e, ln)

                xn = sb("xn", [P, G, D])
                xT = sb("xT", [K + 1, C, S])
                xp = sb("xp", [P, G, D])
                zs = sb("zs", [P, G, D])
                gate = sb("gate", [P, G, D])
                prA = sb("prA", [K, 2, C * D])
                prB = sb("prB", [K, 2, C * D])
                spec = sb("spec", [K, 2, C * D])
                y = sb("y", [P, G, D])
                xs = sb("xs", [K, C, S])
                yx = sb("yx", [K + 1, C, S])
                (xn_ready, xT_psum, xT_ready, xz_psum, xz_ready, v_psum, gate_ready, freq_psum, prod_ready, spec_ready,
                 conv_psum, y_ready, yT_psum, yx_ready, xs_begun, out_psum, h_ready, own, ones,
                 short_ready) = sem_in(
                    ctx, "hy_xn_ready", "hy_xT_in_psum", "hy_xT_ready", "hy_xz_in_psum", "hy_xz_ready", "hy_v_in_psum",
                    "hy_gate_ready", "hy_freq_in_psum", "hy_products_ready", "hy_spectrum_ready", "hy_conv_in_psum",
                    "hy_y_ready", "hy_yT_in_psum", "hy_yx_ready", "hy_short_begun", "hy_out_in_psum", "hy_h_ready",
                    "hy_dve_step", "hy_ones_rows",
                    "hy_short_ready")
                TURNED, XZ, VV, FREQ, CONV = ps(0), bank[1], bank[2], bank[3], ps(1)

                with nc.Block() as block:
                    @block.gpsimd
                    def _(e):
                        e.memset(xT[K:K + 1, :, :], 1.0).then_inc(ones, 1)
                        e.memset(yx[K:K + 1, :, :], 1.0).then_inc(ones, 1)
                        with e.Fori(0, B) as i:
                            e.wait_ge(prod_ready, (i + 1) * 2)
                            e.wait_ge(conv_psum, i)
                            e.tensor_tensor(spec[:, :, :], prA[:, :, :], prB[:, :, :], ALU.add).then_inc(spec_ready, 1)

                    @block.tensor
                    def _(e):
                        def turn_x(i):
                            e.wait_ge(xn_ready, (i + 1) * G)
                            turn(e, TURNED, xn).then_inc(xT_psum, 1)

                        def project(i, half, psum, done, free):
                            if half == 0:
                                e.wait_ge(xT_ready, i + 1)
                            e.wait_ge(free, i)
                            for g in range(G):
                                for c in range(C):
                                    kk = K + c
                                    m = e.matmul(psum[:, g, 0:2 * D], xT[0:kk, c, g * P:(g + 1) * P],
                                                 w_in[0:kk, c, half * 2 * D:(half + 1) * 2 * D],
                                                 start=(c == 0), stop=(c == C - 1))
                            m.then_inc(done, 1)

                        def forward(i):
                            e.wait_ge(xz_ready, i + 1)
                            e.wait_ge(prod_ready, i * 2)
                            for f in range(NF):
                                for g in range(G):
                                    m = e.matmul(FREQ[0:K, f // 2, (f % 2) * D:(f % 2 + 1) * D],
                                                 fwd[:, g, f * K:(f + 1) * K], xp[:, g, :],
                                                 start=(g == 0), stop=(g == G - 1))
                            m.then_inc(freq_psum, 1)

                        def inverse(i):
                            e.wait_ge(spec_ready, i + 1)
                            e.wait_ge(h_ready, i)
                            for g in range(G):
                                for f in range(NF):
                                    m = e.matmul(CONV[:, g * D:(g + 1) * D], inv[:, f, g * P:(g + 1) * P],
                                                 spec[:, f // 2, (f % 2) * D:(f % 2 + 1) * D],
                                                 start=(f == 0), stop=(f == NF - 1))
                            m.then_inc(conv_psum, 1)

                        def turn_y(i):
                            e.wait_ge(y_ready, i + 1)
                            turn(e, TURNED, y).then_inc(yT_psum, 1)

                        def project_out(i):
                            e.wait_ge(yx_ready, i + 1)
                            for g in range(G):
                                for c in range(C):
                                    kk = K + c
                                    m = e.matmul(CONV[:, g * D:(g + 1) * D], yx[0:kk, c, g * P:(g + 1) * P],
                                                 w_out[0:kk, c, :], start=(c == 0), stop=(c == C - 1))
                            m.then_inc(out_psum, 1)

                        e.wait_ge(load, 112)
                        e.wait_ge(ones, 2)
                        turn_x(0)
                        project(0, 0, XZ, xz_psum, xz_ready)
                        project(0, 1, VV, v_psum, gate_ready)
                        forward(0)
                        turn_x(1)

                        def body(i, more):
                            project(i, 0, XZ, xz_psum, xz_ready)
                            inverse(i - 1)
                            project(i, 1, VV, v_psum, gate_ready)
                            turn_y(i - 1)
                            forward(i)
                            if more:
                                e.wait_ge(yx_ready, i)
                                turn_x(i + 1)
                            project_out(i - 1)

                        with e.Fori(1, B - 1) as i:
                            body(i, True)
                        body(B - 1, False)
                        inverse(B - 1)
                        turn_y(B - 1)
                        project_out(B - 1)

                    @block.scalar
                    def _(e):
                        def xT_out(i):
                            e.wait_ge(xT_psum, i + 1)
                            e.wait_ge(v_psum, i)
                            e.wait_ge(short_ready, i * C)
                            e.activation(xT[0:K, :, :], TURNED[0:K, :].rearrange("p (c t) -> p c t", c=C),
                                         ACT.Copy).then_inc(xT_ready, 1)

                        def body(i, more):
                            e.wait_ge(xz_psum, i + 1)
                            e.wait_ge(freq_psum, i)
                            e.activation(xp[:, :, :], XZ[:, :, 0:D], ACT.Copy)
                            e.wait_ge(gate_ready, i)
                            e.activation(zs[:, :, :], XZ[:, :, D:2 * D], ACT.Silu).then_inc(xz_ready, 1)
                            e.wait_ge(yx_ready, i)
                            e.wait_ge(xT_ready, i + 1)
                            for c in range(C):
                                m = e.activation(xs[:, c, :], xT[0:K, c, :], ACT.Identity,
                                                 bias=short[:, c, 3:4], scale=short[:, c, 1:2])
                            m.then_inc(xs_begun, 1)
                            if more:
                                xT_out(i + 1)

                        e.wait_ge(load, 112)
                        xT_out(0)
                        with e.Fori(0, B - 1) as i:
                            body(i, True)
                        body(B - 1, False)

                    @block.vector
                    def _(e):
                        s = Own(e, own)

                        def norm(i):
                            e.wait_ge(xT_psum, i)
                            for g in range(G):
                                normalise(e, xn, i, g).then_inc(xn_ready, 1)

                        def conv_out(i):
                            e.wait_ge(conv_psum, i + 1)
                            e.wait_ge(yT_psum, i)
                            e.tensor_tensor(y[:, :, :], CONV[:, 0:G * D].rearrange("p (g d) -> p g d", g=G),
                                            gate[:, :, :], ALU.mult).then_inc(y_ready, 1)

                        def gates(i):
                            e.wait_ge(v_psum, i + 1)
                            e.wait_ge(xz_ready, i + 1)
                            e.wait_ge(y_ready, i)
                            s.chain(e.tensor_tensor(gate[:, :, :], VV[:, :, 0:D], zs[:, :, :], ALU.mult))
                            e.tensor_tensor(gate[:, :, :], VV[:, :, D:2 * D], gate[:, :, :], ALU.mult
                                            ).then_inc(gate_ready, 1)

                        def join(i):
                            e.wait_ge(yT_psum, i + 1)
                            e.wait_ge(out_psum, i)
                            e.wait_ge(short_ready, (i + 1) * C)
                            e.tensor_tensor(yx[0:K, :, :], TURNED[0:K, :].rearrange("p (c t) -> p c t", c=C),
                                            xs[:, :, :], ALU.add).then_inc(yx_ready, 1)

                        def short_conv(i):
                            e.wait_ge(xs_begun, i + 1)
                            for c in range(C):
                                s.step(e.scalar_tensor_tensor(xs[:, c, 1:S], xT[0:K, c, 0:S - 1], short[:, c, 0:1],
                                                              xs[:, c, 1:S], ALU.mult, ALU.add))
                            s.wait()
                            for c in range(C):
                                e.scalar_tensor_tensor(xs[:, c, 0:S - 1], xT[0:K, c, 1:S], short[:, c, 2:3],
                                                       xs[:, c, 0:S - 1], ALU.mult, ALU.add).then_inc(short_ready, 1)

                        def products(i):
                            e.wait_ge(freq_psum, i + 1)
                            e.wait_ge(spec_ready, i)
                            for n, (pr, sp) in enumerate(((prA, specA), (prB, specB))):
                                e.tensor_tensor(pr[:, :, :], FREQ[0:K, n, 0:C * D].unsqueeze(1).to_broadcast(
                                    [K, 2, C * D]), sp[:, :, :], ALU.mult).then_inc(prod_ready, 1)

                        def add_h(i):
                            e.wait_ge(out_psum, i + 1)
                            hh = h[:, bass.ds(i * G, G), :]
                            e.tensor_tensor(hh, CONV[:, 0:G * D].rearrange("p (g d) -> p g d", g=G), hh,
                                            ALU.add).then_inc(h_ready, 1)
                            e.wait_ge(h_ready, i + 1)
                            for g in range(G):
                                row_stats(e, i * G + g)

                        e.wait_ge(load, 112)
                        norm(0)
                        gates(0)
                        norm(1)
                        short_conv(0)
                        products(0)

                        def body(i, more):
                            conv_out(i - 1)
                            gates(i)
                            if more:
                                norm(i + 1)
                            join(i - 1)
                            short_conv(i)
                            products(i)
                            add_h(i - 1)

                        with e.Fori(1, B - 1) as i:
                            s.enter(i - 1, 3)
                            body(i, True)
                            s.leave(B - 2)
                        body(B - 1, False)
                        conv_out(B - 1)
                        join(B - 1)
                        add_h(B - 1)

        def attention():
            N = 2 * HEADS
            SL = 6 * HD
            NP = 6
            with ExitStack() as ctx:
                sb = lambda n, *x: sb_in(ctx, "at_" + n, *x)
                ln = ln_tensors(ctx, "at")
                wqkv = sb("wqkv", [K, C, 3 * D])
                wo = sb("wo", [P, HG, D])
                rope = sb("rope", [P, G, 2, 2, HD])
                identb = sb("identb", [P, P], BF16)
                causal = sb("causal", [P, P], BF16)
                causalT = sb("causalT", [P, P], BF16)
                keyside = sb("keyside", [SL, HEADS, G, P], BF16)
                xn = sb("xn", [P, G, D])
                xT = sb("xT", [K, C, S])
                tcos, tsin, xr, r1 = (sb(n, [P, 2, G, HEADS, HD]) for n in ("tcos", "tsin", "xr", "r1"))
                hi, mid = (sb(n, [P, 2, N, HD], BF16) for n in ("hi", "mid"))
                slots = sb("slots", [P, 2, N, 6, HD], BF16)
                qkT = [sb(f"qkT{n}", [SL, 2, HEADS, S], BF16) for n in range(2)]
                v1 = [sb(f"v1{n}", [P, G, HEADS, 2, HD]) for n in range(2)]
                bmax = sb("bmax", [P, HEADS, G, NBLK])
                bsum = sb("bsum", [P, HEADS, 3])
                least, other = sb("least", [P, HEADS]), sb("other", [P, HEADS])
                same = sb("same", [P, HEADS, 3])
                drop = sb("drop", [P, HEADS, G, NBLK])
                masked = sb("masked", [P, HEADS, G, NBLK])
                top, negm, nr = (sb(n, [P, HEADS, G]) for n in ("top", "negm", "nr"))
                qside = sb("qside", [P, G, HEADS, 8], BF16)
                qsideT = sb("qsideT", [SL, S], BF16)
                prob = [sb(f"prob{n}", [P, G, S]) for n in range(NP)]
                NS = HG * S // 32
                den = sb("den", [P, NS, 32])
                rden = sb("rden", [P, NS])
                rec, attnT = sb("rec", [P, HG, S]), sb("attnT", [P, HG, S])
                names = ("load", "filled", "xn_ready", "xT_in_psum", "xT_ready", "qk_in_psum", "v_in_psum", "turned_by_angle",
                         "rope_ready", "hi_ready", "rest_ready", "mid_ready", "slots_by_pool", "slots_by_dve",
                         "slots_by_act", "v_ready", "slotsT_in_psum", "slotsT_by_act", "slotsT_by_dve", "scores_in_psum",
                         "blocks_reduced", "qside_ready", "qsideT_in_psum", "qsideT_ready", "scoresT_in_psum",
                         "prob_ready", "pv_done", "attn_ready", "out_in_psum", "h_ready", "dve_step", "gone_on", "pool_goes_on")
                (load, filled, xn_ready, xT_psum, xT_ready, qk_psum, v_psum, rot, rope_ready, hi_ready, rest_ready, mid_ready,
                 slots_pool, slots_dve, slots_act, v_ready, sT_psum, sT_act, sT_dve, s_psum, reduced, qs_ready, qsT_psum,
                 qsT_ready, s2_psum, prob_ready, pv_done, attn_ready, out_psum, h_ready, own, gone_on, pool_on) = sem_in(
                     ctx, *("at_" + n for n in names))
                SA, SC = (ps(0), ps(1)), (ps(2), ps(3))
                MISC, VPS, OPS = ps(4), ps(5), bank[3]
                QK = SA
                SCB = [x.bitcast(BF16) for x in SC]
                SPOOL, SDVE, SACT = 2, 3, 2
                QSPS = OPS[:, 1, S:2 * S].bitcast(BF16)

                def until(e, sem, count):
                    if not isinstance(count, int) or count > 0:
                        e.wait_ge(sem, count)

                def last(j, ahead):
                    return min(j + ahead + 1, B) if isinstance(j, int) else j + ahead + 1

                def run(e, body, own_steps=None):
                    first, trips = 2, (B - 6) // 2
                    for i in range(-4, first):
                        body(i, i % 2, lambda ahead: 0 <= i + ahead < B)
                    with e.Fori(0, trips) as r:
                        if own_steps:
                            own_steps[0].enter(r, own_steps[1])
                        for p in range(2):
                            body(r * 2 + first + p, p, lambda ahead: True)
                        if own_steps:
                            own_steps[0].leave(trips)
                    for i in range(first + 2 * trips, B + 1):
                        body(i, i % 2, lambda ahead: 0 <= i + ahead < B)

                with nc.Block() as block:
                    @block.sync
                    def _(e):
                        for dst, src in ((wqkv, "wqkv"), (wo, "wo"), (rope, "c_rope"), (identb, "c_identb"),
                                         (causal, "c_causal"), (causalT, "c_causalT"), (keyside, "c_keyside"),
                                         (drop, "c_drop")):
                            e.dma_start(dst[:], a[src]).then_inc(load, 16)

                    three = lambda x, n: x.unsqueeze(2).to_broadcast([P, N, n, HD])

                    @block.gpsimd
                    def _(e):
                        for n in range(2):
                            e.memset(v1[n][:, :, :, 1, :], 1.0).then_inc(filled, 1)
                        e.memset(qside[:, :, :, :], 0.0).then_inc(filled, 1)

                        def fill_slots(j):
                            until(e, mid_ready, j + 1)
                            until(e, sT_psum, j * 6)
                            e.sem_inc(pool_on, 1)
                            for dst, src in ((slots[:, 0, :, 0:3, :], three(hi[:, 0], 3)),
                                             (slots[:, 0, :, 3:5, :], three(mid[:, 0], 2))):
                                e.tensor_copy(dst, src).then_inc(slots_pool, 1)

                        def add_rotated(j):
                            until(e, rot, (j + 1) * 3 * G)
                            until(e, rest_ready, j)
                            until(e, hi_ready, j)
                            e.tensor_tensor(xr[:], tcos[:], tsin[:], ALU.add).then_inc(rope_ready, 1)

                        def body(i, p, there):
                            if there(2):
                                fill_slots(i + 2)
                            if there(3):
                                add_rotated(i + 3)

                        run(e, body)

                    @block.tensor
                    def _(e):
                        def turn_x(j):
                            until(e, xn_ready, (j + 1) * G)
                            until(e, h_ready, j - 4)
                            turn(e, MISC, xn).then_inc(xT_psum, 1)

                        def project_qk(j):
                            until(e, xT_ready, j + 1)
                            until(e, prob_ready, (j - 2) * HEADS)
                            until(e, rot, j * 3 * G)
                            for g in range(G):
                                for c in range(C):
                                    m = e.matmul(QK[g][:, 0:2 * D], xT[:, c, g * P:(g + 1) * P],
                                                 wqkv[:, c, 0:2 * D], start=(c == 0), stop=(c == C - 1))
                            m.then_inc(qk_psum, 1)

                        def project_v(j):
                            until(e, xT_ready, j + 1)
                            until(e, v_ready, j)
                            for g in range(G):
                                for c in range(C):
                                    m = e.matmul(VPS[:, g * D:(g + 1) * D], xT[:, c, g * P:(g + 1) * P],
                                                 wqkv[:, c, 2 * D:3 * D], start=(c == 0), stop=(c == C - 1))
                            m.then_inc(v_psum, 1)

                        def turn_slots(j, part):
                            if part == 0:
                                until(e, slots_pool, (j + 1) * SPOOL)
                                until(e, slots_dve, (j + 1) * SDVE)
                                until(e, slots_act, (j + 1) * SACT)
                                until(e, reduced, j * HEADS * 2)
                            for n in (2 * part, 2 * part + 1):
                                if n >= 2:
                                    until(e, (sT_act, sT_dve)[n % 2], j * 3 + n // 2)
                                for k in range(8):
                                    hd, g = 4 * (n % 3) + k // 2, k % 2
                                    m = e.transpose(SCB[n % 2][0:SL, k * P:(k + 1) * P],
                                                    slots[:, n // 3, g * HEADS + hd].rearrange("p s d -> p (s d)"),
                                                    identb[:, :])
                                m.then_inc(sT_psum, 1)

                        def score(j, p, hd):
                            if hd == 0:
                                until(e, sT_act, (j + 1) * 3)
                                until(e, sT_dve, (j + 1) * 3)
                            if hd >= 2:
                                until(e, reduced, (j * HEADS + hd - 1) * 2)
                            for g in range(G):
                                o = SC[hd % 2][:, g * S:(g + 1) * S]
                                e.matmul(o, qkT[p][:, 0, hd, g * P:(g + 1) * P], qkT[p][:, 1, hd, :],
                                         start=True, stop=False)
                                m = e.matmul(o[:, g * P:(g + 1) * P], identb[:, :], causal[:, :],
                                             start=False, stop=True)
                            m.then_inc(s_psum, 1)

                        def turn_qside(j):
                            until(e, qs_ready, (j + 1) * 4)
                            until(e, qsT_ready, j)
                            for g in range(G):
                                m = e.transpose(QSPS[0:SL, g * P:(g + 1) * P],
                                                qside[:, g].rearrange("p h s -> p (h s)"), identb[:, :])
                            m.then_inc(qsT_psum, 1)

                        def scoreT(j, p, hd):
                            if hd == 0:
                                until(e, qsT_ready, j + 1)
                            if hd < 2:
                                until(e, rot, last(j, 2) * 3 * G)
                            else:
                                until(e, prob_ready, j * HEADS + hd - 1)
                            for g in range(G):
                                o = SA[hd % 2][:, g * S:(g + 1) * S]
                                e.matmul(o, qkT[p][:, 1, hd, g * P:(g + 1) * P], qkT[p][:, 0, hd, :],
                                         start=True, stop=False)
                                e.matmul(o, keyside[:, hd, g, :], qsideT[:, :], start=False, stop=False)
                                m = e.matmul(o[:, g * P:(g + 1) * P], identb[:, :], causalT[:, :],
                                             start=False, stop=True)
                            m.then_inc(s2_psum, 1)

                        def values(j, p, n):
                            until(e, prob_ready, j * HEADS + 4 * (n + 1))
                            if n == 0:
                                until(e, v_ready, j + 1)
                                until(e, attn_ready, j * 2)
                            for g in range(G):
                                for q in range(4):
                                    hd = 4 * n + q
                                    m = e.matmul(OPS[q * 32:q * 32 + 32, n // 2, n % 2 * S:(n % 2 + 1) * S],
                                                 v1[p][:, g, hd].rearrange("p two d -> p (two d)"),
                                                 prob[hd % NP][:, g, :], start=(g == 0), stop=(g == G - 1))
                            m.then_inc(pv_done, 1)

                        def project_out(j):
                            until(e, attn_ready, (j + 1) * 2)
                            until(e, xT_ready, last(j, 4))
                            for g in range(G):
                                for n in range(HG):
                                    m = e.matmul(MISC[:, g * D:(g + 1) * D], attnT[:, n, g * P:(g + 1) * P],
                                                 wo[:, n, :], start=(n == 0), stop=(n == HG - 1))
                            m.then_inc(out_psum, 1)

                        def body(i, p, there):
                            for hd in range(HEADS):
                                if there(0):
                                    scoreT(i, p, hd)
                                if there(1):
                                    score(i + 1, 1 - p, hd)
                                if there(0) and hd in (5, 9):
                                    values(i, p, hd // 4 - 1)
                                if there(-1) and hd == 6:
                                    project_out(i - 1)
                            if there(0):
                                values(i, p, HG - 1)
                            if there(2):
                                turn_slots(i + 2, 0)
                            if there(3):
                                project_qk(i + 3)
                            if there(2):
                                turn_slots(i + 2, 1)
                            if there(1):
                                turn_qside(i + 1)
                            if there(3):
                                project_v(i + 3)
                            if there(2):
                                turn_slots(i + 2, 2)
                            if there(4):
                                turn_x(i + 4)

                        e.wait_ge(load, 128)
                        e.wait_ge(filled, 3)
                        run(e, body)

                    @block.scalar
                    def _(e):
                        root(e, ln)

                        def xT_out(j):
                            until(e, xT_psum, j + 1)
                            until(e, v_psum, j)
                            e.activation(xT[:, :, :], MISC[0:K, :].rearrange("p (c t) -> p c t", c=C),
                                         ACT.Identity).then_inc(xT_ready, 1)

                        def his(j):
                            until(e, rope_ready, j + 1)
                            until(e, slots_pool, j * SPOOL)
                            until(e, slots_dve, j * SDVE)
                            until(e, slots_act, j * SACT)
                            until(e, rest_ready, j)
                            e.activation(hi[:].rearrange("p a n d -> p (a n d)"),
                                         xr[:].rearrange("p a g h d -> p (a g h d)"), ACT.Identity).then_inc(hi_ready, 1)

                        def mids(j):
                            until(e, rest_ready, j + 1)
                            until(e, slots_pool, j * SPOOL)
                            until(e, slots_dve, j * SDVE)
                            until(e, slots_act, j * SACT)
                            e.activation(mid[:].rearrange("p a n d -> p (a n d)"),
                                         r1[:].rearrange("p a g h d -> p (a g h d)"), ACT.Identity).then_inc(mid_ready, 1)

                        def fill_slots(j):
                            until(e, mid_ready, j + 1)
                            until(e, sT_psum, j * 6)
                            e.activation(slots[:, 1, :, 1:5:3, :], three(mid[:, 1], 2), ACT.Identity
                                         ).then_inc(slots_act, 1)
                            e.activation(slots[:, 1, :, 5, :], hi[:, 1], ACT.Identity).then_inc(slots_act, 1)

                        def v_out(j, p):
                            until(e, v_psum, j + 1)
                            until(e, pv_done, (j - 1) * HG)
                            e.activation(v1[p][:, :, :, 0, :].rearrange("p g h d -> p (g h) d"),
                                         VPS[:, 0:G * D].rearrange("p (n d) -> p n d", d=HD),
                                         ACT.Identity).then_inc(v_ready, 1)

                        def slotsT_out(j, p, n):
                            until(e, sT_psum, j * 6 + n + 1)
                            if n == 0:
                                until(e, s2_psum, (j - 1) * HEADS)
                            e.activation(qkT[p][:, n // 3, 4 * (n % 3):4 * (n % 3) + 4, :],
                                         SCB[0][0:SL, :].rearrange("p (h t) -> p h t", h=4),
                                         ACT.Identity).then_inc(sT_act, 1)

                        def exponent(j, hd):
                            until(e, s2_psum, j * HEADS + hd + 1)
                            until(e, pv_done, j * HG + (hd - NP) // 4 + 1 if hd >= NP else
                                  (j - 1) * HG + (hd + NP) // 4 + 1)
                            e.activation(prob[hd % NP][:, :, :], SA[hd % 2].rearrange("p (g t) -> p g t", g=G),
                                         ACT.Exp).then_inc(prob_ready, 1)

                        def body(i, p, there):
                            if there(3):
                                xT_out(i + 3)
                            for hd in range(HEADS):
                                if there(0):
                                    exponent(i, hd)
                                if there(2) and hd == 4:
                                    mids(i + 2)
                                if there(2) and hd == 8:
                                    fill_slots(i + 2)
                            if there(2):
                                slotsT_out(i + 2, p, 0)
                                v_out(i + 2, p)
                                slotsT_out(i + 2, p, 2)
                                slotsT_out(i + 2, p, 4)
                            if there(3):
                                his(i + 3)

                        e.wait_ge(filled, 3)
                        run(e, body)

                    @block.vector
                    def _(e):
                        statistics(e, ln)
                        s = Own(e, own)

                        def norm(j):
                            until(e, xT_psum, j)
                            for g in range(G):
                                normalise(e, xn, j, g).then_inc(xn_ready, 1)

                        def rotate(j):
                            until(e, qk_psum, j + 1)
                            until(e, rope_ready, j)
                            for g in range(G):
                                x = QK[g][:, 0:2 * D].rearrange("p (a h d) -> p a h d", a=2, h=HEADS)
                                cos_, sin_ = (rope[:, g, :, n, :].unsqueeze(2).to_broadcast([P, 2, HEADS, HD])
                                              for n in range(2))
                                e.tensor_tensor(tcos[:, :, g], x, cos_, ALU.mult).then_inc(rot, 1)
                                e.tensor_tensor(tsin[:, :, g, :, 0:HD // 2], x[:, :, :, HD // 2:HD],
                                                sin_[:, :, :, 0:HD // 2], ALU.mult).then_inc(rot, 1)
                                e.tensor_tensor(tsin[:, :, g, :, HD // 2:HD], x[:, :, :, 0:HD // 2],
                                                sin_[:, :, :, HD // 2:HD], ALU.mult).then_inc(rot, 1)

                        def rest(j):
                            until(e, hi_ready, j + 1)
                            until(e, mid_ready, j)
                            until(e, slots_dve, j * SDVE)
                            e.tensor_tensor(r1[:].rearrange("p a g h d -> p (a g h d)"),
                                            xr[:].rearrange("p a g h d -> p (a g h d)"),
                                            hi[:].rearrange("p a n d -> p (a n d)"), ALU.subtract
                                            ).then_inc(rest_ready, 1)

                        def fill_slots(j):
                            until(e, mid_ready, j + 1)
                            until(e, sT_psum, j * 6)
                            e.tensor_copy(slots[:, 1, :, 0:4:3, :], three(hi[:, 1], 2)).then_inc(slots_dve, 1)
                            for n, at in ((0, 5), (1, 2)):
                                e.tensor_tensor(slots[:, n, :, at, :], r1[:, n].rearrange("p g h d -> p (g h) d"),
                                                mid[:, n], ALU.subtract).then_inc(slots_dve, 1)

                        def slotsT_out(j, p, n):
                            until(e, sT_psum, j * 6 + n + 1)
                            if n == 1:
                                until(e, s2_psum, (j - 1) * HEADS)
                            e.tensor_copy(qkT[p][:, n // 3, 4 * (n % 3):4 * (n % 3) + 4, :],
                                          SCB[1][0:SL, :].rearrange("p (h t) -> p h t", h=4)).then_inc(sT_dve, 1)

                        def reduce_blocks(j, hd):
                            until(e, s_psum, j * HEADS + hd + 1)
                            x = SC[hd % 2].rearrange("p (n k) -> p n k", k=BLK)
                            e.tensor_reduce(bmax[:, hd].rearrange("p g n -> p (g n)"), x, AX.X, ALU.max
                                            ).then_inc(reduced, 1)
                            e.tensor_reduce(bsum[BLK:P, hd], x[BLK:P, NBLK:NBLK + 3, :], AX.X, ALU.add
                                            ).then_inc(reduced, 1)

                        def query_side(j):
                            until(e, reduced, (j + 1) * HEADS * 2)
                            hb = lambda x: x[BLK:P]
                            s.chain(e.tensor_reduce(hb(least), hb(bsum), AX.X, ALU.min))
                            s.chain(e.tensor_tensor(hb(same), hb(bsum), hb(least).unsqueeze(2).to_broadcast(
                                [BLK, HEADS, 3]), ALU.is_equal))
                            s.step(e.tensor_scalar(drop[BLK:P, :, 1, 2], same[BLK:P, :, 2], NEG, None, ALU.mult))
                            s.chain(e.tensor_scalar(hb(other), same[BLK:P, :, 2], -1.0, 1.0, ALU.mult, ALU.add))
                            s.chain(e.tensor_tensor(hb(least), hb(other), same[BLK:P, :, 1], ALU.mult))
                            s.step(e.tensor_scalar(drop[BLK:P, :, 1, 1], hb(least), NEG, None, ALU.mult))
                            s.chain(e.tensor_tensor(hb(other), hb(other), hb(least), ALU.subtract))
                            s.chain(e.tensor_scalar(drop[BLK:P, :, 1, 0], hb(other), NEG, None, ALU.mult))
                            s.chain(e.tensor_tensor(masked[:], bmax[:], drop[:], ALU.add))
                            s.chain(e.tensor_reduce(top[:], masked[:], AX.X, ALU.max))
                            s.chain(e.tensor_scalar(negm[:], top[:], -1.0, None, ALU.mult))
                            until(e, qsT_psum, j)
                            part = lambda n: qside[:, :, :, n].rearrange("p g h -> p h g")
                            e.tensor_copy(qside[:, :, :, 0:NBLK].rearrange("p g h n -> p h g n"), drop[:]
                                          ).then_inc(qs_ready, 1)
                            e.tensor_copy(part(4), negm[:]).then_inc(qs_ready, 1)
                            until(e, qs_ready, j * 4 + 2)
                            s.chain(e.tensor_tensor(nr[:], negm[:], part(4), ALU.subtract))
                            e.tensor_copy(part(5), nr[:]).then_inc(qs_ready, 1)
                            until(e, qs_ready, j * 4 + 3)
                            e.tensor_tensor(part(6), nr[:], part(5), ALU.subtract).then_inc(qs_ready, 1)

                        def qsideT_out(j):
                            until(e, qsT_psum, j + 1)
                            until(e, s2_psum, j * HEADS)
                            e.tensor_copy(qsideT[:, :], QSPS[0:SL, 0:S]).then_inc(qsT_ready, 1)

                        def turn_denominators(j):
                            until(e, pv_done, (j + 1) * HG)
                            e.sem_inc(gone_on, 1)
                            half = 2 * S // 32
                            s.step(e.transpose(den[:, 0:half, :].rearrange("p n r -> p (n r)"), OPS[:, 0, :]))
                            s.step(e.transpose(den[:, half:NS, :].rearrange("p n r -> p (n r)"), OPS[:, 1, 0:S]))

                        def invert(j):
                            until(e, attn_ready, j * 2)
                            s.wait()
                            s.chain(e.reciprocal(rden[:, :], den[:, :, HD]))
                            e.sem_inc(gone_on, 1)
                            s.step(e.transpose(rec[:].rearrange("p n t -> p (n t)"),
                                               rden[:, :].unsqueeze(2).to_broadcast([P, NS, 32])))

                        def divide(j):
                            until(e, out_psum, j)
                            s.wait()
                            e.tensor_tensor(attnT[:, 0:2, :], OPS[:, 0, :].rearrange("p (n t) -> p n t", n=2),
                                            rec[:, 0:2, :], ALU.mult).then_inc(attn_ready, 1)
                            e.tensor_tensor(attnT[:, 2, :], OPS[:, 1, 0:S], rec[:, 2, :], ALU.mult
                                            ).then_inc(attn_ready, 1)

                        def add_h(j):
                            until(e, out_psum, j + 1)
                            hh = h[:, bass.ds(j * G, G), :]
                            e.tensor_tensor(hh, MISC[:, 0:G * D].rearrange("p (g d) -> p g d", g=G), hh,
                                            ALU.add).then_inc(h_ready, 1)
                            until(e, h_ready, j + 1)
                            for g in range(G):
                                row_stats(e, j * G + g)

                        def body(i, p, there):
                            for hd in range(HEADS):
                                if there(1):
                                    reduce_blocks(i + 1, hd)
                                if there(-1) and hd == 2:
                                    divide(i - 1)
                                if there(-1) and hd == 9:
                                    add_h(i - 1)
                                if there(2) and hd == 1:
                                    rest(i + 2)
                                if there(4) and hd == 6:
                                    norm(i + 4)
                                if there(2) and hd == 6:
                                    fill_slots(i + 2)
                            if there(1):
                                query_side(i + 1)
                            if there(2):
                                slotsT_out(i + 2, p, 1)
                            if there(3):
                                rotate(i + 3)
                            if there(2):
                                slotsT_out(i + 2, p, 3)
                            if there(1):
                                qsideT_out(i + 1)
                            if there(0):
                                turn_denominators(i)
                            if there(2):
                                slotsT_out(i + 2, p, 5)
                            if there(0):
                                invert(i)

                        e.wait_ge(load, 128)
                        e.wait_ge(filled, 3)
                        run(e, body, (s, 2 * 16))

        def route(name, layer, logits, pos, weight, eid, bias, rt):
            with ExitStack() as ctx:
                sb = lambda n, *x: sb_in(ctx, name + n, *x)
                score, sel, eq, top1, top2, both, tmp = (
                    sb(n, [P, T, E]) for n in ("score", "sel", "eq", "top1", "top2", "both", "tmp"))
                best, total, rtotal = (sb(n, [P, T]) for n in ("best", "total", "rtotal"))
                upper, ones = sb("upper", [P, P]), sb("ones", [P, P])
                percnt, upto_, before, overs = (sb(n, [P, E, T]) for n in ("percnt", "upto", "before", "overs"))
                ntile, end, base = (sb(n, [P, E]) for n in ("ntile", "end", "base"))
                at = sb("at", [P, T, 2])
                passed, eidf = sb("passed", [P, XT, E]), sb("eidf", [P, XT])
                load, own, sm_in, sm_out, chosen, counted, filled = sem_in(
                    ctx, *(name + n for n in ("_rt_load", "_rt_step", "_rt_act_in", "_rt_act_out", "_rt_chosen",
                                              "_rt_counted", "_rt_filled")))
                rev, first, tiles, keep = (rt[:, x:y] for x, y in ((0, 8), (8, 40), (40, 40 + XT), (40 + XT, 40 + XT + 256)))
                over = lambda ap: ap.unsqueeze(2).to_broadcast([P, T, E])
                with nc.Block() as block:
                    @block.sync
                    def _(e):
                        e.dma_start(upper[:, :], a["c_upper"]).then_inc(load, 16)

                    @block.gpsimd
                    def _(e):
                        e.memset(ones[:, :], 1.0).then_inc(filled, 1)

                    @block.scalar
                    def _(e):
                        if layer == 0:
                            e.activation(score[:, :, :], logits[:, :, :], ACT.Sigmoid).then_inc(sm_out, 1)
                        else:
                            e.wait_ge(sm_in, 1)
                            e.activation(sel[:, :, :], tmp[:, :, :], ACT.Exp).then_inc(sm_out, 1)

                    @block.tensor
                    def _(e):
                        e.wait_ge(load, 16)
                        e.wait_ge(filled, 1)
                        e.wait_ge(chosen, 1)
                        flat = both[:, :, :].rearrange("p t e -> p (t e)")
                        e.matmul(ps(0)[:, 0:T * E], upper[:, :], flat, start=True, stop=True)
                        e.matmul(ps(1)[:, 0:T * E], ones[:, :], flat, start=True, stop=True).then_inc(counted, 1)

                    @block.vector
                    def _(e):
                        s = Own(e, own)
                        if layer == 0:
                            e.wait_ge(sm_out, 1)
                            s.chain(e.tensor_tensor(sel[:, :, :], score[:, :, :],
                                                    bias[:, :].unsqueeze(1).to_broadcast([P, T, E]), ALU.add))
                        else:
                            s.chain(e.tensor_reduce(best[:, :], logits[:, :, :], AX.X, ALU.max))
                            e.tensor_tensor(tmp[:, :, :], logits[:, :, :], over(best[:, :]), ALU.subtract
                                            ).then_inc(sm_in, 1)
                            e.wait_ge(sm_out, 1)
                            s.chain(e.tensor_reduce(total[:, :], sel[:, :, :], AX.X, ALU.add))
                            s.chain(e.reciprocal(rtotal[:, :], total[:, :]))
                            s.chain(e.tensor_tensor(score[:, :, :], sel[:, :, :], over(rtotal[:, :]), ALU.mult))
                            s.chain(e.tensor_copy(sel[:, :, :], score[:, :, :]))
                        for n, top in enumerate((top1, top2)):
                            s.chain(e.tensor_reduce(best[:, :], sel[:, :, :], AX.X, ALU.max))
                            s.chain(e.tensor_tensor(eq[:, :, :], sel[:, :, :], over(best[:, :]), ALU.is_equal))
                            s.chain(e.tensor_tensor(eq[:, :, :], eq[:, :, :],
                                                    rev.unsqueeze(1).to_broadcast([P, T, E]), ALU.mult))
                            s.chain(e.tensor_reduce(best[:, :], eq[:, :, :], AX.X, ALU.max))
                            s.chain(e.tensor_tensor(top[:, :, :], eq[:, :, :], over(best[:, :]), ALU.is_equal))
                            if n == 0:
                                s.chain(e.scalar_tensor_tensor(sel[:, :, :], top[:, :, :], NEG, sel[:, :, :],
                                                               ALU.mult, ALU.add))
                        s.step(e.tensor_tensor(tmp[:, :, :], top1[:, :, :], score[:, :, :], ALU.mult))
                        s.chain(e.tensor_tensor(eq[:, :, :], top2[:, :, :], score[:, :, :], ALU.mult))
                        e.tensor_tensor(both[:, :, :], top1[:, :, :], top2[:, :, :], ALU.add).then_inc(chosen, 1)
                        s.step(e.tensor_reduce(weight[:, :, 0], tmp[:, :, :], AX.X, ALU.add))
                        s.chain(e.tensor_reduce(weight[:, :, 1], eq[:, :, :], AX.X, ALU.add))
                        s.chain(e.tensor_tensor(total[:, :], weight[:, :, 0], weight[:, :, 1], ALU.add))
                        if layer == 0:
                            s.chain(e.tensor_scalar(total[:, :], total[:, :], 1e-20, None, ALU.add))
                        s.chain(e.reciprocal(rtotal[:, :], total[:, :]))
                        s.step(e.tensor_tensor(weight[:, :, 0], weight[:, :, 0], rtotal[:, :], ALU.mult))
                        s.step(e.tensor_tensor(weight[:, :, 1], weight[:, :, 1], rtotal[:, :], ALU.mult))
                        e.wait_ge(counted, 1)
                        s.chain(e.tensor_copy(percnt[:, :, :], ps(1)[:, 0:T * E].rearrange("p (t e) -> p e t", e=E)))
                        flat = lambda x: x[:, :, :].rearrange("p e t -> p (e t)")
                        s.chain(e.tensor_tensor_scan(flat(upto_), keep, flat(percnt), 0.0, ALU.mult, ALU.add))
                        s.step(e.tensor_tensor(before[:, :, :], upto_[:, :, :], percnt[:, :, :], ALU.subtract))
                        s.chain(e.tensor_tensor(overs[:, :, :], first.unsqueeze(1).to_broadcast([P, E, T]),
                                                upto_[:, :, T - 1:T].to_broadcast([P, E, T]), ALU.is_lt))
                        s.chain(e.tensor_reduce(ntile[:, :], overs[:, :, :], AX.X, ALU.add))
                        s.chain(e.tensor_tensor_scan(end[:, :], keep[:, 1:1 + E], ntile[:, :], 0.0, ALU.mult, ALU.add))
                        s.chain(e.tensor_tensor(base[:, :], end[:, :], ntile[:, :], ALU.subtract))
                        s.chain(e.tensor_scalar(base[:, :], base[:, :], float(P), None, ALU.mult))
                        s.chain(e.tensor_tensor(before[:, :, :], before[:, :, :],
                                                base[:, :].unsqueeze(2).to_broadcast([P, E, T]), ALU.add))
                        s.chain(e.tensor_tensor(tmp[:, :, :], ps(0)[:, 0:T * E].rearrange("p (t e) -> p t e", e=E),
                                                before[:, :, :].rearrange("p e t -> p t e"), ALU.add))
                        for n, top in enumerate((top1, top2)):
                            s.chain(e.tensor_tensor(eq[:, :, :], tmp[:, :, :], top[:, :, :], ALU.mult))
                            s.chain(e.tensor_reduce(at[:, :, n], eq[:, :, :], AX.X, ALU.add))
                        s.step(e.tensor_copy(pos[:, :, :], at[:, :, :]))
                        s.chain(e.tensor_tensor(passed[:, :, :], end[:, :].unsqueeze(1).to_broadcast([P, XT, E]),
                                                tiles.unsqueeze(2).to_broadcast([P, XT, E]), ALU.is_le))
                        s.chain(e.tensor_reduce(eidf[:, :], passed[:, :, :], AX.X, ALU.add))
                        s.chain(e.tensor_scalar(eid[:, :], eidf[:, :], float(E - 1), None, ALU.min))

        def dispatch(name, xkeep, pos):
            U = 4
            with ExitStack() as ctx:
                row = [sb_in(ctx, f"{name}_row{u}", [P, D]) for u in range(U)]
                idx = [sb_in(ctx, f"{name}_idx{u}", [P, 2], I32) for u in range(U)]
                turn = sem_in(ctx, name + "_turn")
                row_ready, idx_ready = sem_in(ctx, name + "_row_ready", name + "_idx_ready")
                sent = [sem_in(top, f"{name}_sent{u}") for u in range(U)]
                with nc.Block() as block:
                    @block.scalar
                    def _(e):
                        with e.Fori(0, T // U) as i:
                            for u in range(U):
                                e.wait_ge(sent[u], i * 32)
                                e.activation(row[u][:, :], xkeep[:, i * U + u, :], ACT.Identity).then_inc(row_ready, 1)

                    @block.vector
                    def _(e):
                        with e.Fori(0, T // U) as i:
                            for u in range(U):
                                e.wait_ge(sent[u], i * 32)
                                e.tensor_copy(idx[u][:, :], pos[:, i * U + u, :]).then_inc(idx_ready, 1)

                    @block.gpsimd
                    def _(e):
                        e.wait_ge(zero_filled, 16)
                        with e.Fori(0, T // U) as i:
                            for u in range(U):
                                e.wait_ge(row_ready, i * U + u + 1)
                                e.wait_ge(idx_ready, i * U + u + 1)
                                e.sem_inc(turn, 1)
                                for n in range(2):
                                    e.indirect_dma_start(slots_x, bass.IndirectOffsetOnAxis(
                                        idx[u][:, n:n + 1].bitcast(U32), 0), row[u][:, :], None).then_inc(sent[u], 16)
                        for u in range(U):
                            e.wait_ge(sent[u], T // U * 32)

        def combine(name, pos, weight, last):
            U = 4
            with ExitStack() as ctx:
                got = [sb_in(ctx, f"{name}_got{u}", [P, 2, D]) for u in range(U)]
                idx = [sb_in(ctx, f"{name}_idx{u}", [P, 2], I32) for u in range(U)]
                turn = sem_in(ctx, name + "_turn")
                idx_ready, half, taken = sem_in(ctx, name + "_idx_ready", name + "_half", name + "_taken")
                here = [sem_in(top, f"{name}_here{u}") for u in range(U)]
                with nc.Block() as block:
                    @block.scalar
                    def _(e):
                        with e.Fori(0, T // U) as i:
                            for u in range(U):
                                e.wait_ge(here[u], i * 32)
                                e.activation(idx[u][:, :], pos[:, i * U + u, :], ACT.Copy).then_inc(idx_ready, 1)

                    @block.gpsimd
                    def _(e):
                        with e.Fori(0, T // U) as i:
                            for u in range(U):
                                e.wait_ge(idx_ready, i * U + u + 1)
                                e.wait_ge(taken, i * U)
                                e.sem_inc(turn, 1)
                                for n in range(2):
                                    e.indirect_dma_start(got[u][:, n, :], None, slots_y, bass.IndirectOffsetOnAxis(
                                        idx[u][:, n:n + 1].bitcast(U32), 0)).then_inc(here[u], 16)

                    @block.vector
                    def _(e):
                        with e.Fori(0, T // U) as i:
                            for u in range(U):
                                t = i * U + u
                                e.wait_ge(here[u], i * 32 + 32)
                                e.scalar_tensor_tensor(h[:, t, :], got[u][:, 0, :], weight[:, t, 0:1], h[:, t, :],
                                                       ALU.mult, ALU.add).then_inc(half, 1)
                                e.wait_ge(half, t + 1)
                                e.scalar_tensor_tensor(h[:, t, :], got[u][:, 1, :], weight[:, t, 1:2], h[:, t, :],
                                                       ALU.mult, ALU.add).then_inc(taken, 1)
                                if not last:
                                    e.wait_ge(taken, t + 1)
                                    row_stats(e, t)

                    if last:
                        @block.sync
                        def _(e):
                            rows = out.rearrange("b (g p) d -> p (b g) d", p=P)
                            with e.Fori(0, T // U) as i:
                                e.wait_ge(taken, i * U + U)
                                e.dma_start(rows[:, bass.ds(i * U, U), :], h[:, bass.ds(i * U, U), :]
                                            ).then_inc(stored, 16)
                            e.wait_ge(stored, 16 * (T // U))

        def experts(name, layer, eid, w1, w2, bias2):
            U = 4
            H = D if layer == 0 else HID
            HC = H // (K if layer == 0 else P)
            HK = H // HC
            with ExitStack() as ctx:
                xg = [sb_in(ctx, f"{name}_xg{u}", [P, D]) for u in range(U)]
                yo = [sb_in(ctx, f"{name}_yo{u}", [P, D]) for u in range(U)]
                xT = sb_in(ctx, name + "_xT", [K + 1, C, P])
                pos_part = sb_in(ctx, name + "_relu", [P, D])
                hid = sb_in(ctx, name + "_hid", [P, H])
                hidT = sb_in(ctx, name + "_hidT", [HK, HC, P])
                loaded = [sem_in(ctx, f"{name}_loaded{u}") for u in range(U)]
                put = [sem_in(top, f"{name}_put{u}") for u in range(U)]
                (xT_psum, xT_ready, hid_psum, relu_ready, hid_ready, hT_psum, hT_ready, y_psum, y_ready, ones) = sem_in(
                    ctx, *(name + n for n in ("_xT_in_psum", "_xT_ready", "_hidden_in_psum", "_relu_ready",
                                              "_hidden_ready", "_hiddenT_in_psum", "_hiddenT_ready", "_y_in_psum",
                                              "_y_ready", "_ones_row")))
                XPS, HPS, TPS, YPS = ps(0), bank[1], bank[2], ps(1)
                HN = H if layer == 0 else H // 2
                x_rows = slots_x.rearrange("(s p) d -> s p d", p=P)
                y_rows = slots_y.rearrange("(s p) d -> s p d", p=P)
                with nc.Block() as block:
                    @block.sync
                    def _(e):
                        for s in range(U):
                            e.dma_start(xg[s][:, :], x_rows[s]).then_inc(loaded[s], 16)
                        with e.Fori(1, XT // U) as i:
                            for u in range(U):
                                e.wait_ge(xT_psum, i * U + u - U + 1)
                                e.dma_start(xg[u][:, :], x_rows[i * U + u]).then_inc(loaded[u], 16)

                    @block.gpsimd
                    def _(e):
                        e.memset(xT[K:K + 1, :, :], 1.0).then_inc(ones, 1)
                        with e.Fori(0, XT // U) as i:
                            for u in range(U):
                                e.wait_ge(y_ready, i * U + u + 1)
                                e.dma_start(y_rows[i * U + u], yo[u][:, :]).then_inc(put[u], 16)
                        for u in range(U):
                            e.wait_ge(put[u], XT // U * 16)

                    @block.tensor
                    def _(e):
                        def turn_x(s, u, n):
                            e.wait_ge(loaded[u], n)
                            e.wait_ge(xT_ready, s)
                            for c in range(C):
                                m = e.transpose(XPS[0:K, c * P:(c + 1) * P], xg[u][:, c * K:(c + 1) * K], ident[:, :])
                            m.then_inc(xT_psum, 1)

                        def up(s, ex):
                            e.wait_ge(xT_ready, s + 1)
                            e.wait_ge(hid_ready, s)
                            for n in range(H // HN):
                                for c in range(C):
                                    kk = K + (c if layer else 0)
                                    m = e.matmul(HPS[:, n, 0:HN], xT[0:kk, c, :],
                                                 w1[0:kk, ex, c, n * HN:(n + 1) * HN],
                                                 start=(c == 0), stop=(c == C - 1))
                            m.then_inc(hid_psum, 1)

                        def turn_hidden(s):
                            e.wait_ge(hid_ready, s + 1)
                            e.wait_ge(hT_ready, s)
                            for c in range(HC):
                                m = e.transpose(TPS[0:HK, c // 4, c % 4 * P:(c % 4 + 1) * P],
                                                hid[:, c * HK:(c + 1) * HK], ident[:, :])
                            m.then_inc(hT_psum, 1)

                        def down(s, ex):
                            e.wait_ge(hT_ready, s + 1)
                            e.wait_ge(y_ready, s)
                            for c in range(HC):
                                m = e.matmul(YPS[:, 0:D], hidT[:, c, :], w2[0:HK, ex, c, :],
                                             start=(c == 0), stop=(c == HC - 1))
                            m.then_inc(y_psum, 1)

                        def expert(s):
                            return e.value_load(eid[0:1, bass.ds(s, 1)], min_val=0, max_val=E - 1)

                        e.wait_ge(wload, wneed[layer])
                        e.wait_ge(ones, 1)
                        turn_x(0, 0, 16)
                        up(0, expert(0))
                        turn_x(1, 1, 16)
                        turn_hidden(0)
                        with e.Fori(0, (XT - 2) // U) as i:
                            for j in range(U):
                                s = i * U + 1 + j
                                up(s, expert(s))
                                u = (j + 2) % U
                                turn_x(s + 1, u, (i + 1) * 16 + (16 if j + 2 >= U else 0))
                                down(s - 1, expert(s - 1))
                                turn_hidden(s)
                        for s in range(1 + (XT - 2) // U * U, XT):
                            up(s, expert(s))
                            if s + 1 < XT:
                                turn_x(s + 1, (s + 1) % U, ((s + 1) // U + 1) * 16)
                            down(s - 1, expert(s - 1))
                            turn_hidden(s)
                        down(XT - 1, expert(XT - 1))

                    @block.scalar
                    def _(e):
                        def xT_out(s):
                            e.wait_ge(xT_psum, s + 1)
                            e.wait_ge(hid_psum, s)
                            e.activation(xT[0:K, :, :], XPS[0:K, 0:C * P].rearrange("p (c t) -> p c t", c=C),
                                         ACT.Copy).then_inc(xT_ready, 1)

                        def hid_out(s):
                            e.wait_ge(hid_psum, s + 1)
                            if layer == 0:
                                e.wait_ge(hid_ready, s)
                                e.activation(pos_part[:, :], HPS[:, 0, 0:D], ACT.Relu).then_inc(relu_ready, 1)
                            else:
                                e.wait_ge(hT_psum, s)
                                e.activation(hid[:, :].rearrange("p (n f) -> p n f", n=2), HPS[:, :, 0:HN],
                                             ACT.Gelu_apprx_tanh).then_inc(hid_ready, 1)

                        if layer == 0:
                            xT_out(0)
                        with e.Fori(0, XT - 1) as s:
                            hid_out(s)
                            if layer == 0:
                                xT_out(s + 1)
                        hid_out(XT - 1)

                    @block.vector
                    def _(e):
                        def xT_out(s):
                            e.wait_ge(xT_psum, s + 1)
                            e.wait_ge(hid_psum, s)
                            e.tensor_copy(xT[0:K, :, :], XPS[0:K, 0:C * P].rearrange("p (c t) -> p c t", c=C)
                                          ).then_inc(xT_ready, 1)

                        def squares(s):
                            e.wait_ge(relu_ready, s + 1)
                            e.wait_ge(hT_psum, s)
                            e.tensor_tensor(hid[:, :], HPS[:, 0, 0:D], pos_part[:, :], ALU.mult).then_inc(hid_ready, 1)

                        def hT_out(s):
                            e.wait_ge(hT_psum, s + 1)
                            e.wait_ge(y_psum, s)
                            if layer == 0:
                                e.tensor_copy(hidT[:, :, :], TPS[0:HK, 0, 0:HC * P].rearrange("p (c t) -> p c t", c=HC)
                                              ).then_inc(hT_ready, 1)
                            else:
                                e.tensor_copy(hidT[:, 0:4, :], TPS[:, 0, :].rearrange("p (c t) -> p c t", c=4))
                                e.tensor_copy(hidT[:, 4:6, :], TPS[:, 1, 0:2 * P].rearrange("p (c t) -> p c t", c=2)
                                              ).then_inc(hT_ready, 1)

                        def y_out(s, u, n):
                            e.wait_ge(y_psum, s + 1)
                            e.wait_ge(put[u], n)
                            if layer == 0:
                                e.tensor_copy(yo[u][:, :], YPS[:, 0:D]).then_inc(y_ready, 1)
                            else:
                                ex = e.value_load(eid[0:1, bass.ds(s, 1)], min_val=0, max_val=E - 1)
                                e.tensor_tensor(yo[u][:, :], YPS[:, 0:D], bias2[:, ex, :], ALU.add).then_inc(y_ready, 1)

                        if layer:
                            e.wait_ge(wload, wneed[layer])
                            xT_out(0)
                            xT_out(1)
                        else:
                            squares(0)
                        hT_out(0)
                        with e.Fori(0, (XT - 2) // U) as i:
                            for j in range(U):
                                s = i * U + 1 + j
                                if layer:
                                    xT_out(s + 1)
                                else:
                                    squares(s)
                                y_out(s - 1, j, i * 16)
                                hT_out(s)
                        for s in range(1 + (XT - 2) // U * U, XT):
                            if layer == 0:
                                squares(s)
                            elif s + 1 < XT:
                                xT_out(s + 1)
                            y_out(s - 1, (s - 1) % U, (s - 1) // U * 16)
                            hT_out(s)
                        y_out(XT - 1, (XT - 1) % U, (XT - 1) // U * 16)

        wneed = [16 * 2, 16 * 2 + 16 * 4]

        def moe(layer):
            name = f"moe{layer}"
            with ExitStack() as ctx:
                sb = lambda n, *x: sb_in(ctx, f"{name}_{n}", *x)
                pos = sb("pos", [P, T, 2], I32)
                weight = sb("weight", [P, T, 2])
                eid = sb("eid", [P, XT], I32)
                w1 = sb("w1", [K + 1, E, C, D if layer == 0 else HID])
                w2 = sb("w2", [K, E, C, D] if layer == 0 else [P, E, HT, D])
                bias2 = sb("bias2", [P, E, D]) if layer else None
                with ExitStack() as c1:
                    xkeep = sb_in(c1, name + "_xkeep", [P, T, D])
                    with ExitStack() as c2:
                        logits = sb_in(c2, name + "_logits", [P, T, E])
                        bias = sb_in(c2, name + "_bias", [P, E])
                        rt = sb_in(c2, name + "_tables", [P, 40 + XT + 256])
                        moe_pre(name, layer, xkeep, logits, bias, rt, w1, w2, bias2)
                        route(name, layer, logits, pos, weight, eid, bias, rt)
                    dispatch(name + "_dispatch", xkeep, pos)
                experts(name + "_experts", layer, eid, w1, w2, bias2)
                combine(name + "_combine", pos, weight, layer == 1)

        def moe_pre(name, layer, xkeep, logits, bias, rt, w1, w2, bias2):
            with ExitStack() as ctx:
                sb = lambda n, *x: sb_in(ctx, f"{name}_{n}", *x)
                ln = ln_tensors(ctx, name)
                router = sb("router", [K + 1, C, E])
                xn = sb("xn", [P, G, D])
                xT = sb("xT", [K + 1, C, S])
                if layer == 0:
                    wfc, wproj = sb("wfc", [K, C, D]), sb("wproj", [K, C, D])
                    relu, hT = sb("relu", [K, C, S]), sb("hT", [K, C, S])
                (load, ones, xn_ready, xT_psum, xT_ready, kept, l_psum, l_ready, hid_psum, relu_ready, hT_ready, o_psum,
                 o_ready) = sem_in(ctx, *(f"{name}_{n}" for n in (
                     "pre_load", "pre_ones", "xn_ready", "xT_in_psum", "xT_ready", "xn_kept", "logits_in_psum",
                     "logits_ready", "shared_in_psum", "shared_relu", "shared_hT_ready", "shared_out_in_psum",
                     "shared_added")))
                TURNED, LPS, HPS, OPS = ps(0), ps(1), ps(2), ps(3)
                nload = 16 * (6 if layer == 0 else 4)
                with nc.Block() as block:
                    @block.sync
                    def _(e):
                        e.dma_start(router[0:K, :, :], a[f"router{layer}"]).then_inc(load, 16)
                        e.dma_start(rt[:, :], a["c_route"]).then_inc(load, 16)
                        if layer == 0:
                            e.dma_start(bias[:, :], a["balance"].partition_broadcast(P)).then_inc(load, 16)
                            e.dma_start(wfc[:, :, :], a["w_fc_sh"]).then_inc(load, 16)
                            e.dma_start(wproj[:, :, :], a["w_proj_sh"]).then_inc(load, 16)
                            e.dma_start(router[K:K + 1, :, :], a["no_bias"]).then_inc(load, 16)
                            e.dma_start(w1[0:K, :, :, :], a["w1_0"]).then_inc(wload, 16)
                            e.dma_start(w2[:, :, :, :], a["w2_0"]).then_inc(wload, 16)
                        else:
                            e.dma_start(router[K:K + 1, 0, :], a["br"]).then_inc(load, 16)
                            e.dma_start(router[K:K + 1, 1, :], a["br"]).then_inc(load, 16)
                            e.dma_start(w1[0:K, :, :, :], a["w1_1"]).then_inc(wload, 16)
                            e.dma_start(w1[K:K + 1, :, 1, :], a["bfc"]).then_inc(wload, 16)
                            e.dma_start(w2[:, :, :, :], a["w2_1"]).then_inc(wload, 16)
                            e.dma_start(bias2[:, :, :], a["bproj"].partition_broadcast(P)).then_inc(wload, 16)

                    @block.gpsimd
                    def _(e):
                        e.memset(xT[K:K + 1, :, :], 1.0).then_inc(ones, 1)
                        e.wait_ge(ones, 1)
                        with e.Fori(0, B) as i:
                            e.wait_ge(xn_ready, (i + 1) * G)
                            e.tensor_copy(xkeep[:, bass.ds(i * G, G), :], xn[:, :, :]).then_inc(kept, 1)
                            if layer == 0:
                                e.wait_ge(relu_ready, i + 1)
                                e.wait_ge(o_psum, i)
                                e.tensor_tensor(hT[:, :, :], relu[:, :, :], relu[:, :, :], ALU.mult
                                                ).then_inc(hT_ready, 1)

                    @block.tensor
                    def _(e):
                        def turn_x(i):
                            e.wait_ge(xn_ready, (i + 1) * G)
                            e.wait_ge(xT_ready, i)
                            turn(e, TURNED, xn).then_inc(xT_psum, 1)

                        def logit(i):
                            e.wait_ge(xT_ready, i + 1)
                            e.wait_ge(l_ready, i)
                            for g in range(G):
                                for c in range(C):
                                    kk = K + c
                                    m = e.matmul(LPS[:, g * E:(g + 1) * E], xT[0:kk, c, g * P:(g + 1) * P],
                                                 router[0:kk, c, :], start=(c == 0), stop=(c == C - 1))
                            m.then_inc(l_psum, 1)

                        def hidden(i):
                            e.wait_ge(relu_ready, i)
                            for n in range(C):
                                for c in range(C):
                                    m = e.matmul(HPS[0:K, n * S:(n + 1) * S], wfc[:, c, n * K:(n + 1) * K],
                                                 xT[0:K, c, :], start=(c == 0), stop=(c == C - 1))
                            m.then_inc(hid_psum, 1)

                        def shared_out(i):
                            e.wait_ge(hT_ready, i + 1)
                            e.wait_ge(o_ready, i)
                            for g in range(G):
                                for c in range(C):
                                    m = e.matmul(OPS[:, g * D:(g + 1) * D], hT[:, c, g * P:(g + 1) * P], wproj[:, c, :],
                                                 start=(c == 0), stop=(c == C - 1))
                            m.then_inc(o_psum, 1)

                        e.wait_ge(load, nload)
                        e.wait_ge(ones, 1)
                        turn_x(0)

                        def body(i, more):
                            logit(i)
                            if layer == 0:
                                hidden(i)
                            if more:
                                turn_x(i + 1)

                        body(0, True)
                        with e.Fori(1, B - 1) as i:
                            body(i, True)
                            if layer == 0:
                                shared_out(i - 1)
                        body(B - 1, False)
                        if layer == 0:
                            shared_out(B - 2)
                            shared_out(B - 1)

                    @block.scalar
                    def _(e):
                        root(e, ln)
                        with e.Fori(0, B) as i:
                            e.wait_ge(xT_psum, i + 1)
                            e.wait_ge(l_psum, i)
                            if layer == 0:
                                e.wait_ge(hid_psum, i)
                            e.activation(xT[0:K, :, :], TURNED[0:K, :].rearrange("p (c t) -> p c t", c=C),
                                         ACT.Identity).then_inc(xT_ready, 1)
                            if layer == 0:
                                e.wait_ge(hid_psum, i + 1)
                                e.wait_ge(hT_ready, i)
                                e.activation(relu[:, :, :], HPS[0:K, :].rearrange("p (c t) -> p c t", c=C),
                                             ACT.Relu).then_inc(relu_ready, 1)

                    @block.vector
                    def _(e):
                        statistics(e, ln)

                        def norm(i):
                            e.wait_ge(xT_psum, i)
                            e.wait_ge(kept, i)
                            for g in range(G):
                                normalise(e, xn, i, g).then_inc(xn_ready, 1)

                        def logits_out(i):
                            e.wait_ge(l_psum, i + 1)
                            e.tensor_copy(logits[:, bass.ds(i * G, G), :], LPS[:, 0:G * E].rearrange(
                                "p (g e) -> p g e", g=G)).then_inc(l_ready, 1)

                        def add_h(i):
                            e.wait_ge(o_psum, i + 1)
                            hh = h[:, bass.ds(i * G, G), :]
                            e.tensor_tensor(hh, OPS[:, 0:G * D].rearrange("p (g d) -> p g d", g=G), hh,
                                            ALU.add).then_inc(o_ready, 1)

                        norm(0)
                        norm(1)
                        logits_out(0)
                        with e.Fori(1, B - 1) as i:
                            norm(i + 1)
                            logits_out(i)
                            if layer == 0:
                                add_h(i - 1)
                        logits_out(B - 1)
                        if layer == 0:
                            add_h(B - 2)
                            add_h(B - 1)

        tokens()
        hyena()
        moe(0)
        nc.clear_and_free_semaphores(stage_sems)
        del stage_sems[:]
        with nc.Block():
            pass
        attention()
        moe(1)


def _chunks(w, rows=96):
    return w.reshape(-1, rows, w.shape[-1]).transpose(1, 0, 2)


def _experts(w, rows):
    return w.reshape(w.shape[0], -1, rows, w.shape[-1]).transpose(2, 0, 1, 3)


def _constants():
    import numpy as np
    c = {}
    f32 = np.float32
    c["c_ident"] = np.eye(128, dtype=f32)
    arg = (np.arange(256, dtype=f32)[:, None] * np.arange(64, dtype=f32)[None] / f32(64)).astype(np.float64)
    c["c_basis"] = np.concatenate([np.sin(arg).T, np.ones((1, 256))]).astype(f32)
    n = 384
    w = np.arange(192)
    t = np.arange(256)
    th = lambda k: 2 * np.pi * ((w[:, None] * k[None]) % n) / n
    alt = lambda k: np.where(k % 2 == 0, 1.0, -1.0)
    cos_, sin_ = np.cos(th(t)), np.sin(th(t))
    sin_[0] = alt(t)
    c["c_fwd"] = np.concatenate([cos_, sin_]).T.reshape(2, 128, 384).transpose(1, 0, 2).astype(f32)
    k = t - 128
    p, q = np.cos(th(k)), np.sin(th(k))
    r = -p.copy()
    r[0] = -alt(k)
    c["c_to_spec"] = np.concatenate([p, q, r]).T.reshape(2, 128, 576).transpose(1, 0, 2).astype(f32)
    two = np.where(w == 0, 1.0, 2.0)[:, None] / n
    ic, is_ = np.cos(th(t)) * two, -np.sin(th(t)) * two
    is_[0] = -alt(t) / n
    c["c_inv"] = np.concatenate([ic, is_]).reshape(4, 96, 256).transpose(1, 0, 2).astype(f32)
    keep = np.ones((8, 32))
    keep[:, 0] = 0
    c["c_route"] = np.tile(np.concatenate([8 - np.arange(8), 128 * np.arange(32), np.arange(72), keep.ravel()])[None],
                           (128, 1)).astype(f32)
    c["c_upper"] = np.triu(np.ones((128, 128)), 1).astype(f32)
    c["no_bias"] = np.zeros((1, 2, 8), f32)
    b16 = np.dtype("bfloat16")
    inv_freq = f32(1) / f32(10000) ** (np.arange(0, 16, 2, dtype=f32) / f32(16))
    ang = (np.arange(256, dtype=f32)[:, None] * inv_freq[None]).astype(f32).astype(np.float64)
    cs = np.stack([np.concatenate([np.cos(ang)] * 2, 1), np.concatenate([-np.sin(ang), np.sin(ang)], 1)], 1).astype(f32)
    c["c_rope"] = np.stack([cs * f32(0.25), cs], 1).reshape(2, 128, 2, 2, 16).transpose(1, 0, 2, 3, 4)
    c["c_identb"] = np.eye(128).astype(b16)
    q, k = np.arange(128)[:, None], np.arange(128)[None]
    causal = np.where((q // 64 == k // 64) & (k > q), -1e30, 0.0)
    c["c_causal"], c["c_causalT"] = causal.astype(b16), causal.T.astype(b16)
    key = np.zeros((12, 8, 12, 2, 128))
    for hd in range(12):
        for n in range(4):
            key[hd, n, hd] = (np.arange(256) // 64 == n).reshape(2, 128)
        key[hd, 4:7, hd] = 1
    c["c_keyside"] = key.reshape(96, 12, 2, 128).astype(b16)
    drop = np.zeros((128, 12, 2, 4))
    drop[:, :, 0, 3] = drop[:64, :, 1, 3] = -1e30
    c["c_drop"] = drop.astype(f32)
    return {k: np.ascontiguousarray(v) for k, v in c.items()}


def _arrays(i):
    import numpy as np
    i = {k: np.asarray(v) for k, v in i.items()}
    r = {}
    r["x"] = i["x"].transpose(2, 3, 0, 1).reshape(84 * 84, 48)
    r["curve"] = i["L0_tok_curve"]
    tw = np.zeros((49, 16, 192), np.float32)
    for b in range(16):
        tw[3 * b:3 * b + 3, b] = i["L0_tok_proj_w"].T
        tw[48, b] = i["L0_tok_proj_b"]
    r["tok_w"] = tw
    r["w_in"] = _chunks(i["L0_attn_w_in"])
    r["b_in"] = i["L0_attn_b_in"].reshape(1, 768)
    r["w_filt"] = i["L0_attn_w_filt"]
    r["b_filt"] = i["L0_attn_b_filt"].reshape(1, 192)
    r["short"] = np.concatenate([i["L0_attn_w_short"][:, 0, :], i["L0_attn_b_short"][:, None]], 1
                                ).reshape(2, 96, 4).transpose(1, 0, 2)
    r["w_out"] = _chunks(i["L0_attn_w_out"])
    r["b_out"] = i["L0_attn_b_out"].reshape(1, 192)
    r["router0"] = _chunks(i["L0_ffn_router_w"].T)
    r["balance"] = i["L0_ffn_balance_bias"]
    r["w_fc_sh"] = _chunks(i["L0_ffn_w_fc_sh"])
    r["w_proj_sh"] = _chunks(i["L0_ffn_w_proj_sh"])
    r["w1_0"] = _experts(i["L0_ffn_w1"], 96)
    r["w2_0"] = _experts(i["L0_ffn_w2"], 96)
    r["router1"] = _chunks(i["L1_ffn_Wr"])
    r["br"] = i["L1_ffn_br"].reshape(1, 8)
    r["w1_1"] = _experts(i["L1_ffn_Wfc"], 96)
    r["bfc"] = i["L1_ffn_bfc"].reshape(1, 8, 768)
    r["w2_1"] = _experts(i["L1_ffn_Wproj"], 128)
    r["bproj"] = i["L1_ffn_bproj"]
    r["wqkv"] = _chunks(np.concatenate([i["L1_attn_Wq"].T, i["L1_attn_Wk"].T, i["L1_attn_Wv"].T], 1))
    wo = np.zeros((3, 4, 32, 192), np.float32)
    wo[:, :, :16] = i["L1_attn_Wo"].T.reshape(3, 4, 16, 192)
    r["wo"] = wo.reshape(3, 128, 192).transpose(1, 0, 2)
    r.update(_constants())
    return {k: np.ascontiguousarray(v) for k, v in r.items()}


def kernel(**inputs):
    import numpy as np
    import concourse.bacc as bacc
    from concourse import mybir
    from concourse.bass_utils import run_bass_kernel_spmd

    nc = bacc.Bacc("TRN2", target_bir_lowering=False, num_devices=1)
    arrays, args = {}, {}
    for name, array in _arrays(inputs).items():
        arrays[f"in_{name}_dram"] = array
        args[name] = nc.dram_tensor(f"in_{name}_dram", array.shape, mybir.dt.from_np(array.dtype),
                                    kind="ExternalInput").ap()
    out = nc.dram_tensor("out_0_dram", (B, S, D), mybir.dt.from_np(np.dtype("float32")), kind="ExternalOutput").ap()
    build(nc, args, out)
    r = run_bass_kernel_spmd(nc, [arrays], core_ids=[0])
    return r.results[0]["out_0_dram"]
```

```python
from contextlib import ExitStack

import concourse.bass as bass
from concourse import mybir

F32 = mybir.dt.float32
BF16 = mybir.dt.bfloat16
I32 = mybir.dt.int32
U32 = mybir.dt.uint32
ALU = mybir.AluOpType
ACT = mybir.ActivationFunctionType
AX = mybir.AxisListType

P = 128
B, S, D = 16, 256, 192
G = S // P
T = B * G
C = 2
K = D // C
E = 8
XT = -(-2 * B * S // P) + E
HID = 768
HT = HID // P
HEADS, HD = 12, 16
HG = HEADS // 4
BLK = 64
NBLK = S // BLK
NEG = -1.0e30
EPS = 1e-5
RT_REV = slice(0, E)
RT_FIRST = slice(RT_REV.stop, RT_REV.stop + T)
RT_TILES = slice(RT_FIRST.stop, RT_FIRST.stop + XT)
RT_KEEP = slice(RT_TILES.stop, RT_TILES.stop + E * T)
RT_ROW = slice(RT_KEEP.stop, RT_KEEP.stop + P)
RT_NUMBER = slice(RT_ROW.stop, RT_ROW.stop + 2 * T)
RT_NO_TOKEN = slice(RT_NUMBER.stop, RT_NUMBER.stop + XT)
RT_PART = slice(RT_NO_TOKEN.stop, RT_NO_TOKEN.stop + 1)
RT = RT_PART.stop
IMG = 84


class Own:

    def __init__(self, eng, sem):
        self.eng, self.sem, self.base, self.k = eng, sem, 0, 0

    def step(self, ins):
        ins.then_inc(self.sem, 1)
        self.k += 1
        return ins

    def wait(self):
        self.eng.wait_ge(self.sem, self.base + self.k)

    def chain(self, ins):
        self.step(ins)
        self.wait()

    def enter(self, i, per):
        self.start = self.base + self.k
        self.per, self.k = per, 0
        self.base = self.start + i * per

    def leave(self, trips):
        assert self.k == self.per, (self.k, self.per)
        self.base, self.k = self.start + trips * self.per, 0


def until(e, sem, count):
    if not isinstance(count, int) or count > 0:
        e.wait_ge(sem, count)


def build(nc, a, out):
    top = ExitStack()
    with top:
        def sb_in(ctx, name, shape, dt=F32):
            return ctx.enter_context(nc.sbuf_tensor(name, shape, dt))

        stage_sems = []

        def sem_in(ctx, *names):
            made = [nc.alloc_semaphore(n) for n in names]
            if ctx is not top:
                stage_sems.extend(made)
            return made if len(made) > 1 else made[0]

        bank = [top.enter_context(nc.psum_tensor(f"bank{n}", [P, 2, 512], F32)) for n in range(4)]

        def ps(n):
            return bank[n // 2][:, n % 2, :]

        h = sb_in(top, "h", [P, T, D])
        stats = sb_in(top, "stats", [P, T, 6])
        mean = sb_in(top, "mean", [P, T])
        rstd = sb_in(top, "rstd", [P, T])
        ident = sb_in(top, "ident", [P, P])
        wload, setup_load = sem_in(top, "weights_loaded", "constants_loaded")
        stored = sem_in(top, "outputs_stored")

        x_rows = [nc.dram_tensor(f"x_rows{n}", (T * P, D), F32, kind="Internal").ap() for n in range(2)]
        y_rows = [nc.dram_tensor(f"y_rows{n}", ((2 * T + XT) * P, D), F32, kind="Internal").ap() for n in range(2)]

        def row_stats(eng, tile):
            return eng.bn_stats(stats[:, tile, :], h[:, tile, :])

        def tokens():
            with ExitStack() as ctx:
                sb = lambda *x: sb_in(ctx, *x)
                curve = sb("curve", [P, G, 2], I32)
                cf = sb("cf", [P, G, 2])
                neg = sb("neg", [P, G, 2])
                at = sb("at", [P, G], I32)
                atf = sb("atf", [P, G])
                pix = sb("pix", [P, G, 3 * B])
                pixT = sb("pixT", [3 * B + 1, G, P])
                wtok = sb("wtok", [3 * B + 1, B, D])
                load, ready = sem_in(ctx, "tok_load", "tok_index")
                gathered = sem_in(top, "tok_gathered")
                tr, trc, mm, hd, own, ones = sem_in(
                    ctx, "tok_pixT_in_psum", "tok_pixT", "tok_matmul", "tok_h", "tok_dve", "tok_ones")
                steps = [(g, b) for b in range(0, B, 2) for g in range(G)]
                with nc.Block() as block:
                    @block.sync
                    def _(e):
                        e.dma_start(curve[:, :, :], a["curve"].rearrange("(g p) c -> p g c", p=P)).then_inc(load, 16)
                        e.dma_start(ident[:, :], a["c_ident"]).then_inc(load, 16)
                        e.dma_start(wtok[:, :, :], a["tok_w"]).then_inc(load, 16)

                    @block.gpsimd
                    def _(e):
                        e.memset(pixT[:, :, :], 1.0).then_inc(ones, 1)
                        e.wait_ge(ready, 1)
                        for g in range(G):
                            e.indirect_dma_start(pix[:, g, :], None, a["x"], bass.IndirectOffsetOnAxis(
                                at[:, g:g + 1].bitcast(U32), 0)).then_inc(gathered, 16)

                    @block.vector
                    def _(e):
                        own_ = Own(e, own)
                        e.wait_ge(load, 48)
                        own_.chain(e.tensor_copy(cf[:, :, :], curve[:, :, :]))
                        own_.chain(e.tensor_scalar(neg[:, :, :], cf[:, :, :], 0.0, float(IMG), ALU.is_lt, ALU.mult))
                        own_.chain(e.tensor_tensor(cf[:, :, :], cf[:, :, :], neg[:, :, :], ALU.add))
                        own_.chain(e.tensor_scalar(cf[:, :, :], cf[:, :, :], 0.0, float(IMG - 1), ALU.max, ALU.min))
                        own_.chain(e.scalar_tensor_tensor(atf[:, :], cf[:, :, 1], float(IMG), cf[:, :, 0],
                                                          ALU.mult, ALU.add))
                        e.tensor_copy(at[:, :], atf[:, :]).then_inc(ready, 1)
                        e.wait_ge(ones, 1)
                        e.wait_ge(tr, 1)
                        e.tensor_copy(pixT[0:3 * B, :, :], ps(0)[0:3 * B, 0:G * P].rearrange("p (g t) -> p g t", g=G)
                                      ).then_inc(trc, 1)
                        for n, (g, b) in enumerate(steps):
                            e.wait_ge(mm, n + 1)
                            e.tensor_copy(h[:, b * G + g:(b + 1) * G + g + 1:G, :],
                                          ps(1 + n % 4)[:, 0:2 * D].rearrange("p (b d) -> p b d", b=2)
                                          ).then_inc(hd, 1)
                        e.wait_ge(hd, len(steps))
                        for t in range(T):
                            row_stats(e, t)

                    @block.tensor
                    def _(e):
                        e.wait_ge(load, 48)
                        e.wait_ge(gathered, 16 * G)
                        for g in range(G):
                            m = e.transpose(ps(0)[0:3 * B, g * P:(g + 1) * P], pix[:, g, :], ident[:, :])
                        m.then_inc(tr, 1)
                        e.wait_ge(trc, 1)
                        for n, (g, b) in enumerate(steps):
                            if n >= 4:
                                e.wait_ge(hd, n - 3)
                            e.matmul(ps(1 + n % 4)[:, 0:2 * D], pixT[:, g, :], wtok[:, b:b + 2, :].rearrange(
                                "p b d -> p (b d)"), start=True, stop=True).then_inc(mm, 1)

        def ln_tensors(ctx, name):
            return dict(own=sem_in(ctx, name + "_ln_step"), var=sem_in(ctx, name + "_ln_var"),
                        root=sem_in(ctx, name + "_ln_root"), tmp=sb_in(ctx, name + "_ln_tmp", [P, 4, T]))

        def statistics(e, ln):
            s = Own(e, ln["own"])
            t = ln["tmp"]
            m0, q0, m1, q1 = (stats[:, :, n] for n in (1, 2, 4, 5))
            s.step(e.tensor_tensor(t[:, 0, :], m0, m1, ALU.add))
            s.step(e.tensor_tensor(t[:, 1, :], m0, m1, ALU.subtract))
            s.step(e.tensor_tensor(t[:, 2, :], q0, q1, ALU.add))
            s.wait()
            s.step(e.tensor_scalar(mean[:, :], t[:, 0, :], 0.5, None, ALU.mult))
            s.chain(e.tensor_tensor(t[:, 3, :], t[:, 1, :], t[:, 1, :], ALU.mult))
            s.chain(e.scalar_tensor_tensor(t[:, 0, :], t[:, 3, :], D / 4.0, t[:, 2, :], ALU.mult, ALU.add))
            e.tensor_scalar(t[:, 1, :], t[:, 0, :], 1.0 / D, EPS, ALU.mult, ALU.add).then_inc(ln["var"], 1)
            e.wait_ge(ln["root"], 1)
            s.chain(e.reciprocal(rstd[:, :], t[:, 2, :]))

        def root(e, ln):
            e.wait_ge(ln["var"], 1)
            e.activation(ln["tmp"][:, 2, :], ln["tmp"][:, 1, :], ACT.Sqrt).then_inc(ln["root"], 1)

        def normalise(e, xn, i, g):
            t = i * G + g
            return e.tensor_scalar(xn[:, g, :], h[:, t, :], mean[:, t:t + 1] if isinstance(t, int) else mean[:, bass.ds(t, 1)],
                                   rstd[:, t:t + 1] if isinstance(t, int) else rstd[:, bass.ds(t, 1)],
                                   ALU.subtract, ALU.mult)

        def turn(e, psum, src):
            for c in range(C):
                for g in range(G):
                    m = e.transpose(psum[0:K, c * S + g * P:c * S + (g + 1) * P], src[:, g, c * K:(c + 1) * K],
                                    ident[:, :])
            return m

        def hyena():
            NF = 4
            with ExitStack() as ctx:
                sb = lambda *x: sb_in(ctx, *x)
                w_in = sb("w_in", [K + 1, C, 4 * D])
                w_out = sb("w_out", [K + 1, C, D])
                fwd = sb("fwd", [P, G, NF * K])
                inv = sb("inv", [K, NF, S])
                short = sb("short", [K, C, 4])
                specA = sb("specA", [K, 2, C * D])
                specB = sb("specB", [K, 2, C * D])
                ln = ln_tensors(ctx, "hy")
                load = sem_in(ctx, "hy_load")

                with ExitStack() as c2:
                    basis = sb_in(c2, "basis", [65, S])
                    wf = sb_in(c2, "wf", [65, D])
                    filt = sb_in(c2, "filt", [P, G, D])
                    to_spec = sb_in(c2, "to_spec", [P, G, 6 * K])
                    fl, fp, ff, sp, sc = sem_in(c2, "filter_load", "filter_in_psum", "filter", "spectrum_in_psum",
                                                "spectrum")
                    with nc.Block() as block:
                        @block.sync
                        def _(e):
                            e.dma_start(basis[:, :], a["c_basis"]).then_inc(fl, 16)
                            e.dma_start(wf[0:64, :], a["w_filt"]).then_inc(fl, 16)
                            e.dma_start(wf[64:65, :], a["b_filt"]).then_inc(fl, 16)
                            e.dma_start(to_spec[:, :, :], a["c_to_spec"]).then_inc(fl, 16)
                            e.dma_start(w_in[0:K, :, :], a["w_in"]).then_inc(load, 16)
                            e.dma_start(w_in[K:K + 1, 1, :], a["b_in"]).then_inc(load, 16)
                            e.dma_start(fwd[:, :, :], a["c_fwd"]).then_inc(load, 16)
                            e.dma_start(inv[:, :, :], a["c_inv"]).then_inc(load, 16)
                            e.dma_start(short[:, :, :], a["short"]).then_inc(load, 16)
                            e.dma_start(w_out[0:K, :, :], a["w_out"]).then_inc(load, 16)
                            e.dma_start(w_out[K:K + 1, 1, :], a["b_out"]).then_inc(load, 16)

                        @block.tensor
                        def _(e):
                            e.wait_ge(fl, 64)
                            for g in range(G):
                                m = e.matmul(ps(0)[:, g * D:(g + 1) * D], basis[:, g * P:(g + 1) * P], wf[:, :],
                                             start=True, stop=True)
                            m.then_inc(fp, 1)
                            e.wait_ge(ff, 1)
                            for n in range(6):
                                for g in range(G):
                                    m = e.matmul(ps(1 + n // 2)[0:K, (n % 2) * D:(n % 2 + 1) * D],
                                                 to_spec[:, g, n * K:(n + 1) * K], filt[:, g, :],
                                                 start=(g == 0), stop=(g == G - 1))
                            m.then_inc(sp, 1)

                        @block.vector
                        def _(e):
                            e.wait_ge(fp, 1)
                            e.tensor_copy(filt[:, :, :], ps(0)[:, 0:G * D].rearrange("p (g d) -> p g d", g=G)
                                          ).then_inc(ff, 1)
                            statistics(e, ln)
                            e.wait_ge(sp, 1)
                            for n, (spec, half) in enumerate(((specA, 0), (specA, 1), (specB, 1))):
                                e.tensor_copy(spec[:, half, :], ps(1 + n)[0:K, 0:C * D])
                            e.tensor_copy(specB[:, 0, :], ps(2)[0:K, 0:C * D])

                        @block.scalar
                        def _(e):
                            root(e, ln)

                xn = sb("xn", [P, G, D])
                xT = sb("xT", [K + 1, C, S])
                xp = sb("xp", [P, G, D])
                zs = sb("zs", [P, G, D])
                gate = sb("gate", [P, G, D])
                prA = sb("prA", [K, 2, C * D])
                prB = sb("prB", [K, 2, C * D])
                spec = sb("spec", [K, 2, C * D])
                y = sb("y", [P, G, D])
                xs = sb("xs", [K, C, S])
                yx = sb("yx", [K + 1, C, S])
                (xn_ready, xT_psum, xT_ready, xz_psum, xz_ready, v_psum, gate_ready, freq_psum, prod_ready, spec_ready,
                 conv_psum, y_ready, yT_psum, yx_ready, xs_begun, out_psum, h_ready, own, ones,
                 short_ready) = sem_in(
                    ctx, "hy_xn_ready", "hy_xT_in_psum", "hy_xT_ready", "hy_xz_in_psum", "hy_xz_ready", "hy_v_in_psum",
                    "hy_gate_ready", "hy_freq_in_psum", "hy_products_ready", "hy_spectrum_ready", "hy_conv_in_psum",
                    "hy_y_ready", "hy_yT_in_psum", "hy_yx_ready", "hy_short_begun", "hy_out_in_psum", "hy_h_ready",
                    "hy_dve_step", "hy_ones_rows",
                    "hy_short_ready")
                TURNED, XZ, VV, FREQ, CONV = ps(0), bank[1], bank[2], bank[3], ps(1)

                with nc.Block() as block:
                    @block.gpsimd
                    def _(e):
                        e.memset(xT[K:K + 1, :, :], 1.0).then_inc(ones, 1)
                        e.memset(yx[K:K + 1, :, :], 1.0).then_inc(ones, 1)
                        with e.Fori(0, B) as i:
                            e.wait_ge(prod_ready, (i + 1) * 2)
                            e.wait_ge(conv_psum, i)
                            e.tensor_tensor(spec[:, :, :], prA[:, :, :], prB[:, :, :], ALU.add).then_inc(spec_ready, 1)

                    @block.tensor
                    def _(e):
                        def turn_x(i):
                            e.wait_ge(xn_ready, (i + 1) * G)
                            turn(e, TURNED, xn).then_inc(xT_psum, 1)

                        def project(i, half, psum, done, free):
                            if half == 0:
                                e.wait_ge(xT_ready, i + 1)
                            e.wait_ge(free, i)
                            for g in range(G):
                                for c in range(C):
                                    kk = K + c
                                    m = e.matmul(psum[:, g, 0:2 * D], xT[0:kk, c, g * P:(g + 1) * P],
                                                 w_in[0:kk, c, half * 2 * D:(half + 1) * 2 * D],
                                                 start=(c == 0), stop=(c == C - 1))
                            m.then_inc(done, 1)

                        def forward(i):
                            e.wait_ge(xz_ready, i + 1)
                            e.wait_ge(prod_ready, i * 2)
                            for f in range(NF):
                                for g in range(G):
                                    m = e.matmul(FREQ[0:K, f // 2, (f % 2) * D:(f % 2 + 1) * D],
                                                 fwd[:, g, f * K:(f + 1) * K], xp[:, g, :],
                                                 start=(g == 0), stop=(g == G - 1))
                            m.then_inc(freq_psum, 1)

                        def inverse(i):
                            e.wait_ge(spec_ready, i + 1)
                            e.wait_ge(h_ready, i)
                            for g in range(G):
                                for f in range(NF):
                                    m = e.matmul(CONV[:, g * D:(g + 1) * D], inv[:, f, g * P:(g + 1) * P],
                                                 spec[:, f // 2, (f % 2) * D:(f % 2 + 1) * D],
                                                 start=(f == 0), stop=(f == NF - 1))
                            m.then_inc(conv_psum, 1)

                        def turn_y(i):
                            e.wait_ge(y_ready, i + 1)
                            turn(e, TURNED, y).then_inc(yT_psum, 1)

                        def project_out(i):
                            e.wait_ge(yx_ready, i + 1)
                            for g in range(G):
                                for c in range(C):
                                    kk = K + c
                                    m = e.matmul(CONV[:, g * D:(g + 1) * D], yx[0:kk, c, g * P:(g + 1) * P],
                                                 w_out[0:kk, c, :], start=(c == 0), stop=(c == C - 1))
                            m.then_inc(out_psum, 1)

                        e.wait_ge(load, 112)
                        e.wait_ge(ones, 2)
                        turn_x(0)
                        project(0, 0, XZ, xz_psum, xz_ready)
                        project(0, 1, VV, v_psum, gate_ready)
                        forward(0)
                        turn_x(1)

                        def body(i, more):
                            project(i, 0, XZ, xz_psum, xz_ready)
                            inverse(i - 1)
                            project(i, 1, VV, v_psum, gate_ready)
                            turn_y(i - 1)
                            forward(i)
                            if more:
                                e.wait_ge(yx_ready, i)
                                turn_x(i + 1)
                            project_out(i - 1)

                        with e.Fori(1, B - 1) as i:
                            body(i, True)
                        body(B - 1, False)
                        inverse(B - 1)
                        turn_y(B - 1)
                        project_out(B - 1)

                    @block.scalar
                    def _(e):
                        def xT_out(i):
                            e.wait_ge(xT_psum, i + 1)
                            e.wait_ge(v_psum, i)
                            e.wait_ge(short_ready, i * C)
                            e.activation(xT[0:K, :, :], TURNED[0:K, :].rearrange("p (c t) -> p c t", c=C),
                                         ACT.Copy).then_inc(xT_ready, 1)

                        def body(i, more):
                            e.wait_ge(xz_psum, i + 1)
                            e.wait_ge(freq_psum, i)
                            e.activation(xp[:, :, :], XZ[:, :, 0:D], ACT.Copy)
                            e.wait_ge(gate_ready, i)
                            e.activation(zs[:, :, :], XZ[:, :, D:2 * D], ACT.Silu).then_inc(xz_ready, 1)
                            e.wait_ge(yx_ready, i)
                            e.wait_ge(xT_ready, i + 1)
                            for c in range(C):
                                m = e.activation(xs[:, c, :], xT[0:K, c, :], ACT.Identity,
                                                 bias=short[:, c, 3:4], scale=short[:, c, 1:2])
                            m.then_inc(xs_begun, 1)
                            if more:
                                xT_out(i + 1)

                        e.wait_ge(load, 112)
                        xT_out(0)
                        with e.Fori(0, B - 1) as i:
                            body(i, True)
                        body(B - 1, False)

                    @block.vector
                    def _(e):
                        s = Own(e, own)

                        def norm(i):
                            e.wait_ge(xT_psum, i)
                            for g in range(G):
                                normalise(e, xn, i, g).then_inc(xn_ready, 1)

                        def conv_out(i):
                            e.wait_ge(conv_psum, i + 1)
                            e.wait_ge(yT_psum, i)
                            e.tensor_tensor(y[:, :, :], CONV[:, 0:G * D].rearrange("p (g d) -> p g d", g=G),
                                            gate[:, :, :], ALU.mult).then_inc(y_ready, 1)

                        def gates(i):
                            e.wait_ge(v_psum, i + 1)
                            e.wait_ge(xz_ready, i + 1)
                            e.wait_ge(y_ready, i)
                            s.chain(e.tensor_tensor(gate[:, :, :], VV[:, :, 0:D], zs[:, :, :], ALU.mult))
                            e.tensor_tensor(gate[:, :, :], VV[:, :, D:2 * D], gate[:, :, :], ALU.mult
                                            ).then_inc(gate_ready, 1)

                        def join(i):
                            e.wait_ge(yT_psum, i + 1)
                            e.wait_ge(out_psum, i)
                            e.wait_ge(short_ready, (i + 1) * C)
                            e.tensor_tensor(yx[0:K, :, :], TURNED[0:K, :].rearrange("p (c t) -> p c t", c=C),
                                            xs[:, :, :], ALU.add).then_inc(yx_ready, 1)

                        def short_conv(i):
                            e.wait_ge(xs_begun, i + 1)
                            for c in range(C):
                                s.step(e.scalar_tensor_tensor(xs[:, c, 1:S], xT[0:K, c, 0:S - 1], short[:, c, 0:1],
                                                              xs[:, c, 1:S], ALU.mult, ALU.add))
                            s.wait()
                            for c in range(C):
                                e.scalar_tensor_tensor(xs[:, c, 0:S - 1], xT[0:K, c, 1:S], short[:, c, 2:3],
                                                       xs[:, c, 0:S - 1], ALU.mult, ALU.add).then_inc(short_ready, 1)

                        def products(i):
                            e.wait_ge(freq_psum, i + 1)
                            e.wait_ge(spec_ready, i)
                            for n, (pr, sp) in enumerate(((prA, specA), (prB, specB))):
                                e.tensor_tensor(pr[:, :, :], FREQ[0:K, n, 0:C * D].unsqueeze(1).to_broadcast(
                                    [K, 2, C * D]), sp[:, :, :], ALU.mult).then_inc(prod_ready, 1)

                        def add_h(i):
                            e.wait_ge(out_psum, i + 1)
                            hh = h[:, bass.ds(i * G, G), :]
                            e.tensor_tensor(hh, CONV[:, 0:G * D].rearrange("p (g d) -> p g d", g=G), hh,
                                            ALU.add).then_inc(h_ready, 1)
                            e.wait_ge(h_ready, i + 1)
                            for g in range(G):
                                row_stats(e, i * G + g)

                        e.wait_ge(load, 112)
                        norm(0)
                        gates(0)
                        norm(1)
                        short_conv(0)
                        products(0)

                        def body(i, more):
                            conv_out(i - 1)
                            gates(i)
                            if more:
                                norm(i + 1)
                            join(i - 1)
                            short_conv(i)
                            products(i)
                            add_h(i - 1)

                        with e.Fori(1, B - 1) as i:
                            s.enter(i - 1, 3)
                            body(i, True)
                            s.leave(B - 2)
                        body(B - 1, False)
                        conv_out(B - 1)
                        join(B - 1)
                        add_h(B - 1)

        def attention():
            N = 2 * HEADS
            SL = 6 * HD
            NP = 6
            with ExitStack() as ctx:
                sb = lambda n, *x: sb_in(ctx, "at_" + n, *x)
                ln = ln_tensors(ctx, "at")
                wqkv = sb("wqkv", [K, C, 3 * D])
                wo = sb("wo", [P, HG, D])
                rope = sb("rope", [P, G, 2, 2, HD])
                identb = sb("identb", [P, P], BF16)
                causal = sb("causal", [P, P], BF16)
                causalT = sb("causalT", [P, P], BF16)
                keyside = sb("keyside", [SL, HEADS, G, P], BF16)
                xn = sb("xn", [P, G, D])
                xT = sb("xT", [K, C, S])
                tcos, tsin, xr, r1 = (sb(n, [P, 2, G, HEADS, HD]) for n in ("tcos", "tsin", "xr", "r1"))
                hi, mid = (sb(n, [P, 2, N, HD], BF16) for n in ("hi", "mid"))
                slots = sb("slots", [P, 2, N, 6, HD], BF16)
                qkT = [sb(f"qkT{n}", [SL, 2, HEADS, S], BF16) for n in range(2)]
                v1 = [sb(f"v1{n}", [P, G, HEADS, 2, HD]) for n in range(2)]
                bmax = sb("bmax", [P, HEADS, G, NBLK])
                bsum = sb("bsum", [P, HEADS, 3])
                least, other = sb("least", [P, HEADS]), sb("other", [P, HEADS])
                same = sb("same", [P, HEADS, 3])
                drop = sb("drop", [P, HEADS, G, NBLK])
                masked = sb("masked", [P, HEADS, G, NBLK])
                top, negm, nr = (sb(n, [P, HEADS, G]) for n in ("top", "negm", "nr"))
                qside = sb("qside", [P, G, HEADS, 8], BF16)
                qsideT = sb("qsideT", [SL, S], BF16)
                prob = [sb(f"prob{n}", [P, G, S]) for n in range(NP)]
                NS = HG * S // 32
                den = sb("den", [P, NS, 32])
                rden = sb("rden", [P, NS])
                rec, attnT = sb("rec", [P, HG, S]), sb("attnT", [P, HG, S])
                names = ("load", "filled", "xn_ready", "xT_in_psum", "xT_ready", "qk_in_psum", "v_in_psum", "turned_by_angle",
                         "rope_ready", "hi_ready", "rest_ready", "mid_ready", "slots_by_pool", "slots_by_dve",
                         "slots_by_act", "v_ready", "slotsT_in_psum", "slotsT_by_act", "slotsT_by_dve", "scores_in_psum",
                         "blocks_reduced", "qside_ready", "qsideT_in_psum", "qsideT_ready", "scoresT_in_psum",
                         "prob_ready", "pv_done", "attn_ready", "out_in_psum", "h_ready", "dve_step", "gone_on", "pool_goes_on")
                (load, filled, xn_ready, xT_psum, xT_ready, qk_psum, v_psum, rot, rope_ready, hi_ready, rest_ready, mid_ready,
                 slots_pool, slots_dve, slots_act, v_ready, sT_psum, sT_act, sT_dve, s_psum, reduced, qs_ready, qsT_psum,
                 qsT_ready, s2_psum, prob_ready, pv_done, attn_ready, out_psum, h_ready, own, gone_on, pool_on) = sem_in(
                     ctx, *("at_" + n for n in names))
                SA, SC = (ps(0), ps(1)), (ps(2), ps(3))
                MISC, VPS, OPS = ps(4), ps(5), bank[3]
                QK = SA
                SCB = [x.bitcast(BF16) for x in SC]
                SPOOL, SDVE, SACT = 2, 3, 2
                QSPS = OPS[:, 1, S:2 * S].bitcast(BF16)

                def last(j, ahead):
                    return min(j + ahead + 1, B) if isinstance(j, int) else j + ahead + 1

                def run(e, body, own_steps=None):
                    first, trips = 2, (B - 6) // 2
                    for i in range(-4, first):
                        body(i, i % 2, lambda ahead: 0 <= i + ahead < B)
                    with e.Fori(0, trips) as r:
                        if own_steps:
                            own_steps[0].enter(r, own_steps[1])
                        for p in range(2):
                            body(r * 2 + first + p, p, lambda ahead: True)
                        if own_steps:
                            own_steps[0].leave(trips)
                    for i in range(first + 2 * trips, B + 1):
                        body(i, i % 2, lambda ahead: 0 <= i + ahead < B)

                with nc.Block() as block:
                    @block.sync
                    def _(e):
                        for dst, src in ((wqkv, "wqkv"), (wo, "wo"), (rope, "c_rope"), (identb, "c_identb"),
                                         (causal, "c_causal"), (causalT, "c_causalT"), (keyside, "c_keyside"),
                                         (drop, "c_drop")):
                            e.dma_start(dst[:], a[src]).then_inc(load, 16)

                    three = lambda x, n: x.unsqueeze(2).to_broadcast([P, N, n, HD])

                    @block.gpsimd
                    def _(e):
                        for n in range(2):
                            e.memset(v1[n][:, :, :, 1, :], 1.0).then_inc(filled, 1)
                        e.memset(qside[:, :, :, :], 0.0).then_inc(filled, 1)

                        def fill_slots(j):
                            until(e, mid_ready, j + 1)
                            until(e, sT_psum, j * 6)
                            e.sem_inc(pool_on, 1)
                            for dst, src in ((slots[:, 0, :, 0:3, :], three(hi[:, 0], 3)),
                                             (slots[:, 0, :, 3:5, :], three(mid[:, 0], 2))):
                                e.tensor_copy(dst, src).then_inc(slots_pool, 1)

                        def add_rotated(j):
                            until(e, rot, (j + 1) * 3 * G)
                            until(e, rest_ready, j)
                            until(e, hi_ready, j)
                            e.tensor_tensor(xr[:], tcos[:], tsin[:], ALU.add).then_inc(rope_ready, 1)

                        def body(i, p, there):
                            if there(2):
                                fill_slots(i + 2)
                            if there(3):
                                add_rotated(i + 3)

                        run(e, body)

                    @block.tensor
                    def _(e):
                        def turn_x(j):
                            until(e, xn_ready, (j + 1) * G)
                            until(e, h_ready, j - 4)
                            turn(e, MISC, xn).then_inc(xT_psum, 1)

                        def project_qk(j):
                            until(e, xT_ready, j + 1)
                            until(e, prob_ready, (j - 2) * HEADS)
                            until(e, rot, j * 3 * G)
                            for g in range(G):
                                for c in range(C):
                                    m = e.matmul(QK[g][:, 0:2 * D], xT[:, c, g * P:(g + 1) * P],
                                                 wqkv[:, c, 0:2 * D], start=(c == 0), stop=(c == C - 1))
                            m.then_inc(qk_psum, 1)

                        def project_v(j):
                            until(e, xT_ready, j + 1)
                            until(e, v_ready, j)
                            for g in range(G):
                                for c in range(C):
                                    m = e.matmul(VPS[:, g * D:(g + 1) * D], xT[:, c, g * P:(g + 1) * P],
                                                 wqkv[:, c, 2 * D:3 * D], start=(c == 0), stop=(c == C - 1))
                            m.then_inc(v_psum, 1)

                        def turn_slots(j, part):
                            if part == 0:
                                until(e, slots_pool, (j + 1) * SPOOL)
                                until(e, slots_dve, (j + 1) * SDVE)
                                until(e, slots_act, (j + 1) * SACT)
                                until(e, reduced, j * HEADS * 2)
                            for n in (2 * part, 2 * part + 1):
                                if n >= 2:
                                    until(e, (sT_act, sT_dve)[n % 2], j * 3 + n // 2)
                                for k in range(8):
                                    hd, g = 4 * (n % 3) + k // 2, k % 2
                                    m = e.transpose(SCB[n % 2][0:SL, k * P:(k + 1) * P],
                                                    slots[:, n // 3, g * HEADS + hd].rearrange("p s d -> p (s d)"),
                                                    identb[:, :])
                                m.then_inc(sT_psum, 1)

                        def score(j, p, hd):
                            if hd == 0:
                                until(e, sT_act, (j + 1) * 3)
                                until(e, sT_dve, (j + 1) * 3)
                            if hd >= 2:
                                until(e, reduced, (j * HEADS + hd - 1) * 2)
                            for g in range(G):
                                o = SC[hd % 2][:, g * S:(g + 1) * S]
                                e.matmul(o, qkT[p][:, 0, hd, g * P:(g + 1) * P], qkT[p][:, 1, hd, :],
                                         start=True, stop=False)
                                m = e.matmul(o[:, g * P:(g + 1) * P], identb[:, :], causal[:, :],
                                             start=False, stop=True)
                            m.then_inc(s_psum, 1)

                        def turn_qside(j):
                            until(e, qs_ready, (j + 1) * 4)
                            until(e, qsT_ready, j)
                            for g in range(G):
                                m = e.transpose(QSPS[0:SL, g * P:(g + 1) * P],
                                                qside[:, g].rearrange("p h s -> p (h s)"), identb[:, :])
                            m.then_inc(qsT_psum, 1)

                        def scoreT(j, p, hd):
                            if hd == 0:
                                until(e, qsT_ready, j + 1)
                            if hd < 2:
                                until(e, rot, last(j, 2) * 3 * G)
                            else:
                                until(e, prob_ready, j * HEADS + hd - 1)
                            for g in range(G):
                                o = SA[hd % 2][:, g * S:(g + 1) * S]
                                e.matmul(o, qkT[p][:, 1, hd, g * P:(g + 1) * P], qkT[p][:, 0, hd, :],
                                         start=True, stop=False)
                                e.matmul(o, keyside[:, hd, g, :], qsideT[:, :], start=False, stop=False)
                                m = e.matmul(o[:, g * P:(g + 1) * P], identb[:, :], causalT[:, :],
                                             start=False, stop=True)
                            m.then_inc(s2_psum, 1)

                        def values(j, p, n):
                            until(e, prob_ready, j * HEADS + 4 * (n + 1))
                            if n == 0:
                                until(e, v_ready, j + 1)
                                until(e, attn_ready, j * 2)
                            for g in range(G):
                                for q in range(4):
                                    hd = 4 * n + q
                                    m = e.matmul(OPS[q * 32:q * 32 + 32, n // 2, n % 2 * S:(n % 2 + 1) * S],
                                                 v1[p][:, g, hd].rearrange("p two d -> p (two d)"),
                                                 prob[hd % NP][:, g, :], start=(g == 0), stop=(g == G - 1))
                            m.then_inc(pv_done, 1)

                        def project_out(j):
                            until(e, attn_ready, (j + 1) * 2)
                            until(e, xT_ready, last(j, 4))
                            for g in range(G):
                                for n in range(HG):
                                    m = e.matmul(MISC[:, g * D:(g + 1) * D], attnT[:, n, g * P:(g + 1) * P],
                                                 wo[:, n, :], start=(n == 0), stop=(n == HG - 1))
                            m.then_inc(out_psum, 1)

                        def body(i, p, there):
                            for hd in range(HEADS):
                                if there(0):
                                    scoreT(i, p, hd)
                                if there(1):
                                    score(i + 1, 1 - p, hd)
                                if there(0) and hd in (5, 9):
                                    values(i, p, hd // 4 - 1)
                                if there(-1) and hd == 6:
                                    project_out(i - 1)
                            if there(0):
                                values(i, p, HG - 1)
                            if there(2):
                                turn_slots(i + 2, 0)
                            if there(3):
                                project_qk(i + 3)
                            if there(2):
                                turn_slots(i + 2, 1)
                            if there(1):
                                turn_qside(i + 1)
                            if there(3):
                                project_v(i + 3)
                            if there(2):
                                turn_slots(i + 2, 2)
                            if there(4):
                                turn_x(i + 4)

                        e.wait_ge(load, 128)
                        e.wait_ge(filled, 3)
                        run(e, body)

                    @block.scalar
                    def _(e):
                        root(e, ln)

                        def xT_out(j):
                            until(e, xT_psum, j + 1)
                            until(e, v_psum, j)
                            e.activation(xT[:, :, :], MISC[0:K, :].rearrange("p (c t) -> p c t", c=C),
                                         ACT.Identity).then_inc(xT_ready, 1)

                        def his(j):
                            until(e, rope_ready, j + 1)
                            until(e, slots_pool, j * SPOOL)
                            until(e, slots_dve, j * SDVE)
                            until(e, slots_act, j * SACT)
                            until(e, rest_ready, j)
                            e.activation(hi[:].rearrange("p a n d -> p (a n d)"),
                                         xr[:].rearrange("p a g h d -> p (a g h d)"), ACT.Identity).then_inc(hi_ready, 1)

                        def mids(j):
                            until(e, rest_ready, j + 1)
                            until(e, slots_pool, j * SPOOL)
                            until(e, slots_dve, j * SDVE)
                            until(e, slots_act, j * SACT)
                            e.activation(mid[:].rearrange("p a n d -> p (a n d)"),
                                         r1[:].rearrange("p a g h d -> p (a g h d)"), ACT.Identity).then_inc(mid_ready, 1)

                        def fill_slots(j):
                            until(e, mid_ready, j + 1)
                            until(e, sT_psum, j * 6)
                            e.activation(slots[:, 1, :, 1:5:3, :], three(mid[:, 1], 2), ACT.Identity
                                         ).then_inc(slots_act, 1)
                            e.activation(slots[:, 1, :, 5, :], hi[:, 1], ACT.Identity).then_inc(slots_act, 1)

                        def v_out(j, p):
                            until(e, v_psum, j + 1)
                            until(e, pv_done, (j - 1) * HG)
                            e.activation(v1[p][:, :, :, 0, :].rearrange("p g h d -> p (g h) d"),
                                         VPS[:, 0:G * D].rearrange("p (n d) -> p n d", d=HD),
                                         ACT.Identity).then_inc(v_ready, 1)

                        def slotsT_out(j, p, n):
                            until(e, sT_psum, j * 6 + n + 1)
                            if n == 0:
                                until(e, s2_psum, (j - 1) * HEADS)
                            e.activation(qkT[p][:, n // 3, 4 * (n % 3):4 * (n % 3) + 4, :],
                                         SCB[0][0:SL, :].rearrange("p (h t) -> p h t", h=4),
                                         ACT.Identity).then_inc(sT_act, 1)

                        def exponent(j, hd):
                            until(e, s2_psum, j * HEADS + hd + 1)
                            until(e, pv_done, j * HG + (hd - NP) // 4 + 1 if hd >= NP else
                                  (j - 1) * HG + (hd + NP) // 4 + 1)
                            e.activation(prob[hd % NP][:, :, :], SA[hd % 2].rearrange("p (g t) -> p g t", g=G),
                                         ACT.Exp).then_inc(prob_ready, 1)

                        def body(i, p, there):
                            if there(3):
                                xT_out(i + 3)
                            for hd in range(HEADS):
                                if there(0):
                                    exponent(i, hd)
                                if there(2) and hd == 4:
                                    mids(i + 2)
                                if there(2) and hd == 8:
                                    fill_slots(i + 2)
                            if there(2):
                                slotsT_out(i + 2, p, 0)
                                v_out(i + 2, p)
                                slotsT_out(i + 2, p, 2)
                                slotsT_out(i + 2, p, 4)
                            if there(3):
                                his(i + 3)

                        e.wait_ge(filled, 3)
                        run(e, body)

                    @block.vector
                    def _(e):
                        statistics(e, ln)
                        s = Own(e, own)

                        def norm(j):
                            until(e, xT_psum, j)
                            for g in range(G):
                                normalise(e, xn, j, g).then_inc(xn_ready, 1)

                        def rotate(j):
                            until(e, qk_psum, j + 1)
                            until(e, rope_ready, j)
                            for g in range(G):
                                x = QK[g][:, 0:2 * D].rearrange("p (a h d) -> p a h d", a=2, h=HEADS)
                                cos_, sin_ = (rope[:, g, :, n, :].unsqueeze(2).to_broadcast([P, 2, HEADS, HD])
                                              for n in range(2))
                                e.tensor_tensor(tcos[:, :, g], x, cos_, ALU.mult).then_inc(rot, 1)
                                e.tensor_tensor(tsin[:, :, g, :, 0:HD // 2], x[:, :, :, HD // 2:HD],
                                                sin_[:, :, :, 0:HD // 2], ALU.mult).then_inc(rot, 1)
                                e.tensor_tensor(tsin[:, :, g, :, HD // 2:HD], x[:, :, :, 0:HD // 2],
                                                sin_[:, :, :, HD // 2:HD], ALU.mult).then_inc(rot, 1)

                        def rest(j):
                            until(e, hi_ready, j + 1)
                            until(e, mid_ready, j)
                            until(e, slots_dve, j * SDVE)
                            e.tensor_tensor(r1[:].rearrange("p a g h d -> p (a g h d)"),
                                            xr[:].rearrange("p a g h d -> p (a g h d)"),
                                            hi[:].rearrange("p a n d -> p (a n d)"), ALU.subtract
                                            ).then_inc(rest_ready, 1)

                        def fill_slots(j):
                            until(e, mid_ready, j + 1)
                            until(e, sT_psum, j * 6)
                            e.tensor_copy(slots[:, 1, :, 0:4:3, :], three(hi[:, 1], 2)).then_inc(slots_dve, 1)
                            for n, at in ((0, 5), (1, 2)):
                                e.tensor_tensor(slots[:, n, :, at, :], r1[:, n].rearrange("p g h d -> p (g h) d"),
                                                mid[:, n], ALU.subtract).then_inc(slots_dve, 1)

                        def slotsT_out(j, p, n):
                            until(e, sT_psum, j * 6 + n + 1)
                            if n == 1:
                                until(e, s2_psum, (j - 1) * HEADS)
                            e.tensor_copy(qkT[p][:, n // 3, 4 * (n % 3):4 * (n % 3) + 4, :],
                                          SCB[1][0:SL, :].rearrange("p (h t) -> p h t", h=4)).then_inc(sT_dve, 1)

                        def reduce_blocks(j, hd):
                            until(e, s_psum, j * HEADS + hd + 1)
                            x = SC[hd % 2].rearrange("p (n k) -> p n k", k=BLK)
                            e.tensor_reduce(bmax[:, hd].rearrange("p g n -> p (g n)"), x, AX.X, ALU.max
                                            ).then_inc(reduced, 1)
                            e.tensor_reduce(bsum[BLK:P, hd], x[BLK:P, NBLK:NBLK + 3, :], AX.X, ALU.add
                                            ).then_inc(reduced, 1)

                        def query_side(j):
                            until(e, reduced, (j + 1) * HEADS * 2)
                            hb = lambda x: x[BLK:P]
                            s.chain(e.tensor_reduce(hb(least), hb(bsum), AX.X, ALU.min))
                            s.chain(e.tensor_tensor(hb(same), hb(bsum), hb(least).unsqueeze(2).to_broadcast(
                                [BLK, HEADS, 3]), ALU.is_equal))
                            s.step(e.tensor_scalar(drop[BLK:P, :, 1, 2], same[BLK:P, :, 2], NEG, None, ALU.mult))
                            s.chain(e.tensor_scalar(hb(other), same[BLK:P, :, 2], -1.0, 1.0, ALU.mult, ALU.add))
                            s.chain(e.tensor_tensor(hb(least), hb(other), same[BLK:P, :, 1], ALU.mult))
                            s.step(e.tensor_scalar(drop[BLK:P, :, 1, 1], hb(least), NEG, None, ALU.mult))
                            s.chain(e.tensor_tensor(hb(other), hb(other), hb(least), ALU.subtract))
                            s.chain(e.tensor_scalar(drop[BLK:P, :, 1, 0], hb(other), NEG, None, ALU.mult))
                            s.chain(e.tensor_tensor(masked[:], bmax[:], drop[:], ALU.add))
                            s.chain(e.tensor_reduce(top[:], masked[:], AX.X, ALU.max))
                            s.chain(e.tensor_scalar(negm[:], top[:], -1.0, None, ALU.mult))
                            until(e, qsT_psum, j)
                            part = lambda n: qside[:, :, :, n].rearrange("p g h -> p h g")
                            e.tensor_copy(qside[:, :, :, 0:NBLK].rearrange("p g h n -> p h g n"), drop[:]
                                          ).then_inc(qs_ready, 1)
                            e.tensor_copy(part(4), negm[:]).then_inc(qs_ready, 1)
                            until(e, qs_ready, j * 4 + 2)
                            s.chain(e.tensor_tensor(nr[:], negm[:], part(4), ALU.subtract))
                            e.tensor_copy(part(5), nr[:]).then_inc(qs_ready, 1)
                            until(e, qs_ready, j * 4 + 3)
                            e.tensor_tensor(part(6), nr[:], part(5), ALU.subtract).then_inc(qs_ready, 1)

                        def qsideT_out(j):
                            until(e, qsT_psum, j + 1)
                            until(e, s2_psum, j * HEADS)
                            e.tensor_copy(qsideT[:, :], QSPS[0:SL, 0:S]).then_inc(qsT_ready, 1)

                        def turn_denominators(j):
                            until(e, pv_done, (j + 1) * HG)
                            e.sem_inc(gone_on, 1)
                            half = 2 * S // 32
                            s.step(e.transpose(den[:, 0:half, :].rearrange("p n r -> p (n r)"), OPS[:, 0, :]))
                            s.step(e.transpose(den[:, half:NS, :].rearrange("p n r -> p (n r)"), OPS[:, 1, 0:S]))

                        def invert(j):
                            until(e, attn_ready, j * 2)
                            s.wait()
                            s.chain(e.reciprocal(rden[:, :], den[:, :, HD]))
                            e.sem_inc(gone_on, 1)
                            s.step(e.transpose(rec[:].rearrange("p n t -> p (n t)"),
                                               rden[:, :].unsqueeze(2).to_broadcast([P, NS, 32])))

                        def divide(j):
                            until(e, out_psum, j)
                            s.wait()
                            e.tensor_tensor(attnT[:, 0:2, :], OPS[:, 0, :].rearrange("p (n t) -> p n t", n=2),
                                            rec[:, 0:2, :], ALU.mult).then_inc(attn_ready, 1)
                            e.tensor_tensor(attnT[:, 2, :], OPS[:, 1, 0:S], rec[:, 2, :], ALU.mult
                                            ).then_inc(attn_ready, 1)

                        def add_h(j):
                            until(e, out_psum, j + 1)
                            hh = h[:, bass.ds(j * G, G), :]
                            e.tensor_tensor(hh, MISC[:, 0:G * D].rearrange("p (g d) -> p g d", g=G), hh,
                                            ALU.add).then_inc(h_ready, 1)
                            until(e, h_ready, j + 1)
                            for g in range(G):
                                row_stats(e, j * G + g)

                        def body(i, p, there):
                            for hd in range(HEADS):
                                if there(1):
                                    reduce_blocks(i + 1, hd)
                                if there(-1) and hd == 2:
                                    divide(i - 1)
                                if there(-1) and hd == 9:
                                    add_h(i - 1)
                                if there(2) and hd == 1:
                                    rest(i + 2)
                                if there(4) and hd == 6:
                                    norm(i + 4)
                                if there(2) and hd == 6:
                                    fill_slots(i + 2)
                            if there(1):
                                query_side(i + 1)
                            if there(2):
                                slotsT_out(i + 2, p, 1)
                            if there(3):
                                rotate(i + 3)
                            if there(2):
                                slotsT_out(i + 2, p, 3)
                            if there(1):
                                qsideT_out(i + 1)
                            if there(0):
                                turn_denominators(i)
                            if there(2):
                                slotsT_out(i + 2, p, 5)
                            if there(0):
                                invert(i)

                        e.wait_ge(load, 128)
                        e.wait_ge(filled, 3)
                        run(e, body, (s, 2 * 16))

        def route(name, layer, logits, at, weight, eid, bias, rt, x_stored):
            with ExitStack() as ctx:
                sb = lambda n, *x: sb_in(ctx, name + n, *x)
                score, sel, eq, top1, top2, both, tmp = (
                    sb(n, [P, T, E]) for n in ("score", "sel", "eq", "top1", "top2", "both", "tmp"))
                best, total, rtotal = (sb(n, [P, T]) for n in ("best", "total", "rtotal"))
                upper, ones = sb("upper", [P, P]), sb("ones", [P, P])
                percnt, upto_, before, overs = (sb(n, [P, E, T]) for n in ("percnt", "upto", "before", "overs"))
                ntile, end, base = (sb(n, [P, E]) for n in ("ntile", "end", "base"))
                passed, eidf = sb("passed", [P, XT, E]), sb("eidf", [P, XT])
                load, own, sm_in, sm_out, chosen, counted, filled = sem_in(
                    ctx, *(name + n for n in ("_rt_load", "_rt_step", "_rt_act_in", "_rt_act_out", "_rt_chosen",
                                              "_rt_counted", "_rt_filled")))
                rev, first, tiles, keep = (rt[:, x] for x in (RT_REV, RT_FIRST, RT_TILES, RT_KEEP))
                over = lambda ap: ap.unsqueeze(2).to_broadcast([P, T, E])
                with nc.Block() as block:
                    @block.sync
                    def _(e):
                        e.dma_start(upper[:, :], a["c_upper"]).then_inc(load, 16)
                        e.wait_ge(x_stored, B // 2 * 16)

                    @block.gpsimd
                    def _(e):
                        e.memset(ones[:, :], 1.0).then_inc(filled, 1)

                    @block.scalar
                    def _(e):
                        if layer == 0:
                            e.activation(score[:, :, :], logits[:, :, :], ACT.Sigmoid).then_inc(sm_out, 1)
                        else:
                            e.wait_ge(sm_in, 1)
                            e.activation(sel[:, :, :], tmp[:, :, :], ACT.Exp).then_inc(sm_out, 1)

                    @block.tensor
                    def _(e):
                        e.wait_ge(load, 16)
                        e.wait_ge(filled, 1)
                        e.wait_ge(chosen, 1)
                        flat = both[:, :, :].rearrange("p t e -> p (t e)")
                        e.matmul(ps(0)[:, 0:T * E], upper[:, :], flat, start=True, stop=True)
                        e.matmul(ps(1)[:, 0:T * E], ones[:, :], flat, start=True, stop=True).then_inc(counted, 1)

                    @block.vector
                    def _(e):
                        s = Own(e, own)
                        if layer == 0:
                            e.wait_ge(sm_out, 1)
                            s.chain(e.tensor_tensor(sel[:, :, :], score[:, :, :],
                                                    bias[:, :].unsqueeze(1).to_broadcast([P, T, E]), ALU.add))
                        else:
                            s.chain(e.tensor_reduce(best[:, :], logits[:, :, :], AX.X, ALU.max))
                            e.tensor_tensor(tmp[:, :, :], logits[:, :, :], over(best[:, :]), ALU.subtract
                                            ).then_inc(sm_in, 1)
                            e.wait_ge(sm_out, 1)
                            s.chain(e.tensor_reduce(total[:, :], sel[:, :, :], AX.X, ALU.add))
                            s.chain(e.reciprocal(rtotal[:, :], total[:, :]))
                            s.chain(e.tensor_tensor(score[:, :, :], sel[:, :, :], over(rtotal[:, :]), ALU.mult))
                            s.chain(e.tensor_copy(sel[:, :, :], score[:, :, :]))
                        for n, top in enumerate((top1, top2)):
                            s.chain(e.tensor_reduce(best[:, :], sel[:, :, :], AX.X, ALU.max))
                            s.chain(e.tensor_tensor(eq[:, :, :], sel[:, :, :], over(best[:, :]), ALU.is_equal))
                            s.chain(e.tensor_tensor(eq[:, :, :], eq[:, :, :],
                                                    rev.unsqueeze(1).to_broadcast([P, T, E]), ALU.mult))
                            s.chain(e.tensor_reduce(best[:, :], eq[:, :, :], AX.X, ALU.max))
                            s.chain(e.tensor_tensor(top[:, :, :], eq[:, :, :], over(best[:, :]), ALU.is_equal))
                            if n == 0:
                                s.chain(e.scalar_tensor_tensor(sel[:, :, :], top[:, :, :], NEG, sel[:, :, :],
                                                               ALU.mult, ALU.add))
                        s.step(e.tensor_tensor(tmp[:, :, :], top1[:, :, :], score[:, :, :], ALU.mult))
                        s.chain(e.tensor_tensor(eq[:, :, :], top2[:, :, :], score[:, :, :], ALU.mult))
                        e.tensor_tensor(both[:, :, :], top1[:, :, :], top2[:, :, :], ALU.add).then_inc(chosen, 1)
                        s.step(e.tensor_reduce(weight[:, :, 0], tmp[:, :, :], AX.X, ALU.add))
                        s.chain(e.tensor_reduce(weight[:, :, 1], eq[:, :, :], AX.X, ALU.add))
                        s.chain(e.tensor_tensor(total[:, :], weight[:, :, 0], weight[:, :, 1], ALU.add))
                        if layer == 0:
                            s.chain(e.tensor_scalar(total[:, :], total[:, :], 1e-20, None, ALU.add))
                        s.chain(e.reciprocal(rtotal[:, :], total[:, :]))
                        s.step(e.tensor_tensor(weight[:, :, 0], weight[:, :, 0], rtotal[:, :], ALU.mult))
                        s.step(e.tensor_tensor(weight[:, :, 1], weight[:, :, 1], rtotal[:, :], ALU.mult))
                        e.wait_ge(counted, 1)
                        s.chain(e.tensor_copy(percnt[:, :, :], ps(1)[:, 0:T * E].rearrange("p (t e) -> p e t", e=E)))
                        flat = lambda x: x[:, :, :].rearrange("p e t -> p (e t)")
                        s.chain(e.tensor_tensor_scan(flat(upto_), keep, flat(percnt), 0.0, ALU.mult, ALU.add))
                        s.step(e.tensor_tensor(before[:, :, :], upto_[:, :, :], percnt[:, :, :], ALU.subtract))
                        s.chain(e.tensor_tensor(overs[:, :, :], first.unsqueeze(1).to_broadcast([P, E, T]),
                                                upto_[:, :, T - 1:T].to_broadcast([P, E, T]), ALU.is_lt))
                        s.chain(e.tensor_reduce(ntile[:, :], overs[:, :, :], AX.X, ALU.add))
                        s.chain(e.tensor_tensor_scan(end[:, :], keep[:, 1:1 + E], ntile[:, :], 0.0, ALU.mult, ALU.add))
                        s.chain(e.tensor_tensor(base[:, :], end[:, :], ntile[:, :], ALU.subtract))
                        s.chain(e.tensor_scalar(base[:, :], base[:, :], float(P), None, ALU.mult))
                        s.chain(e.tensor_tensor(before[:, :, :], before[:, :, :],
                                                base[:, :].unsqueeze(2).to_broadcast([P, E, T]), ALU.add))
                        s.chain(e.tensor_tensor(tmp[:, :, :], ps(0)[:, 0:T * E].rearrange("p (t e) -> p t e", e=E),
                                                before[:, :, :].rearrange("p e t -> p t e"), ALU.add))
                        for n, top in enumerate((top1, top2)):
                            s.chain(e.tensor_tensor(eq[:, :, :], tmp[:, :, :], top[:, :, :], ALU.mult))
                            s.chain(e.tensor_reduce(at[:, :, n], eq[:, :, :], AX.X, ALU.add))
                        s.chain(e.tensor_tensor(passed[:, :, :], end[:, :].unsqueeze(1).to_broadcast([P, XT, E]),
                                                tiles.unsqueeze(2).to_broadcast([P, XT, E]), ALU.is_le))
                        s.chain(e.tensor_reduce(eidf[:, :], passed[:, :, :], AX.X, ALU.add))
                        s.chain(e.tensor_scalar(eid[:, :], eidf[:, :], float(E - 1), None, ALU.min))

        def invert_slots(name, at, ends, rt):
            N, CH = 2 * T, 16
            with ExitStack() as ctx:
                sb = lambda n, *x: sb_in(ctx, f"{name}_{n}", *x)
                ati, low = sb("ati", [P, N], I32), sb("low", [P, N], I32)
                row, tile = sb("row", [P, N]), sb("tile", [P, N])
                rows = [sb(f"rows{n}", [P, CH, P], BF16) for n in range(2)]
                hot = [sb(f"hot{n}", [P, CH, XT], BF16) for n in range(2)]
                carried = [sb(f"carried{n}", [P, CH, 2, XT], BF16) for n in range(2)]
                place, dest, full, src, beyond = (sb(n, [P, XT]) for n in ("place", "dest", "full", "src", "beyond"))
                hot_ready, numbered, chunk_ready, used, own = sem_in(
                    ctx, *(f"{name}_{n}" for n in ("tiles_ready", "numbered", "chunk_ready", "chunk_used", "step")))
                tiles, r128, number, no_token, part = (
                    rt[:, x] for x in (RT_TILES, RT_ROW, RT_NUMBER, RT_NO_TOKEN, RT_PART))
                with nc.Block() as block:
                    def cut(x, c, width):
                        return x[:, c * CH:(c + 1) * CH].unsqueeze(2).to_broadcast([P, CH, width])

                    @block.vector
                    def _(e):
                        s = Own(e, own)
                        s.chain(e.tensor_copy(ati[:, :], at[:, :, :].rearrange("p t n -> p (t n)")))
                        s.chain(e.tensor_scalar(low[:, :], ati[:, :], 7, None, ALU.arith_shift_right))
                        s.step(e.tensor_copy(tile[:, :], low[:, :]))
                        s.chain(e.tensor_scalar(ati[:, :], ati[:, :], P - 1, None, ALU.bitwise_and))
                        s.chain(e.tensor_copy(row[:, :], ati[:, :]))
                        for c in range(N // CH):
                            b = c % 2
                            if c >= 2:
                                e.wait_ge(used, c - 1)
                                e.wait_ge(numbered, c - 1)
                            e.tensor_tensor(hot[b][:], tiles.unsqueeze(1).to_broadcast([P, CH, XT]),
                                            cut(tile, c, XT), ALU.is_equal).then_inc(hot_ready, 1)
                            e.tensor_tensor(rows[b][:], r128.unsqueeze(1).to_broadcast([P, CH, P]), cut(row, c, P),
                                            ALU.is_equal).then_inc(chunk_ready, 1)
                            e.wait_ge(hot_ready, c + 1)
                            e.tensor_scalar(carried[b][:, :, 1, :], hot[b][:], part, None, ALU.mult
                                            ).then_inc(chunk_ready, 1)
                        e.wait_ge(used, N // CH)
                        number_at, place_at = ps(0)[:, 0:XT], ps(0)[:, XT:2 * XT]
                        s.step(e.tensor_scalar(dest[:, :], number_at, -1.0, float(P), ALU.add, ALU.mult))
                        s.step(e.tensor_scalar(full[:, :], number_at, 0.0, None, ALU.is_equal))
                        s.chain(e.tensor_copy(place[:, :], place_at))
                        s.step(e.tensor_tensor(full[:, :], full[:, :], no_token, ALU.mult))
                        s.chain(e.tensor_tensor(dest[:, :], dest[:, :], place[:, :], ALU.add))
                        s.step(e.tensor_scalar(beyond[:, :], dest[:, :], float(T * P), float(-T * P), ALU.is_ge, ALU.mult))
                        s.chain(e.tensor_scalar(src[:, :], dest[:, :], 0.0, None, ALU.max))
                        s.step(e.tensor_tensor(ends[:, :, 0], src[:, :], beyond[:, :], ALU.add))
                        s.step(e.tensor_tensor(ends[:, :, 1], dest[:, :], full[:, :], ALU.add))

                    @block.gpsimd
                    def _(e):
                        for c in range(N // CH):
                            e.wait_ge(hot_ready, c + 1)
                            if c >= 2:
                                e.wait_ge(used, c - 1)
                            e.tensor_tensor(carried[c % 2][:, :, 0, :], hot[c % 2][:], cut(number, c, XT), ALU.mult
                                            ).then_inc(numbered, 1)

                    @block.tensor
                    def _(e):
                        for c in range(N // CH):
                            e.wait_ge(chunk_ready, (c + 1) * 2)
                            e.wait_ge(numbered, c + 1)
                            for n in range(CH):
                                m = e.matmul(ps(0)[:, 0:2 * XT], rows[c % 2][:, n, :],
                                             carried[c % 2][:, n].rearrange("p two s -> p (two s)"),
                                             start=(c == 0 and n == 0), stop=(c == N // CH - 1 and n == CH - 1))
                            m.then_inc(used, 1)

        def combine(name, layer, weight):
            U, Q = 3, 4
            with ExitStack() as ctx:
                got = [sb_in(ctx, f"{name}_got{u}", [P, 2, Q, D]) for u in range(U)]
                half, taken = sem_in(ctx, name + "_half", name + "_taken")
                here = [sem_in(ctx, f"{name}_here{u}") for u in range(U)]
                last = layer == 1
                rows = y_rows[layer][0:2 * T * P].rearrange("(n t p) d -> p n t d", n=2, p=P)
                with nc.Block() as block:
                    @block.sync
                    def _(e):
                        for q in range(T // Q):
                            if q >= U:
                                e.wait_ge(taken, (q - U + 1) * Q)
                            for n in range(2):
                                e.dma_start(got[q % U][:, n], rows[:, n, q * Q:(q + 1) * Q]).then_inc(here[q % U], 16)

                    if last:
                        @block.scalar
                        def _(e):
                            rows_out = out.rearrange("b (g p) d -> p (b g) d", p=P)
                            with e.Fori(0, T // Q) as i:
                                e.wait_ge(taken, i * Q + Q)
                                e.dma_start(rows_out[:, bass.ds(i * Q, Q), :], h[:, bass.ds(i * Q, Q), :]
                                            ).then_inc(stored, 16)
                            e.wait_ge(stored, 16 * (T // Q))

                    @block.vector
                    def _(e):
                        def add(t, n, done):
                            q, k = t // Q, t % Q
                            return e.scalar_tensor_tensor(h[:, t, :], got[q % U][:, n, k], weight[:, t, n:n + 1],
                                                          h[:, t, :], ALU.mult, ALU.add).then_inc(done, 1)

                        for t in range(T + 2):
                            if t < T:
                                if t % Q == 0:
                                    e.wait_ge(here[t // Q % U], (t // Q // U + 1) * 32)
                                add(t, 0, half)
                            if 1 <= t <= T:
                                e.wait_ge(half, t)
                                add(t - 1, 1, taken)
                            if t >= 2 and not last:
                                e.wait_ge(taken, t - 1)
                                row_stats(e, t - 2)

        def experts(name, layer, eid, ends, w1, w2, bias2):
            U, AHEAD = 8, 5
            H = D if layer == 0 else HID
            HC = H // (K if layer == 0 else P)
            HK = H // HC
            with ExitStack() as ctx:
                xg = [sb_in(ctx, f"{name}_xg{u}", [P, D]) for u in range(U)]
                yo = [sb_in(ctx, f"{name}_yo{u}", [P, D]) for u in range(U)]
                xT = sb_in(ctx, name + "_xT", [K + 1, C, P])
                pos_part = [sb_in(ctx, f"{name}_relu{n}", [P, D]) for n in range(2)]
                hid = [sb_in(ctx, f"{name}_hid{n}", [P, H]) for n in range(2)]
                hidT = sb_in(ctx, name + "_hidT", [HK, HC, P])
                loaded = [sem_in(top, f"{name}_loaded{u}") for u in range(U)]
                put = [sem_in(top, f"{name}_put{u}") for u in range(U)]
                source = [sb_in(ctx, f"{name}_source{u}", [P, 1], I32) for u in range(U)]
                goal = [sb_in(ctx, f"{name}_goal{u}", [P, 1], I32) for u in range(U)]
                source_ready, goal_ready, gone_on = sem_in(ctx, name + "_source_ready", name + "_goal_ready",
                                                           name + "_gone_on")
                (xT_psum, xT_ready, hid_psum, relu_ready, hid_ready, hT_psum, hT_ready, y_psum, y_ready, ones) = sem_in(
                    ctx, *(name + n for n in ("_xT_in_psum", "_xT_ready", "_hidden_in_psum", "_relu_ready",
                                              "_hidden_ready", "_hiddenT_in_psum", "_hiddenT_ready", "_y_in_psum",
                                              "_y_ready", "_ones_row")))
                XPS, HPS, TPS, YPS = ps(0), bank[1], bank[2], ps(1)
                HN = H if layer == 0 else H // 2
                ROUNDS = (XT - 3) // U
                with nc.Block() as block:
                    @block.gpsimd
                    def _(e):
                        def fetch(s, u):
                            if not isinstance(s, int) or s >= U:
                                e.wait_ge(xT_psum, s - U + 1)
                            e.wait_ge(source_ready, s + 1)
                            e.sem_inc(gone_on, 1)
                            e.indirect_dma_start(xg[u][:, :], None, x_rows[layer], bass.IndirectOffsetOnAxis(
                                source[u][:, :].bitcast(U32), 0)).then_inc(loaded[u], 16)

                        def store(s, u):
                            e.wait_ge(y_ready, s + 1)
                            e.wait_ge(goal_ready, s + 1)
                            e.sem_inc(gone_on, 1)
                            e.indirect_dma_start(y_rows[layer], bass.IndirectOffsetOnAxis(
                                goal[u][:, :].bitcast(U32), 0), yo[u][:, :], None).then_inc(put[u], 16)

                        e.memset(xT[K:K + 1, :, :], 1.0).then_inc(ones, 1)
                        for s in range(AHEAD):
                            fetch(s, s)
                        for s in range(U):
                            fetch(s + AHEAD, (s + AHEAD) % U)
                            store(s, s)
                        with e.Fori(1, XT // U - 1) as i:
                            for u in range(U):
                                fetch(i * U + u + AHEAD, (u + AHEAD) % U)
                                store(i * U + u, u)
                        for s in range(XT - U, XT):
                            if s + AHEAD < XT:
                                fetch(s + AHEAD, (s + AHEAD) % U)
                            store(s, s % U)
                        for u in range(U):
                            e.wait_ge(put[u], XT // U * 16)

                    @block.tensor
                    def _(e):
                        def turn_x(s, u, n):
                            e.wait_ge(loaded[u], n)
                            e.wait_ge(xT_ready, s)
                            for c in range(C):
                                m = e.transpose(XPS[0:K, c * P:(c + 1) * P], xg[u][:, c * K:(c + 1) * K], ident[:, :])
                            m.then_inc(xT_psum, 1)

                        def up(s, q, ex):
                            e.wait_ge(xT_ready, s + 1)
                            until(e, hid_ready, s if layer else s - 1)
                            for n in range(H // HN):
                                for c in range(C):
                                    kk = K + (c if layer else 0)
                                    m = e.matmul(HPS[:, n if layer else q, 0:HN], xT[0:kk, c, :],
                                                 w1[0:kk, ex, c, n * HN:(n + 1) * HN],
                                                 start=(c == 0), stop=(c == C - 1))
                            m.then_inc(hid_psum, 1)

                        def turn_hidden(s, q):
                            e.wait_ge(hid_ready, s + 1)
                            until(e, hT_ready, s)
                            for c in range(HC):
                                m = e.transpose(TPS[0:HK, c // 4, c % 4 * P:(c % 4 + 1) * P],
                                                hid[q][:, c * HK:(c + 1) * HK], ident[:, :])
                            m.then_inc(hT_psum, 1)

                        def down(s, ex):
                            e.wait_ge(hT_ready, s + 1)
                            e.wait_ge(y_ready, s)
                            for c in range(HC):
                                m = e.matmul(YPS[:, 0:D], hidT[:, c, :], w2[0:HK, ex, c, :],
                                             start=(c == 0), stop=(c == HC - 1))
                            m.then_inc(y_psum, 1)

                        def expert(s):
                            return e.value_load(eid[0:1, bass.ds(s, 1)], min_val=0, max_val=E - 1)

                        e.wait_ge(wload, wneed[layer])
                        e.wait_ge(ones, 1)
                        turn_x(0, 0, 16)

                        def body(s, j, r, ex):
                            there = lambda n: not isinstance(s, int) or 0 <= s + n < XT
                            if there(0):
                                ex.append(expert(s))
                                up(s, j % 2, ex[-1])
                            if there(1):
                                turn_x(s + 1, (j + 1) % U, (r + 1) * 16)
                            if there(-2):
                                down(s - 2, ex.pop(0))
                            if there(-1):
                                turn_hidden(s - 1, (j + 1) % 2)

                        ex = []
                        for s in range(2):
                            body(s, s, 0, ex)
                        with e.Fori(0, ROUNDS) as i:
                            ex = [expert(i * U), expert(i * U + 1)]
                            for j in range(2, U + 2):
                                body(i * U + j, j % U, i + (j + 1) // U, ex)
                        ex = [expert(ROUNDS * U), expert(ROUNDS * U + 1)]
                        for s in range(2 + ROUNDS * U, XT + 2):
                            body(s, s % U, (s + 1) // U, ex)

                    @block.scalar
                    def _(e):
                        def xT_out(s):
                            e.wait_ge(xT_psum, s + 1)
                            e.wait_ge(hid_psum, s)
                            e.activation(xT[0:K, :, :], XPS[0:K, 0:C * P].rearrange("p (c t) -> p c t", c=C),
                                         ACT.Copy).then_inc(xT_ready, 1)

                        def hid_out(s, q):
                            e.wait_ge(hid_psum, s + 1)
                            if layer == 0:
                                until(e, hid_ready, s - 1)
                                e.activation(pos_part[q][:, :], HPS[:, q, 0:D], ACT.Relu).then_inc(relu_ready, 1)
                            else:
                                until(e, hT_psum, s - 1)
                                e.activation(hid[q][:, :].rearrange("p (n f) -> p n f", n=2), HPS[:, :, 0:HN],
                                             ACT.Gelu_apprx_tanh).then_inc(hid_ready, 1)

                        def index(of, n, s, u, done, times, ready):
                            until(e, done[u], times * 16)
                            e.activation(of[u][:, :], ends[:, s, n:n + 1], ACT.Identity).then_inc(ready, 1)

                        AT = AHEAD + 1
                        for s in range(AT):
                            index(source, 0, s, s, loaded, 0, source_ready)
                        if layer == 0:
                            xT_out(0)
                        def body(s, u, r):
                            hid_out(s, u % 2)
                            more = lambda n: not isinstance(s, int) or s + n < XT
                            if layer == 0 and more(1):
                                xT_out(s + 1)
                            if more(AT):
                                index(source, 0, s + AT, (u + AT) % U, loaded, r + (u + AT) // U, source_ready)
                            index(goal, 1, s, u, put, r, goal_ready)

                        for s in range(U):
                            body(s, s, 0)
                        with e.Fori(1, XT // U - 1) as i:
                            for u in range(U):
                                body(i * U + u, u, i)
                        for s in range(XT - U, XT):
                            body(s, s % U, s // U)

                    @block.vector
                    def _(e):
                        def xT_out(s):
                            e.wait_ge(xT_psum, s + 1)
                            e.wait_ge(hid_psum, s)
                            e.tensor_copy(xT[0:K, :, :], XPS[0:K, 0:C * P].rearrange("p (c t) -> p c t", c=C)
                                          ).then_inc(xT_ready, 1)

                        def squares(s, q):
                            e.wait_ge(relu_ready, s + 1)
                            until(e, hT_psum, s - 1)
                            e.tensor_tensor(hid[q][:, :], HPS[:, q, 0:D], pos_part[q][:, :], ALU.mult
                                            ).then_inc(hid_ready, 1)

                        def hT_out(s):
                            e.wait_ge(hT_psum, s + 1)
                            until(e, y_psum, s)
                            if layer == 0:
                                e.tensor_copy(hidT[:, :, :], TPS[0:HK, 0, 0:HC * P].rearrange("p (c t) -> p c t", c=HC)
                                              ).then_inc(hT_ready, 1)
                            else:
                                e.tensor_copy(hidT[:, 0:4, :], TPS[:, 0, :].rearrange("p (c t) -> p c t", c=4))
                                e.tensor_copy(hidT[:, 4:6, :], TPS[:, 1, 0:2 * P].rearrange("p (c t) -> p c t", c=2)
                                              ).then_inc(hT_ready, 1)

                        def y_out(s, u, n):
                            e.wait_ge(y_psum, s + 1)
                            until(e, put[u], n)
                            if layer == 0:
                                e.tensor_copy(yo[u][:, :], YPS[:, 0:D]).then_inc(y_ready, 1)
                            else:
                                ex = e.value_load(eid[0:1, bass.ds(s, 1)], min_val=0, max_val=E - 1)
                                e.tensor_tensor(yo[u][:, :], YPS[:, 0:D], bias2[:, ex, :], ALU.add).then_inc(y_ready, 1)

                        if layer:
                            e.wait_ge(wload, wneed[layer])
                            xT_out(0)

                        def body(s, j, stores):
                            if layer == 0 and (not isinstance(s, int) or s < XT):
                                squares(s, j % 2)
                            if not isinstance(s, int) or s >= 2:
                                y_out(s - 2, (j - 2) % U, stores)
                            if not isinstance(s, int) or 1 <= s <= XT:
                                hT_out(s - 1)
                            if layer and (not isinstance(s, int) or s + 1 < XT):
                                xT_out(s + 1)

                        for s in range(2):
                            body(s, s, 0)
                        with e.Fori(0, ROUNDS) as i:
                            for j in range(U):
                                body(i * U + 2 + j, (2 + j) % U, i * 16)
                        for s in range(2 + ROUNDS * U, XT + 2):
                            body(s, s % U, (s - 2) // U * 16)

        wneed = [16 * 2, 16 * 2 + 16 * 4]

        def moe(layer):
            name = f"moe{layer}"
            with ExitStack() as ctx:
                sb = lambda n, *x: sb_in(ctx, f"{name}_{n}", *x)
                weight = sb("weight", [P, T, 2])
                eid = sb("eid", [P, XT], I32)
                ends = sb("ends", [P, XT, 2], I32)
                w1 = sb("w1", [K + 1, E, C, D if layer == 0 else HID])
                w2 = sb("w2", [K, E, C, D] if layer == 0 else [P, E, HT, D])
                bias2 = sb("bias2", [P, E, D]) if layer else None
                x_stored = sem_in(ctx, name + "_x_rows_stored")
                with ExitStack() as c1:
                    rt = sb_in(c1, name + "_tables", [P, RT])
                    at = sb_in(c1, name + "_at", [P, T, 2])
                    with ExitStack() as c2:
                        xkeep = sb_in(c2, name + "_xkeep", [P, T, D])
                        logits = sb_in(c2, name + "_logits", [P, T, E])
                        bias = sb_in(c2, name + "_bias", [P, E])
                        moe_pre(name, layer, xkeep, logits, bias, rt, w1, w2, bias2, x_stored)
                        route(name, layer, logits, at, weight, eid, bias, rt, x_stored)
                    invert_slots(name + "_slots", at, ends, rt)
                experts(name + "_experts", layer, eid, ends, w1, w2, bias2)
                combine(name + "_combine", layer, weight)

        def moe_pre(name, layer, xkeep, logits, bias, rt, w1, w2, bias2, x_stored):
            with ExitStack() as ctx:
                sb = lambda n, *x: sb_in(ctx, f"{name}_{n}", *x)
                ln = ln_tensors(ctx, name)
                router = sb("router", [K + 1, C, E])
                xn = sb("xn", [P, G, D])
                xT = sb("xT", [K + 1, C, S])
                if layer == 0:
                    wfc, wproj = sb("wfc", [K, C, D]), sb("wproj", [K, C, D])
                    relu, hT = sb("relu", [K, C, S]), sb("hT", [K, C, S])
                (load, ones, xn_ready, xT_psum, xT_ready, kept, l_psum, l_ready, hid_psum, relu_ready, hT_ready, o_psum,
                 o_ready) = sem_in(ctx, *(f"{name}_{n}" for n in (
                     "pre_load", "pre_ones", "xn_ready", "xT_in_psum", "xT_ready", "xn_kept", "logits_in_psum",
                     "logits_ready", "shared_in_psum", "shared_relu", "shared_hT_ready", "shared_out_in_psum",
                     "shared_added")))
                TURNED, LPS, HPS, OPS = ps(0), ps(1), ps(2), ps(3)
                nload = 16 * (6 if layer == 0 else 4)
                with nc.Block() as block:
                    @block.sync
                    def _(e):
                        e.dma_start(router[0:K, :, :], a[f"router{layer}"]).then_inc(load, 16)
                        e.dma_start(rt[:, :], a["c_route"]).then_inc(load, 16)
                        if layer == 0:
                            e.dma_start(bias[:, :], a["balance"].partition_broadcast(P)).then_inc(load, 16)
                            e.dma_start(wfc[:, :, :], a["w_fc_sh"]).then_inc(load, 16)
                            e.dma_start(wproj[:, :, :], a["w_proj_sh"]).then_inc(load, 16)
                            e.dma_start(router[K:K + 1, :, :], a["no_bias"]).then_inc(load, 16)
                            e.dma_start(w1[0:K, :, :, :], a["w1_0"]).then_inc(wload, 16)
                            e.dma_start(w2[:, :, :, :], a["w2_0"]).then_inc(wload, 16)
                        else:
                            e.dma_start(router[K:K + 1, 0, :], a["br"]).then_inc(load, 16)
                            e.dma_start(router[K:K + 1, 1, :], a["br"]).then_inc(load, 16)
                            e.dma_start(w1[0:K, :, :, :], a["w1_1"]).then_inc(wload, 16)
                            e.dma_start(w1[K:K + 1, :, 1, :], a["bfc"]).then_inc(wload, 16)
                            e.dma_start(w2[:, :, :, :], a["w2_1"]).then_inc(wload, 16)
                            e.dma_start(bias2[:, :, :], a["bproj"].partition_broadcast(P)).then_inc(wload, 16)
                        rows = x_rows[layer].rearrange("(t p) d -> p t d", p=P)
                        with e.Fori(0, B // 2) as i:
                            e.wait_ge(kept, (i + 1) * 2)
                            e.dma_start(rows[:, bass.ds(i * 2 * G, 2 * G), :], xkeep[:, bass.ds(i * 2 * G, 2 * G), :]
                                        ).then_inc(x_stored, 16)

                    @block.gpsimd
                    def _(e):
                        e.memset(xT[K:K + 1, :, :], 1.0).then_inc(ones, 1)
                        e.wait_ge(ones, 1)
                        with e.Fori(0, B) as i:
                            e.wait_ge(xn_ready, (i + 1) * G)
                            e.tensor_copy(xkeep[:, bass.ds(i * G, G), :], xn[:, :, :]).then_inc(kept, 1)
                            if layer == 0:
                                e.wait_ge(relu_ready, i + 1)
                                e.wait_ge(o_psum, i)
                                e.tensor_tensor(hT[:, :, :], relu[:, :, :], relu[:, :, :], ALU.mult
                                                ).then_inc(hT_ready, 1)

                    @block.tensor
                    def _(e):
                        def turn_x(i):
                            e.wait_ge(xn_ready, (i + 1) * G)
                            e.wait_ge(xT_ready, i)
                            turn(e, TURNED, xn).then_inc(xT_psum, 1)

                        def logit(i):
                            e.wait_ge(xT_ready, i + 1)
                            e.wait_ge(l_ready, i)
                            for g in range(G):
                                for c in range(C):
                                    kk = K + c
                                    m = e.matmul(LPS[:, g * E:(g + 1) * E], xT[0:kk, c, g * P:(g + 1) * P],
                                                 router[0:kk, c, :], start=(c == 0), stop=(c == C - 1))
                            m.then_inc(l_psum, 1)

                        def hidden(i):
                            e.wait_ge(relu_ready, i)
                            for n in range(C):
                                for c in range(C):
                                    m = e.matmul(HPS[0:K, n * S:(n + 1) * S], wfc[:, c, n * K:(n + 1) * K],
                                                 xT[0:K, c, :], start=(c == 0), stop=(c == C - 1))
                            m.then_inc(hid_psum, 1)

                        def shared_out(i):
                            e.wait_ge(hT_ready, i + 1)
                            e.wait_ge(o_ready, i)
                            for g in range(G):
                                for c in range(C):
                                    m = e.matmul(OPS[:, g * D:(g + 1) * D], hT[:, c, g * P:(g + 1) * P], wproj[:, c, :],
                                                 start=(c == 0), stop=(c == C - 1))
                            m.then_inc(o_psum, 1)

                        e.wait_ge(load, nload)
                        e.wait_ge(ones, 1)
                        turn_x(0)

                        def body(i, more):
                            logit(i)
                            if layer == 0:
                                hidden(i)
                            if more:
                                turn_x(i + 1)

                        body(0, True)
                        with e.Fori(1, B - 1) as i:
                            body(i, True)
                            if layer == 0:
                                shared_out(i - 1)
                        body(B - 1, False)
                        if layer == 0:
                            shared_out(B - 2)
                            shared_out(B - 1)

                    @block.scalar
                    def _(e):
                        root(e, ln)
                        with e.Fori(0, B) as i:
                            e.wait_ge(xT_psum, i + 1)
                            e.wait_ge(l_psum, i)
                            if layer == 0:
                                e.wait_ge(hid_psum, i)
                            e.activation(xT[0:K, :, :], TURNED[0:K, :].rearrange("p (c t) -> p c t", c=C),
                                         ACT.Identity).then_inc(xT_ready, 1)
                            if layer == 0:
                                e.wait_ge(hid_psum, i + 1)
                                e.wait_ge(hT_ready, i)
                                e.activation(relu[:, :, :], HPS[0:K, :].rearrange("p (c t) -> p c t", c=C),
                                             ACT.Relu).then_inc(relu_ready, 1)

                    @block.vector
                    def _(e):
                        statistics(e, ln)

                        def norm(i):
                            e.wait_ge(xT_psum, i)
                            e.wait_ge(kept, i)
                            for g in range(G):
                                normalise(e, xn, i, g).then_inc(xn_ready, 1)

                        def logits_out(i):
                            e.wait_ge(l_psum, i + 1)
                            e.tensor_copy(logits[:, bass.ds(i * G, G), :], LPS[:, 0:G * E].rearrange(
                                "p (g e) -> p g e", g=G)).then_inc(l_ready, 1)

                        def add_h(i):
                            e.wait_ge(o_psum, i + 1)
                            hh = h[:, bass.ds(i * G, G), :]
                            e.tensor_tensor(hh, OPS[:, 0:G * D].rearrange("p (g d) -> p g d", g=G), hh,
                                            ALU.add).then_inc(o_ready, 1)

                        norm(0)
                        norm(1)
                        logits_out(0)
                        with e.Fori(1, B - 1) as i:
                            norm(i + 1)
                            logits_out(i)
                            if layer == 0:
                                add_h(i - 1)
                        logits_out(B - 1)
                        if layer == 0:
                            add_h(B - 2)
                            add_h(B - 1)

        tokens()
        hyena()
        moe(0)
        nc.clear_and_free_semaphores(stage_sems)
        del stage_sems[:]
        with nc.Block():
            pass
        attention()
        moe(1)


def _chunks(w, rows=96):
    return w.reshape(-1, rows, w.shape[-1]).transpose(1, 0, 2)


def _experts(w, rows):
    return w.reshape(w.shape[0], -1, rows, w.shape[-1]).transpose(2, 0, 1, 3)


def _constants():
    import numpy as np
    c = {}
    f32 = np.float32
    c["c_ident"] = np.eye(128, dtype=f32)
    arg = (np.arange(256, dtype=f32)[:, None] * np.arange(64, dtype=f32)[None] / f32(64)).astype(np.float64)
    c["c_basis"] = np.concatenate([np.sin(arg).T, np.ones((1, 256))]).astype(f32)
    n = 384
    w = np.arange(192)
    t = np.arange(256)
    th = lambda k: 2 * np.pi * ((w[:, None] * k[None]) % n) / n
    alt = lambda k: np.where(k % 2 == 0, 1.0, -1.0)
    cos_, sin_ = np.cos(th(t)), np.sin(th(t))
    sin_[0] = alt(t)
    c["c_fwd"] = np.concatenate([cos_, sin_]).T.reshape(2, 128, 384).transpose(1, 0, 2).astype(f32)
    k = t - 128
    p, q = np.cos(th(k)), np.sin(th(k))
    r = -p.copy()
    r[0] = -alt(k)
    c["c_to_spec"] = np.concatenate([p, q, r]).T.reshape(2, 128, 576).transpose(1, 0, 2).astype(f32)
    two = np.where(w == 0, 1.0, 2.0)[:, None] / n
    ic, is_ = np.cos(th(t)) * two, -np.sin(th(t)) * two
    is_[0] = -alt(t) / n
    c["c_inv"] = np.concatenate([ic, is_]).reshape(4, 96, 256).transpose(1, 0, 2).astype(f32)
    keep = np.ones((8, 32))
    keep[:, 0] = 0
    number = np.arange(32)[:, None] + 32 * np.arange(2)[None] + 1
    common = np.concatenate([8 - np.arange(8), 128 * np.arange(32), np.arange(72), keep.ravel(), np.arange(128),
                             number.ravel()])
    part = np.arange(128)[:, None]
    no_token = 128 + 8192 + 128 * np.arange(72)[None] + part
    c["c_route"] = np.concatenate([np.tile(common[None], (128, 1)), no_token, part], 1).astype(f32)
    c["c_upper"] = np.triu(np.ones((128, 128)), 1).astype(f32)
    c["no_bias"] = np.zeros((1, 2, 8), f32)
    b16 = np.dtype("bfloat16")
    inv_freq = f32(1) / f32(10000) ** (np.arange(0, 16, 2, dtype=f32) / f32(16))
    ang = (np.arange(256, dtype=f32)[:, None] * inv_freq[None]).astype(f32).astype(np.float64)
    cs = np.stack([np.concatenate([np.cos(ang)] * 2, 1), np.concatenate([-np.sin(ang), np.sin(ang)], 1)], 1).astype(f32)
    c["c_rope"] = np.stack([cs * f32(0.25), cs], 1).reshape(2, 128, 2, 2, 16).transpose(1, 0, 2, 3, 4)
    c["c_identb"] = np.eye(128).astype(b16)
    q, k = np.arange(128)[:, None], np.arange(128)[None]
    causal = np.where((q // 64 == k // 64) & (k > q), -1e30, 0.0)
    c["c_causal"], c["c_causalT"] = causal.astype(b16), causal.T.astype(b16)
    key = np.zeros((12, 8, 12, 2, 128))
    for hd in range(12):
        for n in range(4):
            key[hd, n, hd] = (np.arange(256) // 64 == n).reshape(2, 128)
        key[hd, 4:7, hd] = 1
    c["c_keyside"] = key.reshape(96, 12, 2, 128).astype(b16)
    drop = np.zeros((128, 12, 2, 4))
    drop[:, :, 0, 3] = drop[:64, :, 1, 3] = -1e30
    c["c_drop"] = drop.astype(f32)
    return {k: np.ascontiguousarray(v) for k, v in c.items()}


def _arrays(i):
    import numpy as np
    i = {k: np.asarray(v) for k, v in i.items()}
    r = {}
    r["x"] = i["x"].transpose(2, 3, 0, 1).reshape(84 * 84, 48)
    r["curve"] = i["L0_tok_curve"]
    tw = np.zeros((49, 16, 192), np.float32)
    for b in range(16):
        tw[3 * b:3 * b + 3, b] = i["L0_tok_proj_w"].T
        tw[48, b] = i["L0_tok_proj_b"]
    r["tok_w"] = tw
    r["w_in"] = _chunks(i["L0_attn_w_in"])
    r["b_in"] = i["L0_attn_b_in"].reshape(1, 768)
    r["w_filt"] = i["L0_attn_w_filt"]
    r["b_filt"] = i["L0_attn_b_filt"].reshape(1, 192)
    r["short"] = np.concatenate([i["L0_attn_w_short"][:, 0, :], i["L0_attn_b_short"][:, None]], 1
                                ).reshape(2, 96, 4).transpose(1, 0, 2)
    r["w_out"] = _chunks(i["L0_attn_w_out"])
    r["b_out"] = i["L0_attn_b_out"].reshape(1, 192)
    r["router0"] = _chunks(i["L0_ffn_router_w"].T)
    r["balance"] = i["L0_ffn_balance_bias"]
    r["w_fc_sh"] = _chunks(i["L0_ffn_w_fc_sh"])
    r["w_proj_sh"] = _chunks(i["L0_ffn_w_proj_sh"])
    r["w1_0"] = _experts(i["L0_ffn_w1"], 96)
    r["w2_0"] = _experts(i["L0_ffn_w2"], 96)
    r["router1"] = _chunks(i["L1_ffn_Wr"])
    r["br"] = i["L1_ffn_br"].reshape(1, 8)
    r["w1_1"] = _experts(i["L1_ffn_Wfc"], 96)
    r["bfc"] = i["L1_ffn_bfc"].reshape(1, 8, 768)
    r["w2_1"] = _experts(i["L1_ffn_Wproj"], 128)
    r["bproj"] = i["L1_ffn_bproj"]
    r["wqkv"] = _chunks(np.concatenate([i["L1_attn_Wq"].T, i["L1_attn_Wk"].T, i["L1_attn_Wv"].T], 1))
    wo = np.zeros((3, 4, 32, 192), np.float32)
    wo[:, :, :16] = i["L1_attn_Wo"].T.reshape(3, 4, 16, 192)
    r["wo"] = wo.reshape(3, 128, 192).transpose(1, 0, 2)
    r.update(_constants())
    return {k: np.ascontiguousarray(v) for k, v in r.items()}


def kernel(**inputs):
    import numpy as np
    import concourse.bacc as bacc
    from concourse import mybir
    from concourse.bass_utils import run_bass_kernel_spmd

    nc = bacc.Bacc("TRN2", target_bir_lowering=False, num_devices=1)
    arrays, args = {}, {}
    for name, array in _arrays(inputs).items():
        arrays[f"in_{name}_dram"] = array
        args[name] = nc.dram_tensor(f"in_{name}_dram", array.shape, mybir.dt.from_np(array.dtype),
                                    kind="ExternalInput").ap()
    out = nc.dram_tensor("out_0_dram", (B, S, D), mybir.dt.from_np(np.dtype("float32")), kind="ExternalOutput").ap()
    build(nc, args, out)
    r = run_bass_kernel_spmd(nc, [arrays], core_ids=[0])
    return r.results[0]["out_0_dram"]
```

```python
from contextlib import ExitStack

import concourse.bass as bass
from concourse import mybir

F32 = mybir.dt.float32
BF16 = mybir.dt.bfloat16
I32 = mybir.dt.int32
U32 = mybir.dt.uint32
ALU = mybir.AluOpType
ACT = mybir.ActivationFunctionType
AX = mybir.AxisListType

P = 128
B, S, D = 16, 256, 192
G = S // P
T = B * G
C = 2
K = D // C
E = 8
XT = -(-2 * B * S // P) + E
HID = 768
HT = HID // P
HEADS, HD = 12, 16
HG = HEADS // 4
BLK = 64
NBLK = S // BLK
NEG = -1.0e30
EPS = 1e-5
RT_REV = slice(0, E)
RT_FIRST = slice(RT_REV.stop, RT_REV.stop + T)
RT_TILES = slice(RT_FIRST.stop, RT_FIRST.stop + XT)
RT_KEEP = slice(RT_TILES.stop, RT_TILES.stop + E * T)
RT_ROW = slice(RT_KEEP.stop, RT_KEEP.stop + P)
RT_NUMBER = slice(RT_ROW.stop, RT_ROW.stop + 2 * T)
RT_NO_TOKEN = slice(RT_NUMBER.stop, RT_NUMBER.stop + XT)
RT_PART = slice(RT_NO_TOKEN.stop, RT_NO_TOKEN.stop + 1)
RT = RT_PART.stop
IMG = 84


class Own:

    def __init__(self, eng, sem):
        self.eng, self.sem, self.base, self.k = eng, sem, 0, 0

    def step(self, ins):
        ins.then_inc(self.sem, 1)
        self.k += 1
        return ins

    def wait(self):
        self.eng.wait_ge(self.sem, self.base + self.k)

    def chain(self, ins):
        self.step(ins)
        self.wait()

    def enter(self, i, per):
        self.start = self.base + self.k
        self.per, self.k = per, 0
        self.base = self.start + i * per

    def leave(self, trips):
        assert self.k == self.per, (self.k, self.per)
        self.base, self.k = self.start + trips * self.per, 0


def until(e, sem, count):
    if not isinstance(count, int) or count > 0:
        e.wait_ge(sem, count)


def build(nc, a, out):
    top = ExitStack()
    with top:
        def sb_in(ctx, name, shape, dt=F32):
            return ctx.enter_context(nc.sbuf_tensor(name, shape, dt))

        stage_sems = []

        def sem_in(ctx, *names):
            made = [nc.alloc_semaphore(n) for n in names]
            if ctx is not top:
                stage_sems.extend(made)
            return made if len(made) > 1 else made[0]

        bank = [top.enter_context(nc.psum_tensor(f"bank{n}", [P, 2, 512], F32)) for n in range(4)]

        def ps(n):
            return bank[n // 2][:, n % 2, :]

        h = sb_in(top, "h", [P, T, D])
        stats = sb_in(top, "stats", [P, T, 6])
        mean = sb_in(top, "mean", [P, T])
        rstd = sb_in(top, "rstd", [P, T])
        ident = sb_in(top, "ident", [P, P])
        stored = sem_in(top, "outputs_stored")

        x_rows = [nc.dram_tensor(f"x_rows{n}", (T * P, D), F32, kind="Internal").ap() for n in range(2)]
        y_rows = [nc.dram_tensor(f"y_rows{n}", ((2 * T + XT) * P, D), F32, kind="Internal").ap() for n in range(2)]

        def row_stats(eng, tile):
            return eng.bn_stats(stats[:, tile, :], h[:, tile, :])

        def tokens(first_loads, loads, filter_pe, filter_dve):
            with ExitStack() as ctx:
                sb = lambda *x: sb_in(ctx, *x)
                curve = sb("curve", [P, G, 2], I32)
                cf = sb("cf", [P, G, 2])
                neg = sb("neg", [P, G, 2])
                at = sb("at", [P, G], I32)
                atf = sb("atf", [P, G])
                pix = sb("pix", [P, G, 3 * B])
                pixT = sb("pixT", [3 * B + 1, G, P])
                wtok = sb("wtok", [3 * B + 1, B, D])
                curve_load, load, ready = sem_in(ctx, "tok_curve_load", "tok_load", "tok_index")
                gathered = sem_in(top, "tok_gathered")
                tr, trc, mm, hd, own, ones = sem_in(
                    ctx, "tok_pixT_in_psum", "tok_pixT", "tok_matmul", "tok_h", "tok_dve", "tok_ones")
                steps = [(g, b) for b in range(0, B, 2) for g in range(G)]
                with nc.Block() as block:
                    @block.sync
                    def _(e):
                        e.dma_start(curve[:, :, :], a["curve"].rearrange("(g p) c -> p g c", p=P)).then_inc(curve_load, 16)
                        for dst, src, sem in first_loads:
                            e.dma_start(dst, src).then_inc(sem, 16)
                        e.dma_start(ident[:, :], a["c_ident"]).then_inc(load, 16)
                        e.dma_start(wtok[:, :, :], a["tok_w"]).then_inc(load, 16)
                        for dst, src, sem in loads:
                            e.dma_start(dst, src).then_inc(sem, 16)

                    @block.gpsimd
                    def _(e):
                        e.memset(pixT[:, :, :], 1.0).then_inc(ones, 1)
                        e.wait_ge(ready, 1)
                        for g in range(G):
                            e.indirect_dma_start(pix[:, g, :], None, a["x"], bass.IndirectOffsetOnAxis(
                                at[:, g:g + 1].bitcast(U32), 0)).then_inc(gathered, 16)

                    def step_stats(e, n):
                        g, b = steps[n]
                        for k in range(2):
                            row_stats(e, (b + k) * G + g)

                    @block.vector
                    def _(e):
                        own_ = Own(e, own)
                        e.wait_ge(curve_load, 16)
                        own_.chain(e.tensor_copy(cf[:, :, :], curve[:, :, :]))
                        own_.chain(e.tensor_scalar(neg[:, :, :], cf[:, :, :], 0.0, float(IMG), ALU.is_lt, ALU.mult))
                        own_.chain(e.tensor_tensor(cf[:, :, :], cf[:, :, :], neg[:, :, :], ALU.add))
                        own_.chain(e.tensor_scalar(cf[:, :, :], cf[:, :, :], 0.0, float(IMG - 1), ALU.max, ALU.min))
                        own_.chain(e.scalar_tensor_tensor(atf[:, :], cf[:, :, 1], float(IMG), cf[:, :, 0],
                                                          ALU.mult, ALU.add))
                        e.tensor_copy(at[:, :], atf[:, :]).then_inc(ready, 1)
                        filter_dve(e)
                        e.wait_ge(ones, 1)
                        e.wait_ge(tr, 1)
                        e.tensor_copy(pixT[0:3 * B, :, :], ps(0)[0:3 * B, 0:G * P].rearrange("p (g t) -> p g t", g=G)
                                      ).then_inc(trc, 1)
                        for n, (g, b) in enumerate(steps):
                            e.wait_ge(mm, n + 1)
                            e.tensor_copy(h[:, b * G + g:(b + 1) * G + g + 1:G, :],
                                          ps(1 + n % 4)[:, 0:2 * D].rearrange("p (b d) -> p b d", b=2)
                                          ).then_inc(hd, 1)
                            if n:
                                e.wait_ge(hd, n)
                                step_stats(e, n - 1)
                        e.wait_ge(hd, len(steps))
                        step_stats(e, len(steps) - 1)

                    @block.tensor
                    def _(e):
                        filter_pe(e)
                        e.wait_ge(load, 32)
                        e.wait_ge(gathered, 16 * G)
                        for g in range(G):
                            m = e.transpose(ps(0)[0:3 * B, g * P:(g + 1) * P], pix[:, g, :], ident[:, :])
                        m.then_inc(tr, 1)
                        e.wait_ge(trc, 1)
                        for n, (g, b) in enumerate(steps):
                            if n >= 4:
                                e.wait_ge(hd, n - 3)
                            e.matmul(ps(1 + n % 4)[:, 0:2 * D], pixT[:, g, :], wtok[:, b:b + 2, :].rearrange(
                                "p b d -> p (b d)"), start=True, stop=True).then_inc(mm, 1)

        def ln_tensors(ctx, name):
            return dict(own=sem_in(ctx, name + "_ln_step"), var=sem_in(ctx, name + "_ln_var"),
                        root=sem_in(ctx, name + "_ln_root"), tmp=sb_in(ctx, name + "_ln_tmp", [P, 4, T]))

        def statistics(e, ln):
            s = Own(e, ln["own"])
            t = ln["tmp"]
            m0, q0, m1, q1 = (stats[:, :, n] for n in (1, 2, 4, 5))
            s.step(e.tensor_tensor(t[:, 0, :], m0, m1, ALU.add))
            s.step(e.tensor_tensor(t[:, 1, :], m0, m1, ALU.subtract))
            s.step(e.tensor_tensor(t[:, 2, :], q0, q1, ALU.add))
            s.wait()
            s.step(e.tensor_scalar(mean[:, :], t[:, 0, :], 0.5, None, ALU.mult))
            s.chain(e.tensor_tensor(t[:, 3, :], t[:, 1, :], t[:, 1, :], ALU.mult))
            s.chain(e.scalar_tensor_tensor(t[:, 0, :], t[:, 3, :], D / 4.0, t[:, 2, :], ALU.mult, ALU.add))
            e.tensor_scalar(t[:, 1, :], t[:, 0, :], 1.0 / D, EPS, ALU.mult, ALU.add).then_inc(ln["var"], 1)
            e.wait_ge(ln["root"], 1)
            s.chain(e.reciprocal(rstd[:, :], t[:, 2, :]))

        def root(e, ln):
            e.wait_ge(ln["var"], 1)
            e.activation(ln["tmp"][:, 2, :], ln["tmp"][:, 1, :], ACT.Sqrt).then_inc(ln["root"], 1)

        def normalise(e, xn, i, g):
            t = i * G + g
            return e.tensor_scalar(xn[:, g, :], h[:, t, :], mean[:, t:t + 1] if isinstance(t, int) else mean[:, bass.ds(t, 1)],
                                   rstd[:, t:t + 1] if isinstance(t, int) else rstd[:, bass.ds(t, 1)],
                                   ALU.subtract, ALU.mult)

        def turn(e, psum, src):
            for c in range(C):
                for g in range(G):
                    m = e.transpose(psum[0:K, c * S + g * P:c * S + (g + 1) * P], src[:, g, c * K:(c + 1) * K],
                                    ident[:, :])
            return m

        def hyena(later_loads):
            NF = 4
            with ExitStack() as ctx:
                sb = lambda *x: sb_in(ctx, *x)
                w_in = sb("w_in", [K + 1, C, 4 * D])
                w_out = sb("w_out", [K + 1, C, D])
                fwd = sb("fwd", [P, G, NF * K])
                inv = sb("inv", [K, NF, S])
                short = sb("short", [K, C, 4])
                specA = sb("specA", [K, 2, C * D])
                specB = sb("specB", [K, 2, C * D])
                ln = ln_tensors(ctx, "hy")
                load = sem_in(ctx, "hy_load")

                with ExitStack() as c2:
                    fl = sem_in(c2, "filter_load")
                    basis = sb_in(c2, "basis", [65, S])
                    wf = sb_in(c2, "wf", [65, D])
                    filt = sb_in(c2, "filt", [P, G, D])
                    to_spec = sb_in(c2, "to_spec", [P, G, 6 * K])
                    fp, ff, sp, sc = sem_in(c2, "filter_in_psum", "filter", "spectrum_in_psum", "spectrum")
                    def filter_pe(e):
                        e.wait_ge(fl, 64)
                        for g in range(G):
                            m = e.matmul(ps(5)[:, g * D:(g + 1) * D], basis[:, g * P:(g + 1) * P], wf[:, :],
                                         start=True, stop=True)
                        m.then_inc(fp, 1)
                        e.wait_ge(ff, 1)
                        for n in range(6):
                            for g in range(G):
                                m = e.matmul(ps((0, 6, 7)[n // 2])[0:K, (n % 2) * D:(n % 2 + 1) * D],
                                             to_spec[:, g, n * K:(n + 1) * K], filt[:, g, :],
                                             start=(g == 0), stop=(g == G - 1))
                        m.then_inc(sp, 1)
                        e.wait_ge(sc, 4)

                    def filter_dve(e):
                        e.wait_ge(fp, 1)
                        e.tensor_copy(filt[:, :, :], ps(5)[:, 0:G * D].rearrange("p (g d) -> p g d", g=G)
                                      ).then_inc(ff, 1)
                        e.wait_ge(sp, 1)
                        for to, n in ((specA[:, 0, :], 0), (specA[:, 1, :], 6), (specB[:, 1, :], 7),
                                      (specB[:, 0, :], 6)):
                            e.tensor_copy(to, ps(n)[0:K, 0:C * D]).then_inc(sc, 1)

                    tokens([(basis[:, :], a["c_basis"], fl), (wf[0:64, :], a["w_filt"], fl), (wf[64:65, :], a["b_filt"], fl),
                            (to_spec[:, :, :], a["c_to_spec"], fl)],
                           [(w_in[0:K, :, :], a["w_in"], load), (w_in[K:K + 1, 1, :], a["b_in"], load),
                            (fwd[:, :, :], a["c_fwd"], load), (inv[:, :, :], a["c_inv"], load),
                            (short[:, :, :], a["short"], load), (w_out[0:K, :, :], a["w_out"], load),
                            (w_out[K:K + 1, 1, :], a["b_out"], load)] + later_loads,
                           filter_pe, filter_dve)

                xn = sb("xn", [P, G, D])
                xT = [sb(f"xT{n}", [K + 1, C, S]) for n in range(2)]
                xp = sb("xp", [P, G, D])
                zs = sb("zs", [P, G, D])
                gate = sb("gate", [P, G, D])
                prA = sb("prA", [K, 2, C * D])
                prB = sb("prB", [K, 2, C * D])
                spec = sb("spec", [K, 2, C * D])
                y = sb("y", [P, G, D])
                xs = sb("xs", [K, C, S])
                yx = sb("yx", [K + 1, C, S])
                (xn_ready, xT_psum, xT_ready, xz_psum, xz_ready, v_psum, gate_ready, freq_psum, prod_ready, spec_ready,
                 conv_psum, y_ready, yT_psum, yx_ready, xs_begun, out_psum, h_ready, own, ones,
                 short_ready) = sem_in(
                    ctx, "hy_xn_ready", "hy_xT_in_psum", "hy_xT_ready", "hy_xz_in_psum", "hy_xz_ready", "hy_v_in_psum",
                    "hy_gate_ready", "hy_freq_in_psum", "hy_products_ready", "hy_spectrum_ready", "hy_conv_in_psum",
                    "hy_y_ready", "hy_yT_in_psum", "hy_yx_ready", "hy_short_begun", "hy_out_in_psum", "hy_h_ready",
                    "hy_dve_step", "hy_ones_rows",
                    "hy_short_ready")

                def pairs(e, body, own_steps=None):
                    trips = (B - 2) // 2
                    with e.Fori(0, trips) as r:
                        if own_steps:
                            own_steps.enter(r, 6)
                        for p in (1, 2):
                            body(r * 2 + p, p % 2, True)
                        if own_steps:
                            own_steps.leave(trips)
                    body(B - 1, (B - 1) % 2, False)

                TURNED, XZ, VV, FREQ, CONV = ps(0), bank[1], bank[2], bank[3], ps(1)

                with nc.Block() as block:
                    @block.gpsimd
                    def _(e):
                        for n in range(2):
                            e.memset(xT[n][K:K + 1, :, :], 1.0).then_inc(ones, 1)
                        e.memset(yx[K:K + 1, :, :], 1.0).then_inc(ones, 1)
                        with e.Fori(0, B) as i:
                            e.wait_ge(prod_ready, (i + 1) * 2)
                            e.wait_ge(conv_psum, i)
                            e.tensor_tensor(spec[:, :, :], prA[:, :, :], prB[:, :, :], ALU.add).then_inc(spec_ready, 1)

                    @block.tensor
                    def _(e):
                        def turn_x(i):
                            e.wait_ge(xn_ready, (i + 1) * G)
                            turn(e, TURNED, xn).then_inc(xT_psum, 1)

                        def project(i, p, half, psum, done, free):
                            if half == 0:
                                e.wait_ge(xT_ready, i + 1)
                            e.wait_ge(free, i)
                            for g in range(G):
                                for c in range(C):
                                    kk = K + c
                                    m = e.matmul(psum[:, g, 0:2 * D], xT[p][0:kk, c, g * P:(g + 1) * P],
                                                 w_in[0:kk, c, half * 2 * D:(half + 1) * 2 * D],
                                                 start=(c == 0), stop=(c == C - 1))
                            m.then_inc(done, 1)

                        def forward(i):
                            e.wait_ge(xz_ready, i + 1)
                            e.wait_ge(prod_ready, i * 2)
                            for f in range(NF):
                                for g in range(G):
                                    m = e.matmul(FREQ[0:K, f // 2, (f % 2) * D:(f % 2 + 1) * D],
                                                 fwd[:, g, f * K:(f + 1) * K], xp[:, g, :],
                                                 start=(g == 0), stop=(g == G - 1))
                            m.then_inc(freq_psum, 1)

                        def inverse(i):
                            e.wait_ge(spec_ready, i + 1)
                            e.wait_ge(h_ready, i)
                            for g in range(G):
                                for f in range(NF):
                                    m = e.matmul(CONV[:, g * D:(g + 1) * D], inv[:, f, g * P:(g + 1) * P],
                                                 spec[:, f // 2, (f % 2) * D:(f % 2 + 1) * D],
                                                 start=(f == 0), stop=(f == NF - 1))
                            m.then_inc(conv_psum, 1)

                        def turn_y(i):
                            e.wait_ge(y_ready, i + 1)
                            turn(e, TURNED, y).then_inc(yT_psum, 1)

                        def project_out(i):
                            e.wait_ge(yx_ready, i + 1)
                            for g in range(G):
                                for c in range(C):
                                    kk = K + c
                                    m = e.matmul(CONV[:, g * D:(g + 1) * D], yx[0:kk, c, g * P:(g + 1) * P],
                                                 w_out[0:kk, c, :], start=(c == 0), stop=(c == C - 1))
                            m.then_inc(out_psum, 1)

                        e.wait_ge(load, 112)
                        e.wait_ge(ones, 3)
                        turn_x(0)
                        project(0, 0, 0, XZ, xz_psum, xz_ready)
                        project(0, 0, 1, VV, v_psum, gate_ready)
                        forward(0)
                        turn_x(1)

                        def body(i, p, more):
                            project(i, p, 0, XZ, xz_psum, xz_ready)
                            inverse(i - 1)
                            project(i, p, 1, VV, v_psum, gate_ready)
                            turn_y(i - 1)
                            forward(i)
                            if more:
                                e.wait_ge(yx_ready, i)
                                turn_x(i + 1)
                            project_out(i - 1)

                        pairs(e, body)
                        inverse(B - 1)
                        turn_y(B - 1)
                        project_out(B - 1)

                    @block.scalar
                    def _(e):
                        def xT_out(i, p):
                            e.wait_ge(xT_psum, i + 1)
                            until(e, v_psum, i - 1)
                            until(e, short_ready, (i - 1) * C)
                            e.activation(xT[p][0:K, :, :], TURNED[0:K, :].rearrange("p (c t) -> p c t", c=C),
                                         ACT.Identity).then_inc(xT_ready, 1)

                        def body(i, p, more):
                            e.wait_ge(xz_psum, i + 1)
                            until(e, gate_ready, i)
                            e.activation(zs[:, :, :], XZ[:, :, D:2 * D], ACT.Silu)
                            until(e, freq_psum, i)
                            e.activation(xp[:, :, :], XZ[:, :, 0:D], ACT.Identity).then_inc(xz_ready, 1)
                            until(e, yx_ready, i)
                            e.wait_ge(xT_ready, i + 1)
                            for c in range(C):
                                m = e.activation(xs[:, c, :], xT[p][0:K, c, :], ACT.Identity,
                                                 bias=short[:, c, 3:4], scale=short[:, c, 1:2])
                            m.then_inc(xs_begun, 1)
                            if more:
                                xT_out(i + 1, 1 - p)

                        root(e, ln)
                        e.wait_ge(load, 112)
                        xT_out(0, 0)
                        body(0, 0, True)
                        pairs(e, body)

                    @block.vector
                    def _(e):
                        s = Own(e, own)

                        def norm(i):
                            e.wait_ge(xT_psum, i)
                            for g in range(G):
                                normalise(e, xn, i, g).then_inc(xn_ready, 1)

                        def conv_out(i):
                            e.wait_ge(conv_psum, i + 1)
                            e.wait_ge(yT_psum, i)
                            e.tensor_tensor(y[:, :, :], CONV[:, 0:G * D].rearrange("p (g d) -> p g d", g=G),
                                            gate[:, :, :], ALU.mult).then_inc(y_ready, 1)

                        def gates(i):
                            e.wait_ge(v_psum, i + 1)
                            e.wait_ge(xz_ready, i + 1)
                            e.wait_ge(y_ready, i)
                            s.chain(e.tensor_tensor(gate[:, :, :], VV[:, :, 0:D], zs[:, :, :], ALU.mult))
                            e.tensor_tensor(gate[:, :, :], VV[:, :, D:2 * D], gate[:, :, :], ALU.mult
                                            ).then_inc(gate_ready, 1)

                        def join(i):
                            e.wait_ge(yT_psum, i + 1)
                            e.wait_ge(out_psum, i)
                            e.wait_ge(short_ready, (i + 1) * C)
                            e.tensor_tensor(yx[0:K, :, :], TURNED[0:K, :].rearrange("p (c t) -> p c t", c=C),
                                            xs[:, :, :], ALU.add).then_inc(yx_ready, 1)

                        def short_conv(i, p):
                            e.wait_ge(xs_begun, i + 1)
                            for c in range(C):
                                s.step(e.scalar_tensor_tensor(xs[:, c, 1:S], xT[p][0:K, c, 0:S - 1], short[:, c, 0:1],
                                                              xs[:, c, 1:S], ALU.mult, ALU.add))
                            s.wait()
                            for c in range(C):
                                e.scalar_tensor_tensor(xs[:, c, 0:S - 1], xT[p][0:K, c, 1:S], short[:, c, 2:3],
                                                       xs[:, c, 0:S - 1], ALU.mult, ALU.add).then_inc(short_ready, 1)

                        def products(i):
                            e.wait_ge(freq_psum, i + 1)
                            e.wait_ge(spec_ready, i)
                            for n, (pr, sp) in enumerate(((prA, specA), (prB, specB))):
                                e.tensor_tensor(pr[:, :, :], FREQ[0:K, n, 0:C * D].unsqueeze(1).to_broadcast(
                                    [K, 2, C * D]), sp[:, :, :], ALU.mult).then_inc(prod_ready, 1)

                        def add_h(i):
                            e.wait_ge(out_psum, i + 1)
                            hh = h[:, bass.ds(i * G, G), :]
                            e.tensor_tensor(hh, CONV[:, 0:G * D].rearrange("p (g d) -> p g d", g=G), hh,
                                            ALU.add).then_inc(h_ready, 1)
                            e.wait_ge(h_ready, i + 1)
                            for g in range(G):
                                row_stats(e, i * G + g)

                        statistics(e, ln)
                        e.wait_ge(load, 112)
                        norm(0)
                        gates(0)
                        norm(1)
                        short_conv(0, 0)
                        products(0)

                        def body(i, p, more):
                            conv_out(i - 1)
                            gates(i)
                            if more:
                                norm(i + 1)
                            join(i - 1)
                            products(i)
                            short_conv(i, p)
                            add_h(i - 1)

                        pairs(e, body, s)
                        conv_out(B - 1)
                        join(B - 1)
                        add_h(B - 1)

        def attention(later_loads):
            N = 2 * HEADS
            SL = 6 * HD
            NP = 6
            with ExitStack() as ctx:
                sb = lambda n, *x: sb_in(ctx, "at_" + n, *x)
                ln = ln_tensors(ctx, "at")
                wqkv = sb("wqkv", [K, C, 3 * D])
                wo = sb("wo", [P, HG, D])
                rope = sb("rope", [P, G, 2, 2, HD])
                identb = sb("identb", [P, P], BF16)
                causal = sb("causal", [P, P], BF16)
                causalT = sb("causalT", [P, P], BF16)
                keyside = sb("keyside", [SL, HEADS, G, P], BF16)
                xn = sb("xn", [P, G, D])
                xT = sb("xT", [K, C, S])
                tcos, tsin, xr, r1 = (sb(n, [P, 2, G, HEADS, HD]) for n in ("tcos", "tsin", "xr", "r1"))
                hi, mid = (sb(n, [P, 2, N, HD], BF16) for n in ("hi", "mid"))
                slots = sb("slots", [P, 2, N, 6, HD], BF16)
                qkT = [sb(f"qkT{n}", [SL, 2, HEADS, S], BF16) for n in range(2)]
                v1 = [sb(f"v1{n}", [P, G, HEADS, 2, HD]) for n in range(2)]
                bmax = sb("bmax", [P, HEADS, G, NBLK])
                bsum = sb("bsum", [P, HEADS, 3])
                least, other = sb("least", [P, HEADS]), sb("other", [P, HEADS])
                same = sb("same", [P, HEADS, 3])
                drop = sb("drop", [P, HEADS, G, NBLK])
                masked = sb("masked", [P, HEADS, G, NBLK])
                top, negm, nr = (sb(n, [P, HEADS, G]) for n in ("top", "negm", "nr"))
                qside = sb("qside", [P, G, HEADS, 8], BF16)
                qsideT = sb("qsideT", [SL, S], BF16)
                prob = [sb(f"prob{n}", [P, G, S]) for n in range(NP)]
                NS = HG * S // 32
                den = sb("den", [P, NS, 32])
                rden = sb("rden", [P, NS])
                rec, attnT = sb("rec", [P, HG, S]), sb("attnT", [P, HG, S])
                names = ("load", "filled", "xn_ready", "xT_in_psum", "xT_ready", "qk_in_psum", "v_in_psum", "turned_by_angle",
                         "rope_ready", "hi_ready", "rest_ready", "mid_ready", "slots_by_pool", "slots_by_dve",
                         "slots_by_act", "v_ready", "slotsT_in_psum", "slotsT_by_act", "slotsT_by_dve", "scores_in_psum",
                         "blocks_reduced", "qside_ready", "qsideT_in_psum", "qsideT_ready", "scoresT_in_psum",
                         "prob_ready", "pv_done", "attn_ready", "out_in_psum", "h_ready", "dve_step", "gone_on", "pool_goes_on")
                (load, filled, xn_ready, xT_psum, xT_ready, qk_psum, v_psum, rot, rope_ready, hi_ready, rest_ready, mid_ready,
                 slots_pool, slots_dve, slots_act, v_ready, sT_psum, sT_act, sT_dve, s_psum, reduced, qs_ready, qsT_psum,
                 qsT_ready, s2_psum, prob_ready, pv_done, attn_ready, out_psum, h_ready, own, gone_on, pool_on) = sem_in(
                     ctx, *("at_" + n for n in names))
                SA, SC = (ps(0), ps(1)), (ps(2), ps(3))
                MISC, VPS, OPS = ps(4), ps(5), bank[3]
                QK = SA
                SCB = [x.bitcast(BF16) for x in SC]
                SPOOL, SDVE, SACT = 2, 3, 2
                QSPS = OPS[:, 1, S:2 * S].bitcast(BF16)

                def last(j, ahead):
                    return min(j + ahead + 1, B) if isinstance(j, int) else j + ahead + 1

                def run(e, body, own_steps=None):
                    first, trips = 2, (B - 6) // 2
                    for i in range(-4, first):
                        body(i, i % 2, lambda ahead: 0 <= i + ahead < B)
                    with e.Fori(0, trips) as r:
                        if own_steps:
                            own_steps[0].enter(r, own_steps[1])
                        for p in range(2):
                            body(r * 2 + first + p, p, lambda ahead: True)
                        if own_steps:
                            own_steps[0].leave(trips)
                    for i in range(first + 2 * trips, B + 1):
                        body(i, i % 2, lambda ahead: 0 <= i + ahead < B)

                with nc.Block() as block:
                    @block.sync
                    def _(e):
                        for dst, src in ((wqkv, "wqkv"), (wo, "wo"), (rope, "c_rope"), (identb, "c_identb"),
                                         (causal, "c_causal"), (causalT, "c_causalT"), (keyside, "c_keyside"),
                                         (drop, "c_drop")):
                            e.dma_start(dst[:], a[src]).then_inc(load, 16)
                        for dst, src, sem in later_loads:
                            e.dma_start(dst, src).then_inc(sem, 16)

                    three = lambda x, n: x.unsqueeze(2).to_broadcast([P, N, n, HD])

                    @block.gpsimd
                    def _(e):
                        for n in range(2):
                            e.memset(v1[n][:, :, :, 1, :], 1.0).then_inc(filled, 1)
                        e.memset(qside[:, :, :, :], 0.0).then_inc(filled, 1)

                        def fill_slots(j):
                            until(e, mid_ready, j + 1)
                            until(e, sT_psum, j * 6)
                            e.sem_inc(pool_on, 1)
                            for dst, src in ((slots[:, 0, :, 0:3, :], three(hi[:, 0], 3)),
                                             (slots[:, 0, :, 3:5, :], three(mid[:, 0], 2))):
                                e.tensor_copy(dst, src).then_inc(slots_pool, 1)

                        def add_rotated(j):
                            until(e, rot, (j + 1) * 3 * G)
                            until(e, rest_ready, j)
                            until(e, hi_ready, j)
                            e.tensor_tensor(xr[:], tcos[:], tsin[:], ALU.add).then_inc(rope_ready, 1)

                        def body(i, p, there):
                            if there(2):
                                fill_slots(i + 2)
                            if there(3):
                                add_rotated(i + 3)

                        run(e, body)

                    @block.tensor
                    def _(e):
                        def turn_x(j):
                            until(e, xn_ready, (j + 1) * G)
                            until(e, h_ready, j - 4)
                            turn(e, MISC, xn).then_inc(xT_psum, 1)

                        def project_qk(j):
                            until(e, xT_ready, j + 1)
                            until(e, prob_ready, (j - 2) * HEADS)
                            until(e, rot, j * 3 * G)
                            for g in range(G):
                                for c in range(C):
                                    m = e.matmul(QK[g][:, 0:2 * D], xT[:, c, g * P:(g + 1) * P],
                                                 wqkv[:, c, 0:2 * D], start=(c == 0), stop=(c == C - 1))
                            m.then_inc(qk_psum, 1)

                        def project_v(j):
                            until(e, xT_ready, j + 1)
                            until(e, v_ready, j)
                            for g in range(G):
                                for c in range(C):
                                    m = e.matmul(VPS[:, g * D:(g + 1) * D], xT[:, c, g * P:(g + 1) * P],
                                                 wqkv[:, c, 2 * D:3 * D], start=(c == 0), stop=(c == C - 1))
                            m.then_inc(v_psum, 1)

                        def turn_slots(j, part):
                            if part == 0:
                                until(e, slots_pool, (j + 1) * SPOOL)
                                until(e, slots_dve, (j + 1) * SDVE)
                                until(e, slots_act, (j + 1) * SACT)
                                until(e, reduced, j * HEADS * 2)
                            for n in (2 * part, 2 * part + 1):
                                if n >= 2:
                                    until(e, (sT_act, sT_dve)[n % 2], j * 3 + n // 2)
                                for k in range(8):
                                    hd, g = 4 * (n % 3) + k // 2, k % 2
                                    m = e.transpose(SCB[n % 2][0:SL, k * P:(k + 1) * P],
                                                    slots[:, n // 3, g * HEADS + hd].rearrange("p s d -> p (s d)"),
                                                    identb[:, :])
                                m.then_inc(sT_psum, 1)

                        def score(j, p, hd):
                            if hd == 0:
                                until(e, sT_act, (j + 1) * 3)
                                until(e, sT_dve, (j + 1) * 3)
                            if hd >= 2:
                                until(e, reduced, (j * HEADS + hd - 1) * 2)
                            for g in range(G):
                                o = SC[hd % 2][:, g * S:(g + 1) * S]
                                e.matmul(o, qkT[p][:, 0, hd, g * P:(g + 1) * P], qkT[p][:, 1, hd, :],
                                         start=True, stop=False)
                                m = e.matmul(o[:, g * P:(g + 1) * P], identb[:, :], causal[:, :],
                                             start=False, stop=True)
                            m.then_inc(s_psum, 1)

                        def turn_qside(j):
                            until(e, qs_ready, (j + 1) * 4)
                            until(e, qsT_ready, j)
                            for g in range(G):
                                m = e.transpose(QSPS[0:SL, g * P:(g + 1) * P],
                                                qside[:, g].rearrange("p h s -> p (h s)"), identb[:, :])
                            m.then_inc(qsT_psum, 1)

                        def scoreT(j, p, hd):
                            if hd == 0:
                                until(e, qsT_ready, j + 1)
                            if hd < 2:
                                until(e, rot, last(j, 2) * 3 * G)
                            else:
                                until(e, prob_ready, j * HEADS + hd - 1)
                            for g in range(G):
                                o = SA[hd % 2][:, g * S:(g + 1) * S]
                                e.matmul(o, qkT[p][:, 1, hd, g * P:(g + 1) * P], qkT[p][:, 0, hd, :],
                                         start=True, stop=False)
                                e.matmul(o, keyside[:, hd, g, :], qsideT[:, :], start=False, stop=False)
                                m = e.matmul(o[:, g * P:(g + 1) * P], identb[:, :], causalT[:, :],
                                             start=False, stop=True)
                            m.then_inc(s2_psum, 1)

                        def values(j, p, n):
                            until(e, prob_ready, j * HEADS + 4 * (n + 1))
                            if n == 0:
                                until(e, v_ready, j + 1)
                                until(e, attn_ready, j * 2)
                            for g in range(G):
                                for q in range(4):
                                    hd = 4 * n + q
                                    m = e.matmul(OPS[q * 32:q * 32 + 32, n // 2, n % 2 * S:(n % 2 + 1) * S],
                                                 v1[p][:, g, hd].rearrange("p two d -> p (two d)"),
                                                 prob[hd % NP][:, g, :], start=(g == 0), stop=(g == G - 1))
                            m.then_inc(pv_done, 1)

                        def project_out(j):
                            until(e, attn_ready, (j + 1) * 2)
                            until(e, xT_ready, last(j, 4))
                            for g in range(G):
                                for n in range(HG):
                                    m = e.matmul(MISC[:, g * D:(g + 1) * D], attnT[:, n, g * P:(g + 1) * P],
                                                 wo[:, n, :], start=(n == 0), stop=(n == HG - 1))
                            m.then_inc(out_psum, 1)

                        def body(i, p, there):
                            for hd in range(HEADS):
                                if there(0):
                                    scoreT(i, p, hd)
                                if there(1):
                                    score(i + 1, 1 - p, hd)
                                if there(0) and hd in (5, 9):
                                    values(i, p, hd // 4 - 1)
                                if there(-1) and hd == 6:
                                    project_out(i - 1)
                            if there(0):
                                values(i, p, HG - 1)
                            if there(2):
                                turn_slots(i + 2, 0)
                            if there(3):
                                project_qk(i + 3)
                            if there(2):
                                turn_slots(i + 2, 1)
                            if there(1):
                                turn_qside(i + 1)
                            if there(3):
                                project_v(i + 3)
                            if there(2):
                                turn_slots(i + 2, 2)
                            if there(4):
                                turn_x(i + 4)

                        e.wait_ge(load, 128)
                        e.wait_ge(filled, 3)
                        run(e, body)

                    @block.scalar
                    def _(e):
                        root(e, ln)

                        def xT_out(j):
                            until(e, xT_psum, j + 1)
                            until(e, v_psum, j)
                            e.activation(xT[:, :, :], MISC[0:K, :].rearrange("p (c t) -> p c t", c=C),
                                         ACT.Identity).then_inc(xT_ready, 1)

                        def his(j):
                            until(e, rope_ready, j + 1)
                            until(e, slots_pool, j * SPOOL)
                            until(e, slots_dve, j * SDVE)
                            until(e, slots_act, j * SACT)
                            until(e, rest_ready, j)
                            e.activation(hi[:].rearrange("p a n d -> p (a n d)"),
                                         xr[:].rearrange("p a g h d -> p (a g h d)"), ACT.Identity).then_inc(hi_ready, 1)

                        def mids(j):
                            until(e, rest_ready, j + 1)
                            until(e, slots_pool, j * SPOOL)
                            until(e, slots_dve, j * SDVE)
                            until(e, slots_act, j * SACT)
                            e.activation(mid[:].rearrange("p a n d -> p (a n d)"),
                                         r1[:].rearrange("p a g h d -> p (a g h d)"), ACT.Identity).then_inc(mid_ready, 1)

                        def fill_slots(j):
                            until(e, mid_ready, j + 1)
                            until(e, sT_psum, j * 6)
                            e.activation(slots[:, 1, :, 1:5:3, :], three(mid[:, 1], 2), ACT.Identity
                                         ).then_inc(slots_act, 1)
                            e.activation(slots[:, 1, :, 5, :], hi[:, 1], ACT.Identity).then_inc(slots_act, 1)

                        def v_out(j, p):
                            until(e, v_psum, j + 1)
                            until(e, pv_done, (j - 1) * HG)
                            e.activation(v1[p][:, :, :, 0, :].rearrange("p g h d -> p (g h) d"),
                                         VPS[:, 0:G * D].rearrange("p (n d) -> p n d", d=HD),
                                         ACT.Identity).then_inc(v_ready, 1)

                        def slotsT_out(j, p, n):
                            until(e, sT_psum, j * 6 + n + 1)
                            if n == 0:
                                until(e, s2_psum, (j - 1) * HEADS)
                            e.activation(qkT[p][:, n // 3, 4 * (n % 3):4 * (n % 3) + 4, :],
                                         SCB[0][0:SL, :].rearrange("p (h t) -> p h t", h=4),
                                         ACT.Identity).then_inc(sT_act, 1)

                        def exponent(j, hd):
                            until(e, s2_psum, j * HEADS + hd + 1)
                            until(e, pv_done, j * HG + (hd - NP) // 4 + 1 if hd >= NP else
                                  (j - 1) * HG + (hd + NP) // 4 + 1)
                            e.activation(prob[hd % NP][:, :, :], SA[hd % 2].rearrange("p (g t) -> p g t", g=G),
                                         ACT.Exp).then_inc(prob_ready, 1)

                        def body(i, p, there):
                            if there(3):
                                xT_out(i + 3)
                            for hd in range(HEADS):
                                if there(0):
                                    exponent(i, hd)
                                if there(2) and hd == 4:
                                    mids(i + 2)
                                if there(2) and hd == 8:
                                    fill_slots(i + 2)
                            if there(2):
                                slotsT_out(i + 2, p, 0)
                                v_out(i + 2, p)
                                slotsT_out(i + 2, p, 2)
                                slotsT_out(i + 2, p, 4)
                            if there(3):
                                his(i + 3)

                        e.wait_ge(filled, 3)
                        run(e, body)

                    @block.vector
                    def _(e):
                        statistics(e, ln)
                        s = Own(e, own)

                        def norm(j):
                            until(e, xT_psum, j)
                            for g in range(G):
                                normalise(e, xn, j, g).then_inc(xn_ready, 1)

                        def rotate(j):
                            until(e, qk_psum, j + 1)
                            until(e, rope_ready, j)
                            for g in range(G):
                                x = QK[g][:, 0:2 * D].rearrange("p (a h d) -> p a h d", a=2, h=HEADS)
                                cos_, sin_ = (rope[:, g, :, n, :].unsqueeze(2).to_broadcast([P, 2, HEADS, HD])
                                              for n in range(2))
                                e.tensor_tensor(tcos[:, :, g], x, cos_, ALU.mult).then_inc(rot, 1)
                                e.tensor_tensor(tsin[:, :, g, :, 0:HD // 2], x[:, :, :, HD // 2:HD],
                                                sin_[:, :, :, 0:HD // 2], ALU.mult).then_inc(rot, 1)
                                e.tensor_tensor(tsin[:, :, g, :, HD // 2:HD], x[:, :, :, 0:HD // 2],
                                                sin_[:, :, :, HD // 2:HD], ALU.mult).then_inc(rot, 1)

                        def rest(j):
                            until(e, hi_ready, j + 1)
                            until(e, mid_ready, j)
                            until(e, slots_dve, j * SDVE)
                            e.tensor_tensor(r1[:].rearrange("p a g h d -> p (a g h d)"),
                                            xr[:].rearrange("p a g h d -> p (a g h d)"),
                                            hi[:].rearrange("p a n d -> p (a n d)"), ALU.subtract
                                            ).then_inc(rest_ready, 1)

                        def fill_slots(j):
                            until(e, mid_ready, j + 1)
                            until(e, sT_psum, j * 6)
                            e.tensor_copy(slots[:, 1, :, 0:4:3, :], three(hi[:, 1], 2)).then_inc(slots_dve, 1)
                            for n, at in ((0, 5), (1, 2)):
                                e.tensor_tensor(slots[:, n, :, at, :], r1[:, n].rearrange("p g h d -> p (g h) d"),
                                                mid[:, n], ALU.subtract).then_inc(slots_dve, 1)

                        def slotsT_out(j, p, n):
                            until(e, sT_psum, j * 6 + n + 1)
                            if n == 1:
                                until(e, s2_psum, (j - 1) * HEADS)
                            e.tensor_copy(qkT[p][:, n // 3, 4 * (n % 3):4 * (n % 3) + 4, :],
                                          SCB[1][0:SL, :].rearrange("p (h t) -> p h t", h=4)).then_inc(sT_dve, 1)

                        def reduce_blocks(j, hd):
                            until(e, s_psum, j * HEADS + hd + 1)
                            x = SC[hd % 2].rearrange("p (n k) -> p n k", k=BLK)
                            e.tensor_reduce(bmax[:, hd].rearrange("p g n -> p (g n)"), x, AX.X, ALU.max
                                            ).then_inc(reduced, 1)
                            e.tensor_reduce(bsum[BLK:P, hd], x[BLK:P, NBLK:NBLK + 3, :], AX.X, ALU.add
                                            ).then_inc(reduced, 1)

                        def query_side(j):
                            until(e, reduced, (j + 1) * HEADS * 2)
                            hb = lambda x: x[BLK:P]
                            s.chain(e.tensor_reduce(hb(least), hb(bsum), AX.X, ALU.min))
                            s.chain(e.tensor_tensor(hb(same), hb(bsum), hb(least).unsqueeze(2).to_broadcast(
                                [BLK, HEADS, 3]), ALU.is_equal))
                            s.step(e.tensor_scalar(drop[BLK:P, :, 1, 2], same[BLK:P, :, 2], NEG, None, ALU.mult))
                            s.chain(e.tensor_scalar(hb(other), same[BLK:P, :, 2], -1.0, 1.0, ALU.mult, ALU.add))
                            s.chain(e.tensor_tensor(hb(least), hb(other), same[BLK:P, :, 1], ALU.mult))
                            s.step(e.tensor_scalar(drop[BLK:P, :, 1, 1], hb(least), NEG, None, ALU.mult))
                            s.chain(e.tensor_tensor(hb(other), hb(other), hb(least), ALU.subtract))
                            s.chain(e.tensor_scalar(drop[BLK:P, :, 1, 0], hb(other), NEG, None, ALU.mult))
                            s.chain(e.tensor_tensor(masked[:], bmax[:], drop[:], ALU.add))
                            s.chain(e.tensor_reduce(top[:], masked[:], AX.X, ALU.max))
                            s.chain(e.tensor_scalar(negm[:], top[:], -1.0, None, ALU.mult))
                            until(e, qsT_psum, j)
                            part = lambda n: qside[:, :, :, n].rearrange("p g h -> p h g")
                            e.tensor_copy(qside[:, :, :, 0:NBLK].rearrange("p g h n -> p h g n"), drop[:]
                                          ).then_inc(qs_ready, 1)
                            e.tensor_copy(part(4), negm[:]).then_inc(qs_ready, 1)
                            until(e, qs_ready, j * 4 + 2)
                            s.chain(e.tensor_tensor(nr[:], negm[:], part(4), ALU.subtract))
                            e.tensor_copy(part(5), nr[:]).then_inc(qs_ready, 1)
                            until(e, qs_ready, j * 4 + 3)
                            e.tensor_tensor(part(6), nr[:], part(5), ALU.subtract).then_inc(qs_ready, 1)

                        def qsideT_out(j):
                            until(e, qsT_psum, j + 1)
                            until(e, s2_psum, j * HEADS)
                            e.tensor_copy(qsideT[:, :], QSPS[0:SL, 0:S]).then_inc(qsT_ready, 1)

                        def turn_denominators(j):
                            until(e, pv_done, (j + 1) * HG)
                            e.sem_inc(gone_on, 1)
                            half = 2 * S // 32
                            s.step(e.transpose(den[:, 0:half, :].rearrange("p n r -> p (n r)"), OPS[:, 0, :]))
                            s.step(e.transpose(den[:, half:NS, :].rearrange("p n r -> p (n r)"), OPS[:, 1, 0:S]))

                        def invert(j):
                            until(e, attn_ready, j * 2)
                            s.wait()
                            s.chain(e.reciprocal(rden[:, :], den[:, :, HD]))
                            e.sem_inc(gone_on, 1)
                            s.step(e.transpose(rec[:].rearrange("p n t -> p (n t)"),
                                               rden[:, :].unsqueeze(2).to_broadcast([P, NS, 32])))

                        def divide(j):
                            until(e, out_psum, j)
                            s.wait()
                            e.tensor_tensor(attnT[:, 0:2, :], OPS[:, 0, :].rearrange("p (n t) -> p n t", n=2),
                                            rec[:, 0:2, :], ALU.mult).then_inc(attn_ready, 1)
                            e.tensor_tensor(attnT[:, 2, :], OPS[:, 1, 0:S], rec[:, 2, :], ALU.mult
                                            ).then_inc(attn_ready, 1)

                        def add_h(j):
                            until(e, out_psum, j + 1)
                            hh = h[:, bass.ds(j * G, G), :]
                            e.tensor_tensor(hh, MISC[:, 0:G * D].rearrange("p (g d) -> p g d", g=G), hh,
                                            ALU.add).then_inc(h_ready, 1)
                            until(e, h_ready, j + 1)
                            for g in range(G):
                                row_stats(e, j * G + g)

                        def body(i, p, there):
                            for hd in range(HEADS):
                                if there(1):
                                    reduce_blocks(i + 1, hd)
                                if there(-1) and hd == 2:
                                    divide(i - 1)
                                if there(-1) and hd == 9:
                                    add_h(i - 1)
                                if there(2) and hd == 1:
                                    rest(i + 2)
                                if there(4) and hd == 6:
                                    norm(i + 4)
                                if there(2) and hd == 6:
                                    fill_slots(i + 2)
                            if there(1):
                                query_side(i + 1)
                            if there(2):
                                slotsT_out(i + 2, p, 1)
                            if there(3):
                                rotate(i + 3)
                            if there(2):
                                slotsT_out(i + 2, p, 3)
                            if there(1):
                                qsideT_out(i + 1)
                            if there(0):
                                turn_denominators(i)
                            if there(2):
                                slotsT_out(i + 2, p, 5)
                            if there(0):
                                invert(i)

                        e.wait_ge(load, 128)
                        e.wait_ge(filled, 3)
                        run(e, body, (s, 2 * 16))

        def route(name, layer, logits, at, weight, eid, w):
            with ExitStack() as ctx:
                sb = lambda n, *x: sb_in(ctx, name + n, *x)
                score, sel, eq, top1, top2, both, tmp = (
                    sb(n, [P, T, E]) for n in ("score", "sel", "eq", "top1", "top2", "both", "tmp"))
                best, total, rtotal = (sb(n, [P, T]) for n in ("best", "total", "rtotal"))
                upper, ones = sb("upper", [P, P]), sb("ones", [P, P])
                percnt, upto_, before, overs = (sb(n, [P, E, T]) for n in ("percnt", "upto", "before", "overs"))
                ntile, end, base = (sb(n, [P, E]) for n in ("ntile", "end", "base"))
                passed, eidf = sb("passed", [P, XT, E]), sb("eidf", [P, XT])
                load, own, sm_in, sm_out, chosen, counted, filled = sem_in(
                    ctx, *(name + n for n in ("_rt_load", "_rt_step", "_rt_act_in", "_rt_act_out", "_rt_chosen",
                                              "_rt_counted", "_rt_filled")))
                rt = w["tables"]
                rev, first, tiles, keep = (rt[:, x] for x in (RT_REV, RT_FIRST, RT_TILES, RT_KEEP))
                over = lambda ap: ap.unsqueeze(2).to_broadcast([P, T, E])
                with nc.Block() as block:
                    @block.sync
                    def _(e):
                        e.dma_start(upper[:, :], a["c_upper"]).then_inc(load, 16)

                    @block.gpsimd
                    def _(e):
                        e.memset(ones[:, :], 1.0).then_inc(filled, 1)

                    @block.scalar
                    def _(e):
                        if layer == 0:
                            e.activation(score[:, :, :], logits[:, :, :], ACT.Sigmoid).then_inc(sm_out, 1)
                        else:
                            e.wait_ge(sm_in, 1)
                            e.activation(sel[:, :, :], tmp[:, :, :], ACT.Exp).then_inc(sm_out, 1)

                    @block.tensor
                    def _(e):
                        e.wait_ge(load, 16)
                        e.wait_ge(filled, 1)
                        e.wait_ge(chosen, 1)
                        flat = both[:, :, :].rearrange("p t e -> p (t e)")
                        e.matmul(ps(0)[:, 0:T * E], upper[:, :], flat, start=True, stop=True)
                        e.matmul(ps(1)[:, 0:T * E], ones[:, :], flat, start=True, stop=True).then_inc(counted, 1)

                    @block.vector
                    def _(e):
                        s = Own(e, own)
                        if layer == 0:
                            e.wait_ge(sm_out, 1)
                            s.chain(e.tensor_tensor(sel[:, :, :], score[:, :, :],
                                                    w["balance"][:, :].unsqueeze(1).to_broadcast([P, T, E]), ALU.add))
                        else:
                            s.chain(e.tensor_reduce(best[:, :], logits[:, :, :], AX.X, ALU.max))
                            e.tensor_tensor(tmp[:, :, :], logits[:, :, :], over(best[:, :]), ALU.subtract
                                            ).then_inc(sm_in, 1)
                            e.wait_ge(sm_out, 1)
                            s.chain(e.tensor_reduce(total[:, :], sel[:, :, :], AX.X, ALU.add))
                            s.chain(e.reciprocal(rtotal[:, :], total[:, :]))
                            s.chain(e.tensor_tensor(score[:, :, :], sel[:, :, :], over(rtotal[:, :]), ALU.mult))
                            s.chain(e.tensor_copy(sel[:, :, :], score[:, :, :]))
                        for n, top in enumerate((top1, top2)):
                            s.chain(e.tensor_reduce(best[:, :], sel[:, :, :], AX.X, ALU.max))
                            s.chain(e.tensor_tensor(eq[:, :, :], sel[:, :, :], over(best[:, :]), ALU.is_equal))
                            s.chain(e.tensor_tensor(eq[:, :, :], eq[:, :, :],
                                                    rev.unsqueeze(1).to_broadcast([P, T, E]), ALU.mult))
                            s.chain(e.tensor_reduce(best[:, :], eq[:, :, :], AX.X, ALU.max))
                            s.chain(e.tensor_tensor(top[:, :, :], eq[:, :, :], over(best[:, :]), ALU.is_equal))
                            if n == 0:
                                s.chain(e.scalar_tensor_tensor(sel[:, :, :], top[:, :, :], NEG, sel[:, :, :],
                                                               ALU.mult, ALU.add))
                        s.step(e.tensor_tensor(tmp[:, :, :], top1[:, :, :], score[:, :, :], ALU.mult))
                        s.chain(e.tensor_tensor(eq[:, :, :], top2[:, :, :], score[:, :, :], ALU.mult))
                        e.tensor_tensor(both[:, :, :], top1[:, :, :], top2[:, :, :], ALU.add).then_inc(chosen, 1)
                        s.step(e.tensor_reduce(weight[:, :, 0], tmp[:, :, :], AX.X, ALU.add))
                        s.chain(e.tensor_reduce(weight[:, :, 1], eq[:, :, :], AX.X, ALU.add))
                        s.chain(e.tensor_tensor(total[:, :], weight[:, :, 0], weight[:, :, 1], ALU.add))
                        if layer == 0:
                            s.chain(e.tensor_scalar(total[:, :], total[:, :], 1e-20, None, ALU.add))
                        s.chain(e.reciprocal(rtotal[:, :], total[:, :]))
                        s.step(e.tensor_tensor(weight[:, :, 0], weight[:, :, 0], rtotal[:, :], ALU.mult))
                        s.step(e.tensor_tensor(weight[:, :, 1], weight[:, :, 1], rtotal[:, :], ALU.mult))
                        e.wait_ge(counted, 1)
                        s.chain(e.tensor_copy(percnt[:, :, :], ps(1)[:, 0:T * E].rearrange("p (t e) -> p e t", e=E)))
                        flat = lambda x: x[:, :, :].rearrange("p e t -> p (e t)")
                        s.chain(e.tensor_tensor_scan(flat(upto_), keep, flat(percnt), 0.0, ALU.mult, ALU.add))
                        s.step(e.tensor_tensor(before[:, :, :], upto_[:, :, :], percnt[:, :, :], ALU.subtract))
                        s.chain(e.tensor_tensor(overs[:, :, :], first.unsqueeze(1).to_broadcast([P, E, T]),
                                                upto_[:, :, T - 1:T].to_broadcast([P, E, T]), ALU.is_lt))
                        s.chain(e.tensor_reduce(ntile[:, :], overs[:, :, :], AX.X, ALU.add))
                        s.chain(e.tensor_tensor_scan(end[:, :], keep[:, 1:1 + E], ntile[:, :], 0.0, ALU.mult, ALU.add))
                        s.chain(e.tensor_tensor(base[:, :], end[:, :], ntile[:, :], ALU.subtract))
                        s.chain(e.tensor_scalar(base[:, :], base[:, :], float(P), None, ALU.mult))
                        s.chain(e.tensor_tensor(before[:, :, :], before[:, :, :],
                                                base[:, :].unsqueeze(2).to_broadcast([P, E, T]), ALU.add))
                        s.chain(e.tensor_tensor(tmp[:, :, :], ps(0)[:, 0:T * E].rearrange("p (t e) -> p t e", e=E),
                                                before[:, :, :].rearrange("p e t -> p t e"), ALU.add))
                        for n, top in enumerate((top1, top2)):
                            s.chain(e.tensor_tensor(eq[:, :, :], tmp[:, :, :], top[:, :, :], ALU.mult))
                            s.chain(e.tensor_reduce(at[:, :, n], eq[:, :, :], AX.X, ALU.add))
                        s.chain(e.tensor_tensor(passed[:, :, :], end[:, :].unsqueeze(1).to_broadcast([P, XT, E]),
                                                tiles.unsqueeze(2).to_broadcast([P, XT, E]), ALU.is_le))
                        s.chain(e.tensor_reduce(eidf[:, :], passed[:, :, :], AX.X, ALU.add))
                        s.chain(e.tensor_scalar(eid[:, :], eidf[:, :], float(E - 1), None, ALU.min))

        def invert_slots(name, at, ends, rt):
            N, CH = 2 * T, 16
            with ExitStack() as ctx:
                sb = lambda n, *x: sb_in(ctx, f"{name}_{n}", *x)
                ati, low = sb("ati", [P, N], I32), sb("low", [P, N], I32)
                row, tile = sb("row", [P, N]), sb("tile", [P, N])
                rows = [sb(f"rows{n}", [P, CH, P], BF16) for n in range(2)]
                hot = [sb(f"hot{n}", [P, CH, XT], BF16) for n in range(2)]
                carried = [sb(f"carried{n}", [P, CH, 2, XT], BF16) for n in range(2)]
                place, dest, full, src, beyond = (sb(n, [P, XT]) for n in ("place", "dest", "full", "src", "beyond"))
                hot_ready, numbered, chunk_ready, used, own = sem_in(
                    ctx, *(f"{name}_{n}" for n in ("tiles_ready", "numbered", "chunk_ready", "chunk_used", "step")))
                tiles, r128, number, no_token, part = (
                    rt[:, x] for x in (RT_TILES, RT_ROW, RT_NUMBER, RT_NO_TOKEN, RT_PART))
                with nc.Block() as block:
                    def cut(x, c, width):
                        return x[:, c * CH:(c + 1) * CH].unsqueeze(2).to_broadcast([P, CH, width])

                    @block.vector
                    def _(e):
                        s = Own(e, own)
                        s.chain(e.tensor_copy(ati[:, :], at[:, :, :].rearrange("p t n -> p (t n)")))
                        s.chain(e.tensor_scalar(low[:, :], ati[:, :], 7, None, ALU.arith_shift_right))
                        s.step(e.tensor_copy(tile[:, :], low[:, :]))
                        s.chain(e.tensor_scalar(ati[:, :], ati[:, :], P - 1, None, ALU.bitwise_and))
                        s.chain(e.tensor_copy(row[:, :], ati[:, :]))
                        for c in range(N // CH):
                            b = c % 2
                            if c >= 2:
                                e.wait_ge(used, c - 1)
                                e.wait_ge(numbered, c - 1)
                            e.tensor_tensor(hot[b][:], tiles.unsqueeze(1).to_broadcast([P, CH, XT]),
                                            cut(tile, c, XT), ALU.is_equal).then_inc(hot_ready, 1)
                            e.tensor_tensor(rows[b][:], r128.unsqueeze(1).to_broadcast([P, CH, P]), cut(row, c, P),
                                            ALU.is_equal).then_inc(chunk_ready, 1)
                            e.wait_ge(hot_ready, c + 1)
                            e.tensor_scalar(carried[b][:, :, 1, :], hot[b][:], part, None, ALU.mult
                                            ).then_inc(chunk_ready, 1)
                        e.wait_ge(used, N // CH)
                        number_at, place_at = ps(0)[:, 0:XT], ps(0)[:, XT:2 * XT]
                        s.step(e.tensor_scalar(dest[:, :], number_at, -1.0, float(P), ALU.add, ALU.mult))
                        s.step(e.tensor_scalar(full[:, :], number_at, 0.0, None, ALU.is_equal))
                        s.chain(e.tensor_copy(place[:, :], place_at))
                        s.step(e.tensor_tensor(full[:, :], full[:, :], no_token, ALU.mult))
                        s.chain(e.tensor_tensor(dest[:, :], dest[:, :], place[:, :], ALU.add))
                        s.step(e.tensor_scalar(beyond[:, :], dest[:, :], float(T * P), float(-T * P), ALU.is_ge, ALU.mult))
                        s.chain(e.tensor_scalar(src[:, :], dest[:, :], 0.0, None, ALU.max))
                        s.step(e.tensor_tensor(ends[:, :, 0], src[:, :], beyond[:, :], ALU.add))
                        s.step(e.tensor_tensor(ends[:, :, 1], dest[:, :], full[:, :], ALU.add))

                    @block.gpsimd
                    def _(e):
                        for c in range(N // CH):
                            e.wait_ge(hot_ready, c + 1)
                            if c >= 2:
                                e.wait_ge(used, c - 1)
                            e.tensor_tensor(carried[c % 2][:, :, 0, :], hot[c % 2][:], cut(number, c, XT), ALU.mult
                                            ).then_inc(numbered, 1)

                    @block.tensor
                    def _(e):
                        for c in range(N // CH):
                            e.wait_ge(chunk_ready, (c + 1) * 2)
                            e.wait_ge(numbered, c + 1)
                            for n in range(CH):
                                m = e.matmul(ps(0)[:, 0:2 * XT], rows[c % 2][:, n, :],
                                             carried[c % 2][:, n].rearrange("p two s -> p (two s)"),
                                             start=(c == 0 and n == 0), stop=(c == N // CH - 1 and n == CH - 1))
                            m.then_inc(used, 1)

        def combine(name, layer, weight):
            U, Q = 3, 4
            with ExitStack() as ctx:
                got = [sb_in(ctx, f"{name}_got{u}", [P, 2, Q, D]) for u in range(U)]
                half, taken = sem_in(ctx, name + "_half", name + "_taken")
                here = [sem_in(ctx, f"{name}_here{u}") for u in range(U)]
                last = layer == 1
                rows = y_rows[layer][0:2 * T * P].rearrange("(n t p) d -> p n t d", n=2, p=P)
                with nc.Block() as block:
                    @block.sync
                    def _(e):
                        for q in range(T // Q):
                            if q >= U:
                                e.wait_ge(taken, (q - U + 1) * Q)
                            for n in range(2):
                                e.dma_start(got[q % U][:, n], rows[:, n, q * Q:(q + 1) * Q]).then_inc(here[q % U], 16)

                    if last:
                        @block.scalar
                        def _(e):
                            rows_out = out.rearrange("b (g p) d -> p (b g) d", p=P)
                            with e.Fori(0, T // Q) as i:
                                e.wait_ge(taken, i * Q + Q)
                                e.dma_start(rows_out[:, bass.ds(i * Q, Q), :], h[:, bass.ds(i * Q, Q), :]
                                            ).then_inc(stored, 16)
                            e.wait_ge(stored, 16 * (T // Q))

                    @block.vector
                    def _(e):
                        def add(t, n, done):
                            q, k = t // Q, t % Q
                            return e.scalar_tensor_tensor(h[:, t, :], got[q % U][:, n, k], weight[:, t, n:n + 1],
                                                          h[:, t, :], ALU.mult, ALU.add).then_inc(done, 1)

                        for t in range(T + 2):
                            if t < T:
                                if t % Q == 0:
                                    e.wait_ge(here[t // Q % U], (t // Q // U + 1) * 32)
                                add(t, 0, half)
                            if 1 <= t <= T:
                                e.wait_ge(half, t)
                                add(t - 1, 1, taken)
                            if t >= 2 and not last:
                                e.wait_ge(taken, t - 1)
                                row_stats(e, t - 2)

        def experts(name, layer, eid, ends, w, w2_load):
            w1, w2, bias2 = w["w1"], w["w2"], w.get("bias2")
            U, AHEAD = 8, 5
            H = D if layer == 0 else HID
            HC = H // (K if layer == 0 else P)
            HK = H // HC
            with ExitStack() as ctx:
                xg = [sb_in(ctx, f"{name}_xg{u}", [P, D]) for u in range(U)]
                yo = [sb_in(ctx, f"{name}_yo{u}", [P, D]) for u in range(U)]
                xT = sb_in(ctx, name + "_xT", [K + 1, C, P])
                pos_part = [sb_in(ctx, f"{name}_relu{n}", [P, D]) for n in range(2)]
                hid = [sb_in(ctx, f"{name}_hid{n}", [P, H]) for n in range(2)]
                hidT = sb_in(ctx, name + "_hidT", [HK, HC, P])
                loaded = [sem_in(top, f"{name}_loaded{u}") for u in range(U)]
                put = [sem_in(top, f"{name}_put{u}") for u in range(U)]
                source = [sb_in(ctx, f"{name}_source{u}", [P, 1], I32) for u in range(U)]
                goal = [sb_in(ctx, f"{name}_goal{u}", [P, 1], I32) for u in range(U)]
                source_ready, goal_ready, gone_on = sem_in(ctx, name + "_source_ready", name + "_goal_ready",
                                                           name + "_gone_on")
                (xT_psum, xT_ready, hid_psum, relu_ready, hid_ready, hT_psum, hT_ready, y_psum, y_ready, ones) = sem_in(
                    ctx, *(name + n for n in ("_xT_in_psum", "_xT_ready", "_hidden_in_psum", "_relu_ready",
                                              "_hidden_ready", "_hiddenT_in_psum", "_hiddenT_ready", "_y_in_psum",
                                              "_y_ready", "_ones_row")))
                XPS, HPS, TPS, YPS = ps(0), bank[1], bank[2], ps(1)
                HN = H if layer == 0 else H // 2
                ROUNDS = (XT - 3) // U
                with nc.Block() as block:
                    @block.gpsimd
                    def _(e):
                        def fetch(s, u):
                            if not isinstance(s, int) or s >= U:
                                e.wait_ge(xT_psum, s - U + 1)
                            e.wait_ge(source_ready, s + 1)
                            e.sem_inc(gone_on, 1)
                            e.indirect_dma_start(xg[u][:, :], None, x_rows[layer], bass.IndirectOffsetOnAxis(
                                source[u][:, :].bitcast(U32), 0)).then_inc(loaded[u], 16)

                        def store(s, u):
                            e.wait_ge(y_ready, s + 1)
                            e.wait_ge(goal_ready, s + 1)
                            e.sem_inc(gone_on, 1)
                            e.indirect_dma_start(y_rows[layer], bass.IndirectOffsetOnAxis(
                                goal[u][:, :].bitcast(U32), 0), yo[u][:, :], None).then_inc(put[u], 16)

                        e.memset(xT[K:K + 1, :, :], 1.0).then_inc(ones, 1)
                        for s in range(AHEAD):
                            fetch(s, s)
                        for s in range(U):
                            fetch(s + AHEAD, (s + AHEAD) % U)
                            store(s, s)
                        with e.Fori(1, XT // U - 1) as i:
                            for u in range(U):
                                fetch(i * U + u + AHEAD, (u + AHEAD) % U)
                                store(i * U + u, u)
                        for s in range(XT - U, XT):
                            if s + AHEAD < XT:
                                fetch(s + AHEAD, (s + AHEAD) % U)
                            store(s, s % U)
                        for u in range(U):
                            e.wait_ge(put[u], XT // U * 16)

                    @block.tensor
                    def _(e):
                        def turn_x(s, u, n):
                            e.wait_ge(loaded[u], n)
                            e.wait_ge(xT_ready, s)
                            for c in range(C):
                                m = e.transpose(XPS[0:K, c * P:(c + 1) * P], xg[u][:, c * K:(c + 1) * K], ident[:, :])
                            m.then_inc(xT_psum, 1)

                        def up(s, q, ex):
                            e.wait_ge(xT_ready, s + 1)
                            until(e, hid_ready, s if layer else s - 1)
                            for n in range(H // HN):
                                for c in range(C):
                                    kk = K + (c if layer else 0)
                                    m = e.matmul(HPS[:, n if layer else q, 0:HN], xT[0:kk, c, :],
                                                 w1[0:kk, ex, c, n * HN:(n + 1) * HN],
                                                 start=(c == 0), stop=(c == C - 1))
                            m.then_inc(hid_psum, 1)

                        def turn_hidden(s, q):
                            e.wait_ge(hid_ready, s + 1)
                            until(e, hT_ready, s)
                            for c in range(HC):
                                m = e.transpose(TPS[0:HK, c // 4, c % 4 * P:(c % 4 + 1) * P],
                                                hid[q][:, c * HK:(c + 1) * HK], ident[:, :])
                            m.then_inc(hT_psum, 1)

                        def down(s, ex):
                            e.wait_ge(hT_ready, s + 1)
                            e.wait_ge(y_ready, s)
                            for c in range(HC):
                                m = e.matmul(YPS[:, 0:D], hidT[:, c, :], w2[0:HK, ex, c, :],
                                             start=(c == 0), stop=(c == HC - 1))
                            m.then_inc(y_psum, 1)

                        def expert(s):
                            return e.value_load(eid[0:1, bass.ds(s, 1)], min_val=0, max_val=E - 1)

                        if layer:
                            e.wait_ge(w2_load, 16)
                        e.wait_ge(ones, 1)
                        turn_x(0, 0, 16)

                        def body(s, j, r, ex):
                            there = lambda n: not isinstance(s, int) or 0 <= s + n < XT
                            if there(0):
                                ex.append(expert(s))
                                up(s, j % 2, ex[-1])
                            if there(1):
                                turn_x(s + 1, (j + 1) % U, (r + 1) * 16)
                            if there(-2):
                                down(s - 2, ex.pop(0))
                            if there(-1):
                                turn_hidden(s - 1, (j + 1) % 2)

                        ex = []
                        for s in range(2):
                            body(s, s, 0, ex)
                        with e.Fori(0, ROUNDS) as i:
                            ex = [expert(i * U), expert(i * U + 1)]
                            for j in range(2, U + 2):
                                body(i * U + j, j % U, i + (j + 1) // U, ex)
                        ex = [expert(ROUNDS * U), expert(ROUNDS * U + 1)]
                        for s in range(2 + ROUNDS * U, XT + 2):
                            body(s, s % U, (s + 1) // U, ex)

                    @block.scalar
                    def _(e):
                        def xT_out(s):
                            e.wait_ge(xT_psum, s + 1)
                            e.wait_ge(hid_psum, s)
                            e.activation(xT[0:K, :, :], XPS[0:K, 0:C * P].rearrange("p (c t) -> p c t", c=C),
                                         ACT.Copy).then_inc(xT_ready, 1)

                        def hid_out(s, q):
                            e.wait_ge(hid_psum, s + 1)
                            if layer == 0:
                                until(e, hid_ready, s - 1)
                                e.activation(pos_part[q][:, :], HPS[:, q, 0:D], ACT.Relu).then_inc(relu_ready, 1)
                            else:
                                until(e, hT_psum, s - 1)
                                e.activation(hid[q][:, :].rearrange("p (n f) -> p n f", n=2), HPS[:, :, 0:HN],
                                             ACT.Gelu_apprx_tanh).then_inc(hid_ready, 1)

                        def index(of, n, s, u, done, times, ready):
                            until(e, done[u], times * 16)
                            e.activation(of[u][:, :], ends[:, s, n:n + 1], ACT.Identity).then_inc(ready, 1)

                        AT = AHEAD + 1
                        for s in range(AT):
                            index(source, 0, s, s, loaded, 0, source_ready)
                        if layer == 0:
                            xT_out(0)
                        def body(s, u, r):
                            hid_out(s, u % 2)
                            more = lambda n: not isinstance(s, int) or s + n < XT
                            if layer == 0 and more(1):
                                xT_out(s + 1)
                            if more(AT):
                                index(source, 0, s + AT, (u + AT) % U, loaded, r + (u + AT) // U, source_ready)
                            index(goal, 1, s, u, put, r, goal_ready)

                        for s in range(U):
                            body(s, s, 0)
                        with e.Fori(1, XT // U - 1) as i:
                            for u in range(U):
                                body(i * U + u, u, i)
                        for s in range(XT - U, XT):
                            body(s, s % U, s // U)

                    @block.vector
                    def _(e):
                        def xT_out(s):
                            e.wait_ge(xT_psum, s + 1)
                            e.wait_ge(hid_psum, s)
                            e.tensor_copy(xT[0:K, :, :], XPS[0:K, 0:C * P].rearrange("p (c t) -> p c t", c=C)
                                          ).then_inc(xT_ready, 1)

                        def squares(s, q):
                            e.wait_ge(relu_ready, s + 1)
                            until(e, hT_psum, s - 1)
                            e.tensor_tensor(hid[q][:, :], HPS[:, q, 0:D], pos_part[q][:, :], ALU.mult
                                            ).then_inc(hid_ready, 1)

                        def hT_out(s):
                            e.wait_ge(hT_psum, s + 1)
                            until(e, y_psum, s)
                            if layer == 0:
                                e.tensor_copy(hidT[:, :, :], TPS[0:HK, 0, 0:HC * P].rearrange("p (c t) -> p c t", c=HC)
                                              ).then_inc(hT_ready, 1)
                            else:
                                e.tensor_copy(hidT[:, 0:4, :], TPS[:, 0, :].rearrange("p (c t) -> p c t", c=4))
                                e.tensor_copy(hidT[:, 4:6, :], TPS[:, 1, 0:2 * P].rearrange("p (c t) -> p c t", c=2)
                                              ).then_inc(hT_ready, 1)

                        def y_out(s, u, n):
                            e.wait_ge(y_psum, s + 1)
                            until(e, put[u], n)
                            if layer == 0:
                                e.tensor_copy(yo[u][:, :], YPS[:, 0:D]).then_inc(y_ready, 1)
                            else:
                                ex = e.value_load(eid[0:1, bass.ds(s, 1)], min_val=0, max_val=E - 1)
                                e.tensor_tensor(yo[u][:, :], YPS[:, 0:D], bias2[:, ex, :], ALU.add).then_inc(y_ready, 1)

                        if layer:
                            xT_out(0)

                        def body(s, j, stores):
                            if layer == 0 and (not isinstance(s, int) or s < XT):
                                squares(s, j % 2)
                            if layer and (not isinstance(s, int) or s + 1 < XT):
                                xT_out(s + 1)
                            if not isinstance(s, int) or s >= 2:
                                y_out(s - 2, (j - 2) % U, stores)
                            if not isinstance(s, int) or 1 <= s <= XT:
                                hT_out(s - 1)

                        for s in range(2):
                            body(s, s, 0)
                        with e.Fori(0, ROUNDS) as i:
                            for j in range(U):
                                body(i * U + 2 + j, (2 + j) % U, i * 16)
                        for s in range(2 + ROUNDS * U, XT + 2):
                            body(s, s % U, (s - 2) // U * 16)

        def moe_weights(ctx, layer):
            name = f"moe{layer}"
            sb = lambda n, *x: sb_in(ctx, f"{name}_{n}", *x)
            w = dict(w1=sb("w1", [K + 1, E, C, D if layer == 0 else HID]), router=sb("router", [K + 1, C, E]),
                     tables=sb("tables", [P, RT]))
            loads = [(w["router"][0:K, :, :], a[f"router{layer}"]), (w["tables"][:, :], a["c_route"]),
                     (w["w1"][0:K, :, :, :], a[f"w1_{layer}"])]
            if layer == 0:
                w.update(w2=sb("w2", [K, E, C, D]), wfc=sb("wfc", [K, C, D]), wproj=sb("wproj", [K, C, D]),
                         balance=sb("balance", [P, E]))
                loads += [(w["router"][K:K + 1, :, :], a["no_bias"]), (w["w2"][:, :, :, :], a["w2_0"]),
                          (w["wfc"][:, :, :], a["w_fc_sh"]), (w["wproj"][:, :, :], a["w_proj_sh"]),
                          (w["balance"][:, :], a["balance"].partition_broadcast(P))]
            else:
                w.update(bias2=sb("bias2", [P, E, D]))
                loads += [(w["router"][K:K + 1, 0, :], a["br"]), (w["router"][K:K + 1, 1, :], a["br"]),
                          (w["w1"][K:K + 1, :, 1, :], a["bfc"]),
                          (w["bias2"][:, :, :], a["bproj"].partition_broadcast(P))]
            w["sem"] = sem_in(top, f"{name}_weights_loaded")
            w["count"] = 16 * len(loads)
            return w, [(dst, src, w["sem"]) for dst, src in loads]

        def moe(layer, w):
            name = f"moe{layer}"
            with ExitStack() as ctx:
                sb = lambda n, *x: sb_in(ctx, f"{name}_{n}", *x)
                weight = sb("weight", [P, T, 2])
                eid = sb("eid", [P, XT], I32)
                ends = sb("ends", [P, XT, 2], I32)
                if layer:
                    w["w2"] = sb("w2", [P, E, HT, D])
                w2_load = sem_in(ctx, name + "_w2_loaded")
                with ExitStack() as c1:
                    at = sb_in(c1, name + "_at", [P, T, 2])
                    with ExitStack() as c2:
                        logits = sb_in(c2, name + "_logits", [P, T, E])
                        moe_pre(name, layer, logits, w, w2_load)
                        route(name, layer, logits, at, weight, eid, w)
                    invert_slots(name + "_slots", at, ends, w["tables"])
                experts(name + "_experts", layer, eid, ends, w, w2_load)
                combine(name + "_combine", layer, weight)

        def moe_pre(name, layer, logits, w, w2_load):
            U = 4
            ROUNDS = (B - 4) // U
            with ExitStack() as ctx:
                sb = lambda n, *x: sb_in(ctx, f"{name}_{n}", *x)
                ln = ln_tensors(ctx, name)
                router = w["router"]
                xn = [sb(f"xn{n}", [P, G, D]) for n in range(U)]
                xT = [sb(f"xT{n}", [K + 1, C, S]) for n in range(2)]
                if layer == 0:
                    wfc, wproj = w["wfc"], w["wproj"]
                    relu, hT = ([sb(f"{n}{q}", [K, C, S]) for q in range(2)] for n in ("relu", "hT"))
                (ones, xn_ready, xT_psum, xT_ready, l_psum, l_ready, hid_psum, relu_ready, hT_ready, o_psum,
                 o_ready) = sem_in(ctx, *(f"{name}_{n}" for n in (
                     "pre_ones", "xn_ready", "xT_in_psum", "xT_ready", "logits_in_psum", "logits_ready",
                     "shared_in_psum", "shared_relu", "shared_hT_ready", "shared_out_in_psum", "shared_added")))
                kept = [sem_in(ctx, f"{name}_x_rows_stored{u}") for u in range(U)]
                TURNED, LPS, HPS, OPS = ((ps(n), ps(n + 4)) for n in range(4))

                def steps(e, body):
                    def static(i):
                        body(i, i % U, i // U, lambda ahead: 0 <= i + ahead < B)

                    for i in range(2):
                        static(i)
                    with e.Fori(0, ROUNDS) as r:
                        for u in range(2, U + 2):
                            body(r * U + u, u % U, r + u // U, lambda ahead: True)
                    for i in range(ROUNDS * U + 2, B + 1):
                        static(i)

                with nc.Block() as block:
                    @block.sync
                    def _(e):
                        rows = x_rows[layer].rearrange("(t p) d -> p t d", p=P)
                        with e.Fori(0, B // U) as i:
                            for u in range(U):
                                e.wait_ge(xn_ready, (i * U + u + 1) * G)
                                e.dma_start(rows[:, bass.ds((i * U + u) * G, G), :], xn[u][:, :, :]
                                            ).then_inc(kept[u], 16)
                        if layer:
                            e.dma_start(w["w2"][:, :, :, :], a["w2_1"]).then_inc(w2_load, 16)
                        for u in range(U):
                            e.wait_ge(kept[u], B // U * 16)

                    @block.gpsimd
                    def _(e):
                        for n in range(2):
                            e.memset(xT[n][K:K + 1, :, :], 1.0).then_inc(ones, 1)
                        if layer == 0:
                            e.wait_ge(ones, 2)

                            def body(i, u, r, there):
                                if there(0):
                                    q = u % 2
                                    e.wait_ge(relu_ready, i + 1)
                                    until(e, o_psum, i - 1)
                                    e.tensor_tensor(hT[q][:, :, :], relu[q][:, :, :], relu[q][:, :, :], ALU.mult
                                                    ).then_inc(hT_ready, 1)

                            steps(e, body)

                    @block.tensor
                    def _(e):
                        def turn_x(j, u):
                            e.wait_ge(xn_ready, (j + 1) * G)
                            until(e, xT_ready, j - 1)
                            turn(e, TURNED[u % 2], xn[u]).then_inc(xT_psum, 1)

                        def logit(j, u):
                            e.wait_ge(xT_ready, j + 1)
                            until(e, l_ready, j - 1)
                            for g in range(G):
                                for c in range(C):
                                    kk = K + c
                                    m = e.matmul(LPS[u % 2][:, g * E:(g + 1) * E], xT[u % 2][0:kk, c, g * P:(g + 1) * P],
                                                 router[0:kk, c, :], start=(c == 0), stop=(c == C - 1))
                            m.then_inc(l_psum, 1)

                        def hidden(j, u):
                            until(e, relu_ready, j - 1)
                            for n in range(C):
                                for c in range(C):
                                    m = e.matmul(HPS[u % 2][0:K, n * S:(n + 1) * S], wfc[:, c, n * K:(n + 1) * K],
                                                 xT[u % 2][0:K, c, :], start=(c == 0), stop=(c == C - 1))
                            m.then_inc(hid_psum, 1)

                        def shared_out(j, u):
                            e.wait_ge(hT_ready, j + 1)
                            until(e, o_ready, j - 1)
                            for g in range(G):
                                for c in range(C):
                                    m = e.matmul(OPS[u % 2][:, g * D:(g + 1) * D], hT[u % 2][:, c, g * P:(g + 1) * P],
                                                 wproj[:, c, :], start=(c == 0), stop=(c == C - 1))
                            m.then_inc(o_psum, 1)

                        def body(i, u, r, there):
                            if there(1):
                                turn_x(i + 1, (u + 1) % U)
                            if there(0):
                                logit(i, u)
                                if layer == 0:
                                    hidden(i, u)
                            if there(-1) and layer == 0:
                                shared_out(i - 1, (u - 1) % U)

                        e.wait_ge(w["sem"], w["count"])
                        e.wait_ge(ones, 2)
                        turn_x(0, 0)
                        steps(e, body)

                    @block.scalar
                    def _(e):
                        def xT_out(j, u):
                            e.wait_ge(xT_psum, j + 1)
                            until(e, l_psum, j - 1)
                            if layer == 0:
                                until(e, hid_psum, j - 1)
                            e.activation(xT[u % 2][0:K, :, :], TURNED[u % 2][0:K, :].rearrange("p (c t) -> p c t", c=C),
                                         ACT.Identity).then_inc(xT_ready, 1)

                        def relu_out(j, u):
                            e.wait_ge(hid_psum, j + 1)
                            until(e, hT_ready, j - 1)
                            e.activation(relu[u % 2][:, :, :], HPS[u % 2][0:K, :].rearrange("p (c t) -> p c t", c=C),
                                         ACT.Relu).then_inc(relu_ready, 1)

                        def body(i, u, r, there):
                            if there(1):
                                xT_out(i + 1, (u + 1) % U)
                            if there(0) and layer == 0:
                                relu_out(i, u)

                        root(e, ln)
                        xT_out(0, 0)
                        steps(e, body)

                    @block.vector
                    def _(e):
                        statistics(e, ln)

                        def norm(j, u, r):
                            until(e, xT_psum, j - U + 1)
                            until(e, kept[u], r * 16)
                            for g in range(G):
                                normalise(e, xn[u], j, g).then_inc(xn_ready, 1)

                        def logits_out(j, u):
                            e.wait_ge(l_psum, j + 1)
                            e.tensor_copy(logits[:, bass.ds(j * G, G), :], LPS[u % 2][:, 0:G * E].rearrange(
                                "p (g e) -> p g e", g=G)).then_inc(l_ready, 1)

                        def add_h(j, u):
                            e.wait_ge(o_psum, j + 1)
                            hh = h[:, bass.ds(j * G, G), :]
                            e.tensor_tensor(hh, OPS[u % 2][:, 0:G * D].rearrange("p (g d) -> p g d", g=G), hh,
                                            ALU.add).then_inc(o_ready, 1)

                        def body(i, u, r, there):
                            if there(2):
                                norm(i + 2, (u + 2) % U, r + (u + 2) // U)
                            if there(0):
                                logits_out(i, u)
                            if there(-1) and layer == 0:
                                add_h(i - 1, (u - 1) % U)

                        norm(0, 0, 0)
                        norm(1, 1, 0)
                        steps(e, body)

        with ExitStack() as weights0:
            w, loads = moe_weights(weights0, 0)
            hyena(loads)
            moe(0, w)
        nc.clear_and_free_semaphores(stage_sems)
        with nc.Block():
            pass
        w, loads = moe_weights(top, 1)
        attention(loads)
        moe(1, w)


def _chunks(w, rows=96):
    return w.reshape(-1, rows, w.shape[-1]).transpose(1, 0, 2)


def _experts(w, rows):
    return w.reshape(w.shape[0], -1, rows, w.shape[-1]).transpose(2, 0, 1, 3)


def _constants():
    import numpy as np
    c = {}
    f32 = np.float32
    c["c_ident"] = np.eye(128, dtype=f32)
    arg = (np.arange(256, dtype=f32)[:, None] * np.arange(64, dtype=f32)[None] / f32(64)).astype(np.float64)
    c["c_basis"] = np.concatenate([np.sin(arg).T, np.ones((1, 256))]).astype(f32)
    n = 384
    w = np.arange(192)
    t = np.arange(256)
    th = lambda k: 2 * np.pi * ((w[:, None] * k[None]) % n) / n
    alt = lambda k: np.where(k % 2 == 0, 1.0, -1.0)
    cos_, sin_ = np.cos(th(t)), np.sin(th(t))
    sin_[0] = alt(t)
    c["c_fwd"] = np.concatenate([cos_, sin_]).T.reshape(2, 128, 384).transpose(1, 0, 2).astype(f32)
    k = t - 128
    p, q = np.cos(th(k)), np.sin(th(k))
    r = -p.copy()
    r[0] = -alt(k)
    c["c_to_spec"] = np.concatenate([p, q, r]).T.reshape(2, 128, 576).transpose(1, 0, 2).astype(f32)
    two = np.where(w == 0, 1.0, 2.0)[:, None] / n
    ic, is_ = np.cos(th(t)) * two, -np.sin(th(t)) * two
    is_[0] = -alt(t) / n
    c["c_inv"] = np.concatenate([ic, is_]).reshape(4, 96, 256).transpose(1, 0, 2).astype(f32)
    keep = np.ones((8, 32))
    keep[:, 0] = 0
    number = np.arange(32)[:, None] + 32 * np.arange(2)[None] + 1
    common = np.concatenate([8 - np.arange(8), 128 * np.arange(32), np.arange(72), keep.ravel(), np.arange(128),
                             number.ravel()])
    part = np.arange(128)[:, None]
    no_token = 128 + 8192 + 128 * np.arange(72)[None] + part
    c["c_route"] = np.concatenate([np.tile(common[None], (128, 1)), no_token, part], 1).astype(f32)
    c["c_upper"] = np.triu(np.ones((128, 128)), 1).astype(f32)
    c["no_bias"] = np.zeros((1, 2, 8), f32)
    b16 = np.dtype("bfloat16")
    inv_freq = f32(1) / f32(10000) ** (np.arange(0, 16, 2, dtype=f32) / f32(16))
    ang = (np.arange(256, dtype=f32)[:, None] * inv_freq[None]).astype(f32).astype(np.float64)
    cs = np.stack([np.concatenate([np.cos(ang)] * 2, 1), np.concatenate([-np.sin(ang), np.sin(ang)], 1)], 1).astype(f32)
    c["c_rope"] = np.stack([cs * f32(0.25), cs], 1).reshape(2, 128, 2, 2, 16).transpose(1, 0, 2, 3, 4)
    c["c_identb"] = np.eye(128).astype(b16)
    q, k = np.arange(128)[:, None], np.arange(128)[None]
    causal = np.where((q // 64 == k // 64) & (k > q), -1e30, 0.0)
    c["c_causal"], c["c_causalT"] = causal.astype(b16), causal.T.astype(b16)
    key = np.zeros((12, 8, 12, 2, 128))
    for hd in range(12):
        for n in range(4):
            key[hd, n, hd] = (np.arange(256) // 64 == n).reshape(2, 128)
        key[hd, 4:7, hd] = 1
    c["c_keyside"] = key.reshape(96, 12, 2, 128).astype(b16)
    drop = np.zeros((128, 12, 2, 4))
    drop[:, :, 0, 3] = drop[:64, :, 1, 3] = -1e30
    c["c_drop"] = drop.astype(f32)
    return {k: np.ascontiguousarray(v) for k, v in c.items()}


def _arrays(i):
    import numpy as np
    i = {k: np.asarray(v) for k, v in i.items()}
    r = {}
    r["x"] = i["x"].transpose(2, 3, 0, 1).reshape(84 * 84, 48)
    r["curve"] = i["L0_tok_curve"]
    tw = np.zeros((49, 16, 192), np.float32)
    for b in range(16):
        tw[3 * b:3 * b + 3, b] = i["L0_tok_proj_w"].T
        tw[48, b] = i["L0_tok_proj_b"]
    r["tok_w"] = tw
    r["w_in"] = _chunks(i["L0_attn_w_in"])
    r["b_in"] = i["L0_attn_b_in"].reshape(1, 768)
    r["w_filt"] = i["L0_attn_w_filt"]
    r["b_filt"] = i["L0_attn_b_filt"].reshape(1, 192)
    r["short"] = np.concatenate([i["L0_attn_w_short"][:, 0, :], i["L0_attn_b_short"][:, None]], 1
                                ).reshape(2, 96, 4).transpose(1, 0, 2)
    r["w_out"] = _chunks(i["L0_attn_w_out"])
    r["b_out"] = i["L0_attn_b_out"].reshape(1, 192)
    r["router0"] = _chunks(i["L0_ffn_router_w"].T)
    r["balance"] = i["L0_ffn_balance_bias"]
    r["w_fc_sh"] = _chunks(i["L0_ffn_w_fc_sh"])
    r["w_proj_sh"] = _chunks(i["L0_ffn_w_proj_sh"])
    r["w1_0"] = _experts(i["L0_ffn_w1"], 96)
    r["w2_0"] = _experts(i["L0_ffn_w2"], 96)
    r["router1"] = _chunks(i["L1_ffn_Wr"])
    r["br"] = i["L1_ffn_br"].reshape(1, 8)
    r["w1_1"] = _experts(i["L1_ffn_Wfc"], 96)
    r["bfc"] = i["L1_ffn_bfc"].reshape(1, 8, 768)
    r["w2_1"] = _experts(i["L1_ffn_Wproj"], 128)
    r["bproj"] = i["L1_ffn_bproj"]
    r["wqkv"] = _chunks(np.concatenate([i["L1_attn_Wq"].T, i["L1_attn_Wk"].T, i["L1_attn_Wv"].T], 1))
    wo = np.zeros((3, 4, 32, 192), np.float32)
    wo[:, :, :16] = i["L1_attn_Wo"].T.reshape(3, 4, 16, 192)
    r["wo"] = wo.reshape(3, 128, 192).transpose(1, 0, 2)
    r.update(_constants())
    return {k: np.ascontiguousarray(v) for k, v in r.items()}


def kernel(**inputs):
    import numpy as np
    import concourse.bacc as bacc
    from concourse import mybir
    from concourse.bass_utils import run_bass_kernel_spmd

    nc = bacc.Bacc("TRN2", target_bir_lowering=False, num_devices=1)
    arrays, args = {}, {}
    for name, array in _arrays(inputs).items():
        arrays[f"in_{name}_dram"] = array
        args[name] = nc.dram_tensor(f"in_{name}_dram", array.shape, mybir.dt.from_np(array.dtype),
                                    kind="ExternalInput").ap()
    out = nc.dram_tensor("out_0_dram", (B, S, D), mybir.dt.from_np(np.dtype("float32")), kind="ExternalOutput").ap()
    build(nc, args, out)
    r = run_bass_kernel_spmd(nc, [arrays], core_ids=[0])
    return r.results[0]["out_0_dram"]
```
